# Optimizing a Trainium2 kernel written in Bass

```python
import numpy as np
import jax
import jax.numpy as jnp

def _softmax(x, axis=-1):
    return jax.nn.softmax(x, axis=axis)
def _gelu(x):
    return jax.nn.gelu(x, approximate=True)
def _silu(x):
    return jax.nn.silu(x)
def _sigmoid(x):
    return jax.nn.sigmoid(x)
def _layernorm(x, axis=-1, eps=1e-5):
    m = jnp.mean(x, axis=axis, keepdims=True)
    v = jnp.var(x, axis=axis, keepdims=True)
    return (x - m) / jnp.sqrt(v + eps)
def _scatter_add(tgt, idx, src, axis=0):
    return tgt.at[idx].add(src)
def _segment_sum(src, seg, n):
    return jax.ops.segment_sum(src, seg, n)

kernel_name = 'mk_adj_resnorm_d2_adj_256_7b468e'

def setup_inputs(seed: int = 0):
    np.random.seed(seed)
    _w = jnp.asarray
    def _rec_inputs():
        import jax
        import jax.numpy as jnp
        _gk = jax.random.key(seed)
        x = -0.0002928 + 1 * jax.random.normal(jax.random.fold_in(_gk, 1), (16, 1024, 256), jnp.float32)
        _w = (1.0 + jnp.arange(1024, dtype=jnp.float32)) ** -0.5
        _w = _w / _w.mean()
        _pij = jnp.clip(0.0078125 * _w[:, None] * _w[None, :], 0.0, 1.0)
        _a = jax.random.uniform(jax.random.fold_in(_gk, 2), (1024, 1024)) < _pij
        _a = jnp.logical_or(_a, jnp.swapaxes(_a, -1, -2))
        _a = jnp.logical_or(_a, jnp.eye(1024, dtype=bool))
        _af = _a.astype(jnp.float32)
        _af = _af * jax.random.uniform(jax.random.fold_in(_gk, 3), (1024, 1024), jnp.float32, 0.05, 5.06092)
        adj = _af
        return x, adj
    x, adj = _rec_inputs()
    def _L0_gnn_setup():
        import jax, jax.numpy as jnp
        import numpy as np
        HEADS = 4
        key = jax.random.key(seed)
        k1, k2, k3 = jax.random.split(key, 3)
        B, N, C = (16, 1024, 256)
        x = jax.random.normal(k1, (B, N, C), dtype=jnp.float32)
        para = jnp.ones((1, C, 32, 32), dtype=jnp.float32)
        adj = jax.random.normal(k2, (N, N), dtype=jnp.float32)
        kv_w = jax.random.normal(k3, (C, 2 * C), dtype=jnp.float32) * 0.02
        return {'x': x, 'para': para, 'adj': adj, 'kv_w': kv_w}
    _L0_gnn_all = _L0_gnn_setup()
    _L0_gnn_in = {k: v for k, v in _L0_gnn_all.items() if k in ('para', 'kv_w', )}
    del _L0_gnn_all

    def _L1_gnn_setup():
        import jax, jax.numpy as jnp
        import numpy as np
        EPS = 1e-05

        def _batchnorm(x, gamma, beta):
            mu = jnp.mean(x, axis=0)
            var = jnp.var(x, axis=0)
            return (x - mu) * jax.lax.rsqrt(var + EPS) * gamma + beta
        key = jax.random.key(seed)
        ks = jax.random.split(key, 4)
        b, n, d, h, o = (32, 2048, 256, 512, 256)
        features = jax.random.normal(ks[0], (b, n, d), dtype=jnp.float32)
        A = jax.random.uniform(ks[1], (n, n), dtype=jnp.float32)
        lim1 = float(np.sqrt(6.0 / (d + h)))
        W1 = jax.random.uniform(ks[2], (h, d), minval=-lim1, maxval=lim1, dtype=jnp.float32)
        b1 = jnp.zeros((h,), jnp.float32)
        lim2 = float(np.sqrt(6.0 / (h + o)))
        W2 = jax.random.uniform(ks[3], (o, h), minval=-lim2, maxval=lim2, dtype=jnp.float32)
        b2 = jnp.zeros((o,), jnp.float32)
        g1 = jnp.ones((h,), jnp.float32)
        be1 = jnp.zeros((h,), jnp.float32)
        g2 = jnp.ones((o,), jnp.float32)
        be2 = jnp.zeros((o,), jnp.float32)
        return {'features': features, 'A': A, 'W1': W1, 'b1': b1, 'g1': g1, 'be1': be1, 'W2': W2, 'b2': b2, 'g2': g2, 'be2': be2}
    _L1_gnn_all = _L1_gnn_setup()
    _L1_gnn_in = {k: v for k, v in _L1_gnn_all.items() if k in ('W1', 'b1', 'g1', 'be1', 'W2', 'b2', 'g2', 'be2', )}
    del _L1_gnn_all

    return {
        "x": x,
        "adj": adj,
        "L0_gnn_para": _L0_gnn_in["para"],
        "L0_gnn_kv_w": _L0_gnn_in["kv_w"],
        "L1_gnn_W1": _L1_gnn_in["W1"],
        "L1_gnn_b1": _L1_gnn_in["b1"],
        "L1_gnn_g1": _L1_gnn_in["g1"],
        "L1_gnn_be1": _L1_gnn_in["be1"],
        "L1_gnn_W2": _L1_gnn_in["W2"],
        "L1_gnn_b2": _L1_gnn_in["b2"],
        "L1_gnn_g2": _L1_gnn_in["g2"],
        "L1_gnn_be2": _L1_gnn_in["be2"],
    }

def reference(x, adj, L0_gnn_para, L0_gnn_kv_w, L1_gnn_W1, L1_gnn_b1, L1_gnn_g1, L1_gnn_be1, L1_gnn_W2, L1_gnn_b2, L1_gnn_g2, L1_gnn_be2):
    import jax
    import jax.numpy as jnp
    def _L0_gnn_ref(x, para, adj, kv_w):
        import jax, jax.numpy as jnp
        import numpy as np
        HEADS = 4
        B, N, C = x.shape
        h = HEADS
        hd = C // h
        fea = jnp.transpose(x, (0, 2, 1))
        c_adj = jnp.mean(fea, axis=1)
        diff = c_adj[:, None, :] - c_adj[:, :, None]
        A = jnp.abs(jnp.abs(jax.nn.sigmoid(diff) - 0.5) - 0.5) * 2.0
        A_s = (A + jnp.transpose(A, (0, 2, 1))) * 0.5
        Wg = adj[None, :, :] * A_s
        g = jnp.einsum('bcn,bnm->bcm', fea, Wg)
        g = jax.nn.relu(g * para.reshape(1, C, N))
        q = jnp.transpose(g, (0, 2, 1)).reshape(B, N, h, hd).transpose(0, 2, 1, 3)
        kv = (x @ kv_w).reshape(B, N, 2, h, hd).transpose(2, 0, 3, 1, 4)
        k, v = (kv[0], kv[1])
        scale = (1.0 + 1e-06) / (np.sqrt(hd) + 1e-06)
        attn = jax.nn.softmax(jnp.einsum('bhnd,bhmd->bhnm', q, k) * scale, axis=-1)
        out = jnp.einsum('bhnm,bhmd->bhnd', attn, v)
        return out.transpose(0, 2, 1, 3).reshape(B, N, C)

    def _L1_gnn_ref(features, A, W1, b1, g1, be1, W2, b2, g2, be2):
        import jax, jax.numpy as jnp
        import numpy as np
        EPS = 1e-05

        def _batchnorm(x, gamma, beta):
            mu = jnp.mean(x, axis=0)
            var = jnp.var(x, axis=0)
            return (x - mu) * jax.lax.rsqrt(var + EPS) * gamma + beta
        b, n, d = features.shape
        A_norm = A + jnp.eye(n, dtype=A.dtype)
        deg = jnp.sum(A_norm, axis=0) + jnp.sum(A_norm, axis=1) - jnp.diagonal(A_norm)
        dinv = jax.lax.rsqrt(deg)
        A_hat = A_norm * dinv[:, None] * dinv[None, :]
        agg = jnp.einsum('nm,bmd->bnd', A_hat, features)
        x = agg.reshape(-1, d)
        h = jax.nn.relu(_batchnorm(x @ W1.T + b1, g1, be1))
        out = h @ W2.T + b2
        out = _batchnorm(out, g2, be2)
        return out.reshape(b, n, -1)

    x = _layernorm(x + _L0_gnn_ref(x, L0_gnn_para, adj, L0_gnn_kv_w), axis=-1)
    x = _layernorm(x + _L1_gnn_ref(x, adj, L1_gnn_W1, L1_gnn_b1, L1_gnn_g1, L1_gnn_be1, L1_gnn_W2, L1_gnn_b2, L1_gnn_g2, L1_gnn_be2), axis=-1)
    return x


_drawn_inputs = setup_inputs


def setup_inputs(seed=0):
    import zlib

    import numpy as np

    out = dict(_drawn_inputs(seed))
    spreads = {'L0_gnn_para': (1.0, 0.2),
     'L1_gnn_b1': (0.0, 0.1),
     'L1_gnn_g1': (1.0, 0.2),
     'L1_gnn_be1': (0.0, 0.1),
     'L1_gnn_b2': (0.0, 0.1),
     'L1_gnn_g2': (1.0, 0.2),
     'L1_gnn_be2': (0.0, 0.1)}
    factors = {}
    for name, (base, spread) in spreads.items():
        noise = np.random.default_rng([zlib.crc32(name.encode()), seed]).standard_normal(out[name].shape)
        drawn = base * np.exp(spread * noise) if base else spread * noise
        out[name] = jnp.asarray(drawn.astype(out[name].dtype))
    for name, factor in factors.items():
        out[name] = (out[name] * factor).astype(out[name].dtype)
    return out
```

```python
import concourse.bass as bass
from concourse import mybir
from contextlib import ExitStack

F32 = mybir.dt.float32
F32R = mybir.dt.float32r
ALU = mybir.AluOpType
ACT = mybir.ActivationFunctionType
AX = mybir.AxisListType

P = 128
BANK = 512
HEADS = 4
EPS = 1e-5


def wait(eng, sem, count):
    if isinstance(count, int) and count <= 0:
        return
    eng.wait_ge(sem, count)


def over_batches(eng, n, body):
    body(0, n == 1)
    if n > 2:
        with eng.Fori(1, n - 1) as b:
            body(b, False)
    if n > 1:
        body(n - 1, True)


def row_moments(nc, dve, stats, part, mean, veps, n, part_done, veps_done, base):
    mean_a, mean_b, sq_a, sq_b = (stats[:, :, k] for k in (1, 4, 2, 5))
    nc.vector.tensor_tensor(part[:, 0, :], mean_a, mean_b, ALU.add).then_inc(part_done, 1)
    nc.vector.tensor_tensor(part[:, 1, :], mean_a, mean_b, ALU.subtract).then_inc(part_done, 1)
    nc.vector.tensor_tensor(part[:, 2, :], sq_a, sq_b, ALU.add).then_inc(part_done, 1)
    wait(dve, part_done, base + 3)
    nc.vector.tensor_scalar(mean, part[:, 0, :], 0.5, None, ALU.mult).then_inc(part_done, 1)
    nc.vector.tensor_tensor(part[:, 1, :], part[:, 1, :], part[:, 1, :], ALU.mult).then_inc(part_done, 1)
    wait(dve, part_done, base + 5)
    nc.vector.scalar_tensor_tensor(part[:, 2, :], part[:, 2, :], 4.0 / n, part[:, 1, :], ALU.mult, ALU.add)\
        .then_inc(part_done, 1)
    wait(dve, part_done, base + 6)
    nc.vector.tensor_scalar(veps, part[:, 2, :], 0.25, EPS, ALU.mult, ALU.add).then_inc(veps_done, 1)


def attention_layer(nc, x, adj, para, kv_w, x1):
    B, N, C = x.shape
    T = N // P
    CT = C // P
    HD = C // HEADS
    NH = N // BANK
    VW = HD + 1
    SCALE = (1.0 + 1e-6) / (HD ** 0.5 + 1e-6)
    WR, DR, AR = 3, 3, 2
    MAX_TILES = [2, 1, 2, 1, 2, 0, 0, 0]
    ROW_STEP = 5

    x_v = x.rearrange("b (t p) c -> b p t c", p=P)
    x1_v = x1.rearrange("b (t p) c -> b p t c", p=P)
    adj_v = adj.rearrange("(t p) m -> t p m", p=P)
    para_v = para.rearrange("o (c p) h w -> p (o c) (h w)", p=P)
    kvw_v = kv_w.rearrange("(c p) n -> p c n", p=P)

    with ExitStack() as ctx:
        def sb(name, shape, dt=F32):
            return ctx.enter_context(nc.sbuf_tensor(name, shape, dt))

        def pb(name, shape):
            return ctx.enter_context(nc.psum_tensor(name, shape, F32))

        def sem(name):
            return ctx.enter_context(nc.semaphore(name))

        ident = sb("ident", [P, P])
        mean_w = sb("mean_w", [P, P], F32R)
        mean32 = sb("mean32", [P, P])
        neg_para = sb("neg_para", [P, CT, N])
        kvw_hi = sb("kvw_hi", [P, CT, 2 * C], F32R)
        kvw_lo = sb("kvw_lo", [P, CT, 2 * C], F32R)
        adj_ring = sb("adj_ring", [P, AR, N])
        scr = sb("scr", [P, DR, N])
        w_hi = sb("w_hi", [P, WR, N], F32R)
        w_lo = sb("w_lo", [P, WR, N], F32R)
        x32 = sb("x32", [P, T, C])
        x_hi = sb("x_hi", [P, T, C], F32R)
        x_lo = sb("x_lo", [P, T, C], F32R)
        xT_hi = sb("xT_hi", [P, CT, N], F32R)
        xT_lo = sb("xT_lo", [P, CT, N], F32R)
        cb = sb("cb", [P, N])
        ccol = sb("ccol", [P, T])
        csum = sb("csum", [P, T])
        ka = [sb(f"ka{h}", [P, N], F32R) for h in range(HEADS)]
        kb = [sb(f"kb{h}", [P, N], F32R) for h in range(HEADS)]
        qa = [sb(f"qa{h}", [P, N], F32R) for h in range(HEADS)]
        qb = [sb(f"qb{h}", [P, N], F32R) for h in range(HEADS)]
        v = sb("v", [P, T, HEADS, VW])
        probs = sb("probs", [P, 2, N])
        res = sb("res", [P, T, C])
        pvn = sb("pvn", [P, T, HD])
        rden = sb("rden", [P, T])
        mxs = sb("mxs", [P, T])
        row = sb("row", [T, P], F32R)
        stats = sb("stats", [P, T, 6])
        mean = sb("mean", [P, T])
        part = sb("part", [P, 3, T])
        veps = sb("veps", [P, T])
        rstd = sb("rstd", [P, T])
        neg_half = sb("neg_half", [P, T])

        sc_ps = pb("sc_ps", [P, 2, N])
        pv_ps = pb("pv_ps", [P, 2, BANK])
        mx_ps = pb("mx_ps", [P, 2, BANK])

        def own(h):
            return slice(HD * (h % 2), HD * (h % 2) + HD)

        def other(h):
            return slice(HD - HD * (h % 2), 2 * HD - HD * (h % 2))

        s = {n: sem(n) for n in (
            "const_in", "ident_set", "consts_set", "x_in", "res_in", "x1_out", "row_in",
            "xt_ready", "cb_ready", "k_ready", "g_step", "v_ready", "mx_ready", "st_ready", "pv_done", "rowT_ready",
            "xth_done", "cb_done", "abs_done", "tanh_done", "whi_done", "kh_done", "qh_done", "v_evac", "exp_done",
            "xhi_done", "x_split", "csum_done", "ccol_done", "xtl_done", "w_done", "wlo_done", "kl_done", "qt_done",
            "ql_done", "max_done", "row_done", "rden_done", "pv_evac", "res_added", "stats_done", "mv_done",
            "veps_done", "rstd_done", "res_done", "kvw_hi_done")}
        adj_in = [sem(f"adj_in{i}") for i in range(AR)]
        qa_in = [sem(f"qa_in{h}") for h in range(HEADS)]
        kb_in = [sem(f"kb_in{h}") for h in range(HEADS)]

        block = ctx.enter_context(nc.Block())

        @block.sync
        def _(sp):
            sp.dma_start(neg_para[:, :, :], para_v).then_inc(s["const_in"], 16)
            sp.dma_start(scr[:, 0, :].rearrange("p (c n) -> p c n", c=CT), kvw_v).then_inc(s["const_in"], 16)

            def load_adj(b, n):
                wait(sp, s["w_done"], 8 * b + n - 1)
                sp.dma_start(adj_ring[:, n % AR, :], adj_v[n]).then_inc(adj_in[n % AR], 16)

            def load_x(b):
                wait(sp, s["xt_ready"], 2 * b)
                wait(sp, s["x_split"], b)
                wait(sp, s["csum_done"], b)
                sp.dma_start(x32[:, :, :], x_v[b]).then_inc(s["x_in"], 16)

            def copy_kb(b, h):
                wait(sp, s["kh_done"], 4 * b + h + 1)
                sp.dma_start(kb[h][own(h), :].bitcast(F32), ka[h][own(h), :].bitcast(F32)).then_inc(kb_in[h], 16)

            def copy_qa(b, h):
                wait(sp, s["qh_done"], 4 * b + h + 1)
                sp.dma_start(qa[h][other(h), :].bitcast(F32), qa[h][own(h), :].bitcast(F32)).then_inc(qa_in[h], 16)

            def store_row(b, h):
                wait(sp, s["row_done"], 4 * b + h + 1)
                r = other(h).start
                sp.dma_start(qb[h][r:r + 1, :].rearrange("o (t p) -> o t p", p=P).bitcast(F32), row[:, :].bitcast(F32)).then_inc(s["row_in"], 16)

            def store_x1(b):
                wait(sp, s["res_done"], b + 1)
                sp.dma_start(x1_v[b], res[:, :, :]).then_inc(s["x1_out"], 16)

            def body(b, last):
                load_adj(b, 3)
                load_adj(b, 4)
                if not isinstance(b, int) or b > 0:
                    store_x1(b - 1)
                for n in range(5, T):
                    load_adj(b, n)
                wait(sp, s["x1_out"], 16 * b)
                sp.dma_start(res[:, :, :], x_v[b]).then_inc(s["res_in"], 16)
                copy_qa(b, 0)
                copy_qa(b, 1)
                copy_kb(b, 2)
                copy_kb(b, 3)
                if not last:
                    load_x(b + 1)
                    load_adj(b + 1, 0)
                    load_adj(b + 1, 1)
                copy_qa(b, 2)
                copy_qa(b, 3)
                for h in range(HEADS):
                    store_row(b, h)
                if not last:
                    copy_kb(b + 1, 0)
                    copy_kb(b + 1, 1)
                    load_adj(b + 1, 2)

            load_x(0)
            load_adj(0, 0)
            load_adj(0, 1)
            copy_kb(0, 0)
            copy_kb(0, 1)
            load_adj(0, 2)
            over_batches(sp, B, body)
            store_x1(B - 1)
            wait(sp, s["x1_out"], 16 * B)

        @block.gpsimd
        def _(pool):
            pool.memset(ident[:, :], 0.0).then_inc(s["ident_set"], 1)
            pool.wait_ge(s["ident_set"], 1)
            pool.affine_select(out=ident[:, :], in_=ident[:, :], compare_op=ALU.not_equal, fill=1.0, base=0,
                               pattern=[[-1, P]], channel_multiplier=1).then_inc(s["ident_set"], 1)
            pool.memset(neg_half[:, :], -0.5).then_inc(s["ident_set"], 1)
            pool.wait_ge(s["ident_set"], 3)

            def body(b, last):
                wait(pool, s["veps_done"], b + 1)
                pool.tensor_tensor(rstd[:, :], veps[:, :], neg_half[:, :], ALU.pow).then_inc(s["rstd_done"], 1)

            over_batches(pool, B, body)

        @block.scalar
        def _(act):
            def xt_high(b, half):
                wait(act, s["xt_ready"], 2 * b + half + 1)
                nc.scalar.activation(xT_hi[:, :, half * BANK:(half + 1) * BANK], mx_ps[:, :, :], ACT.Copy)\
                    .then_inc(s["xth_done"], 1)

            def mean_rows(b):
                wait(act, s["cb_ready"], b + 1)
                nc.scalar.activation(cb[:, :], mx_ps[:, :, :].rearrange("p a n -> p (a n)"), ACT.Copy)\
                    .then_inc(s["cb_done"], 1)

            def distance(b, n):
                if n == 0:
                    wait(act, s["cb_done"], b + 1)
                    wait(act, s["ccol_done"], b + 1)
                    wait(act, s["ql_done"], 4 * b)
                else:
                    wait(act, s["wlo_done"], 8 * b + n - 2)
                d = scr[:, n % DR, :]
                nc.scalar.activation(d, cb[:, :], ACT.Abs, bias=ccol[:, n:n + 1]).then_inc(s["abs_done"], 1)
                wait(act, s["abs_done"], 8 * b + n + 1)
                nc.scalar.activation(d, d, ACT.Tanh, scale=0.5).then_inc(s["tanh_done"], 1)

            def w_high(b, n):
                wait(act, s["w_done"], 8 * b + n + 1)
                wait(act, s["g_step"], 8 * b if n < WR else 8 * b + n - WR + 1)
                nc.scalar.activation(w_hi[:, n % WR, :], scr[:, n % DR, :], ACT.Copy).then_inc(s["whi_done"], 1)

            def k_high(b, h):
                wait(act, s["k_ready"], 2 * b + h // 2 + 1)
                src = (mx_ps, pv_ps)[h // 2]
                nc.scalar.activation(ka[h][own(h), :], src[own(h), :, :].rearrange("p a n -> p (a n)"), ACT.Copy)\
                    .then_inc(s["kh_done"], 1)

            def q_high(b, h):
                wait(act, s["qt_done"], 2 * b + h // 2 + 1)
                nc.scalar.activation(qa[h][own(h), :], scr[own(h), h // 2, :], ACT.Relu).then_inc(s["qh_done"], 1)

            def v_copy(b, j):
                wait(act, s["v_ready"], 2 * b + j + 1)
                src = (mx_ps, pv_ps)[j]
                nc.scalar.activation(v[:, 4 * j:4 * j + 4, :, 0:HD],
                                     src[:, :, :].rearrange("p a (m h d) -> p (a m) h d", m=2, d=HD), ACT.Copy)\
                    .then_inc(s["v_evac"], 1)

            def exponential(b, h, i):
                t = 8 * h + i
                wait(act, s["st_ready"], 32 * b + t + 1)
                wait(act, s["pv_done"], 32 * b + t - 1)
                nc.scalar.activation(probs[:, t % 2, :], sc_ps[:, t % 2, :], ACT.Exp, scale=SCALE)\
                    .then_inc(s["exp_done"], 1)

            def prepare(b, between):
                between(0)
                xt_high(b, 0)
                between(1)
                xt_high(b, 1)
                between(2)
                mean_rows(b)
                between(3)
                distance(b, 0)
                between(4)
                distance(b, 1)
                between(5)
                k_high(b, 0)
                k_high(b, 1)
                w_high(b, 0)
                between(6)
                distance(b, 2)
                between(7)
                w_high(b, 1)
                w_high(b, 2)

            def body(b, last):
                for n in range(3, T + 1):
                    if n < T:
                        distance(b, n)
                    if n > 3:
                        w_high(b, n - 1)
                q_high(b, 0)
                q_high(b, 1)
                k_high(b, 2)
                k_high(b, 3)
                v_copy(b, 0)
                v_copy(b, 1)
                q_high(b, 2)
                q_high(b, 3)
                for h in range(HEADS - 1):
                    for i in range(T):
                        exponential(b, h, i)
                if last:
                    for i in range(T):
                        exponential(b, HEADS - 1, i)
                else:
                    prepare(b + 1, lambda i: exponential(b, HEADS - 1, i))

            prepare(0, lambda i: None)
            over_batches(act, B, body)

        @block.vector
        def _(dve):
            dve.memset(mean32[:, :], 1.0 / C).then_inc(s["consts_set"], 1)
            for h in range(HEADS):
                o = other(h)
                dve.memset(kb[h][o, :].bitcast(F32), 0.0).then_inc(s["consts_set"], 1)
                dve.memset(qb[h][o, :].bitcast(F32), 0.0).then_inc(s["consts_set"], 1)
            dve.wait_ge(s["consts_set"], 1 + 2 * HEADS)
            nc.vector.tensor_copy(mean_w[:, :], mean32[:, :]).then_inc(s["consts_set"], 1)
            for h in range(HEADS):
                r = other(h).start
                dve.memset(kb[h][r:r + 1, :].bitcast(F32), 1.0).then_inc(s["consts_set"], 1)
            dve.memset(v[:, :, :, HD:VW], 1.0).then_inc(s["consts_set"], 1)
            dve.wait_ge(s["const_in"], 32)
            nc.vector.tensor_scalar(neg_para[:, :, :], neg_para[:, :, :], -1.0, None, ALU.mult)\
                .then_inc(s["consts_set"], 1)
            kvw32 = scr[:, 0, :].rearrange("p (c n) -> p c n", c=CT)
            nc.vector.tensor_copy(kvw_hi[:, :, :], kvw32).then_inc(s["consts_set"], 1)
            dve.wait_ge(s["consts_set"], 4 + 3 * HEADS + 1)
            nc.vector.tensor_tensor(kvw_lo[:, :, :], kvw32, kvw_hi[:, :, :].bitcast(F32), ALU.subtract)\
                .then_inc(s["consts_set"], 1)

            def split_x(b):
                wait(dve, s["x_in"], 16 * (b + 1))
                wait(dve, s["g_step"], 8 * b)
                nc.vector.tensor_copy(x_hi[:, :, :], x32[:, :, :]).then_inc(s["xhi_done"], 1)
                wait(dve, s["xhi_done"], b + 1)
                nc.vector.tensor_tensor(x_lo[:, :, :], x32[:, :, :], x_hi[:, :, :].bitcast(F32), ALU.subtract)\
                    .then_inc(s["x_split"], 1)

            def mean_columns(b):
                wait(dve, s["tanh_done"], 8 * b)
                nc.vector.tensor_reduce(csum[:, :], x32[:, :, :], AX.X, ALU.add).then_inc(s["csum_done"], 1)
                wait(dve, s["csum_done"], b + 1)
                nc.vector.tensor_scalar(ccol[:, :], csum[:, :], -1.0 / C, None, ALU.mult).then_inc(s["ccol_done"], 1)

            def xt_low(b, half):
                wait(dve, s["xth_done"], 2 * b + half + 1)
                cols = slice(half * BANK, (half + 1) * BANK)
                nc.vector.tensor_tensor(xT_lo[:, :, cols], mx_ps[:, :, :], xT_hi[:, :, cols].bitcast(F32),
                                        ALU.subtract).then_inc(s["xtl_done"], 1)

            def weigh(b, n):
                wait(dve, s["tanh_done"], 8 * b + n + 1)
                wait(dve, adj_in[n % AR], 16 * (4 * b + n // AR + 1))
                d = scr[:, n % DR, :]
                nc.vector.scalar_tensor_tensor(d, d, -1.0, adj_ring[:, n % AR, :], ALU.add, ALU.mult)\
                    .then_inc(s["w_done"], 1)

            def w_low(b, n):
                wait(dve, s["whi_done"], 8 * b + n + 1)
                nc.vector.tensor_tensor(w_lo[:, n % WR, :], scr[:, n % DR, :], w_hi[:, n % WR, :].bitcast(F32),
                                        ALU.subtract).then_inc(s["wlo_done"], 1)

            def k_low(b, h):
                wait(dve, s["kh_done"], 4 * b + h + 1)
                src = (mx_ps, pv_ps)[h // 2]
                nc.vector.tensor_tensor(ka[h][other(h), :], src[own(h), :, :].rearrange("p a n -> p (a n)"),
                                        ka[h][own(h), :].bitcast(F32), ALU.subtract).then_inc(s["kl_done"], 1)

            def q_times_para(b, c):
                wait(dve, s["g_step"], 8 * b + 8)
                nc.vector.tensor_tensor(scr[:, c, :], sc_ps[:, c, :], neg_para[:, c, :], ALU.mult)\
                    .then_inc(s["qt_done"], 1)

            def q_low(b, h):
                wait(dve, s["qh_done"], 4 * b + h + 1)
                nc.vector.scalar_tensor_tensor(qb[h][own(h), :], scr[own(h), h // 2, :], 0.0,
                                               qa[h][own(h), :].bitcast(F32), ALU.max, ALU.subtract)\
                    .then_inc(s["ql_done"], 1)

            def maxima(b, h):
                for n in range(T):
                    wait(dve, s["mx_ready"], 32 * b + 8 * h + n + 1)
                    nc.vector.tensor_reduce(mxs[:, n:n + 1], mx_ps[:, :, :].rearrange("p a n -> p (a n)"), AX.X,
                                            ALU.max).then_inc(s["max_done"], 1)
                wait(dve, s["rowT_ready"], 4 * b + h + 1)
                wait(dve, s["row_in"], 16 * (4 * b + h))
                nc.vector.tensor_scalar(row[:, :], mx_ps[0:T, 0, 0:P], -1.0, None, ALU.mult)\
                    .then_inc(s["row_done"], 1)

            def add_head(b, h):
                wait(dve, s["pv_done"], 32 * b + 8 * h + 8)
                pv = pv_ps[:, :, 0:4 * VW].rearrange("p a (t w) -> p a t w", w=VW)
                nc.vector.reciprocal(rden[:, :].rearrange("p (a t o) -> p a t o", a=2, o=1), pv[:, :, :, HD:VW])\
                    .then_inc(s["rden_done"], 1)
                wait(dve, s["rden_done"], 4 * b + h + 1)
                nc.vector.tensor_tensor(pvn[:, :, :].rearrange("p (a t) d -> p a t d", a=2), pv[:, :, :, 0:HD],
                                        rden[:, :].rearrange("p (a t o) -> p a t o", a=2, o=1)
                                        .broadcast_to([P, 2, 4, HD]), ALU.mult).then_inc(s["pv_evac"], 1)
                wait(dve, s["pv_evac"], 4 * b + h + 1)
                if h == 0:
                    wait(dve, s["res_in"], 16 * (b + 1))
                out = res[:, :, h * HD:(h + 1) * HD]
                nc.vector.tensor_tensor(out, out, pvn[:, :, :], ALU.add).then_inc(s["res_added"], 1)

            def layernorm(b):
                wait(dve, s["res_added"], 4 * b + 4)
                for n in range(T):
                    nc.vector.bn_stats(stats[:, n, :], res[:, n, :]).then_inc(s["stats_done"], 1)
                wait(dve, s["stats_done"], T * (b + 1))
                row_moments(nc, dve, stats, part, mean[:, :], veps[:, :], C, s["mv_done"], s["veps_done"], 6 * b)
                wait(dve, s["rstd_done"], b + 1)
                for n in range(T):
                    last = nc.vector.tensor_scalar(res[:, n, :], res[:, n, :], mean[:, n:n + 1], rstd[:, n:n + 1],
                                                   ALU.subtract, ALU.mult)
                last.then_inc(s["res_done"], 1)

            def body(b, last):
                if not isinstance(b, int) or b > 0:
                    layernorm(b - 1)
                for n in range(3, T + 1):
                    if n < T:
                        weigh(b, n)
                    if n > 3:
                        w_low(b, n - 1)
                q_times_para(b, 0)
                q_times_para(b, 1)
                q_low(b, 0)
                q_low(b, 1)
                k_low(b, 2)
                k_low(b, 3)
                maxima(b, 0)
                q_low(b, 2)
                q_low(b, 3)
                for h in range(HEADS):
                    if h + 1 < HEADS:
                        maxima(b, h + 1)
                    if h == 1 and not last:
                        split_x(b + 1)
                    if h == 2 and not last:
                        mean_columns(b + 1)
                    if h == 3 and not last:
                        prepare(b + 1)
                    add_head(b, h)

            def prepare(b):
                xt_low(b, 0)
                xt_low(b, 1)
                weigh(b, 0)
                weigh(b, 1)
                k_low(b, 0)
                k_low(b, 1)
                w_low(b, 0)
                weigh(b, 2)
                w_low(b, 1)
                w_low(b, 2)

            split_x(0)
            mean_columns(0)
            prepare(0)
            over_batches(dve, B, body)
            layernorm(B - 1)

        @block.tensor
        def _(pe):
            def product(out, terms):
                for k, (lhsT, rhs) in enumerate(terms):
                    ins = nc.tensor.matmul(out, lhsT, rhs, start=k == 0, stop=k == len(terms) - 1)
                return ins

            def split_terms(pairs):
                out = []
                for (a_hi, a_lo), (b_hi, b_lo) in pairs:
                    out += [(a_hi, b_hi), (a_lo, b_hi), (a_hi, b_lo)]
                return out

            def transpose_x(b, half):
                if half == 0:
                    wait(pe, s["x_in"], 16 * (b + 1))
                    wait(pe, s["row_done"], 4 * b)
                else:
                    wait(pe, s["xtl_done"], 2 * b + 1)
                for c in range(CT):
                    for q in range(4):
                        ins = nc.tensor.transpose(mx_ps[:, c, q * P:(q + 1) * P],
                                                  x32[:, 4 * half + q, c * P:(c + 1) * P], ident[:, :])
                ins.then_inc(s["xt_ready"], 1)

            def broadcast_means(b):
                wait(pe, s["xtl_done"], 2 * b + 2)
                for nh in range(NH):
                    cols = slice(nh * BANK, (nh + 1) * BANK)
                    ins = product(mx_ps[:, nh, :], [(mean_w[:, :], t[:, c, cols]) for c in range(CT)
                                                    for t in (xT_hi, xT_lo)])
                ins.then_inc(s["cb_ready"], 1)

            def k_product(b, c):
                if c == 0:
                    wait(pe, s["cb_done"], b + 1)
                else:
                    wait(pe, s["pv_evac"], 4 * b)
                out = (mx_ps, pv_ps)[c]
                ws = slice(c * P, (c + 1) * P)
                for nh in range(NH):
                    cols = slice(nh * BANK, (nh + 1) * BANK)
                    ins = product(out[:, nh, :], split_terms(
                        [((kvw_hi[:, k, ws], kvw_lo[:, k, ws]), (xT_hi[:, k, cols], xT_lo[:, k, cols]))
                         for k in range(CT)]))
                ins.then_inc(s["k_ready"], 1)

            def v_product(b, j):
                wait(pe, s["kl_done"], 4 * b + 2 * j + 2)
                out = (mx_ps, pv_ps)[j]
                for m in range(4):
                    rows = slice((4 * j + m) * P, (4 * j + m + 1) * P)
                    ins = product(out[:, m // 2, (m % 2) * C:(m % 2 + 1) * C], split_terms(
                        [((xT_hi[:, k, rows], xT_lo[:, k, rows]), (kvw_hi[:, k, C:2 * C], kvw_lo[:, k, C:2 * C]))
                         for k in range(CT)]))
                ins.then_inc(s["v_ready"], 1)

            def g_product(b):
                wait(pe, s["exp_done"], 32 * b)
                wait(pe, s["x_split"], b + 1)
                for n in range(T):
                    wait(pe, s["wlo_done"], 8 * b + n + 1)
                    for c in range(CT):
                        ch = slice(c * P, (c + 1) * P)
                        for nh in range(NH):
                            cols = slice(nh * BANK, (nh + 1) * BANK)
                            terms = split_terms([((x_hi[:, n, ch], x_lo[:, n, ch]),
                                                  (w_hi[:, n % WR, cols], w_lo[:, n % WR, cols]))])
                            for k, (lhsT, rhs) in enumerate(terms):
                                ins = nc.tensor.matmul(sc_ps[:, c, cols], lhsT, rhs,
                                                       start=n == 0 and k == 0, stop=n == T - 1 and k == 2)
                    ins.then_inc(s["g_step"], 1)

            def max_scores(b, h, n):
                if n == 0 and h == 0:
                    wait(pe, s["v_evac"], 2 * b + 1)
                    wait(pe, s["qh_done"], 4 * b + 1)
                    wait(pe, s["kh_done"], 4 * b + 1)
                elif n == 0:
                    wait(pe, s["row_done"], 4 * b + h)
                    wait(pe, s["qh_done"], 4 * b + h + 1)
                else:
                    wait(pe, s["max_done"], 32 * b + 8 * h + n)
                for nh in range(NH):
                    ins = nc.tensor.matmul(mx_ps[:, nh, :], qa[h][own(h), n * P:(n + 1) * P],
                                           ka[h][own(h), nh * BANK:(nh + 1) * BANK], start=True, stop=True)
                ins.then_inc(s["mx_ready"], 1)

            def transpose_maxima(b, h):
                wait(pe, s["max_done"], 32 * b + 8 * h + 8)
                nc.tensor.transpose(mx_ps[0:T, 0, 0:P], mxs[:, :], ident[:, :]).then_inc(s["rowT_ready"], 1)

            def scores(b, h, i):
                t = 8 * h + i
                wait(pe, s["exp_done"], 32 * b + t - 1)
                if t < 2:
                    wait(pe, s["qt_done"], 2 * b + t + 1)
                if i == 0:
                    wait(pe, s["row_in"], 16 * (4 * b + h + 1))
                    wait(pe, qa_in[h], 16 * (b + 1))
                    wait(pe, kb_in[h], 16 * (b + 1))
                    wait(pe, s["ql_done"], 4 * b + h + 1)
                    wait(pe, s["kl_done"], 4 * b + h + 1)
                keys = slice(i * P, (i + 1) * P)
                for nh in range(NH):
                    cols = slice(nh * BANK, (nh + 1) * BANK)
                    ins = product(sc_ps[:, t % 2, cols], [(ka[h][:, keys], qa[h][:, cols]),
                                                          (kb[h][:, keys], qb[h][:, cols])])
                ins.then_inc(s["st_ready"], 1)

            def values(b, h, i):
                t = 8 * h + i
                wait(pe, s["exp_done"], 32 * b + t + 1)
                if i == 0 and h == 0:
                    wait(pe, s["v_evac"], 2 * b + 2)
                elif i == 0:
                    wait(pe, s["pv_evac"], 4 * b + h)
                for n in range(T):
                    ins = nc.tensor.matmul(pv_ps[:, n // 4, (n % 4) * VW:(n % 4 + 1) * VW],
                                           probs[:, t % 2, n * P:(n + 1) * P], v[:, i, h, :],
                                           start=i == 0 and n % 4 == 0, stop=i == T - 1, skip_group_check=True)
                ins.then_inc(s["pv_done"], 1)

            def body(b, last):
                g_product(b)
                k_product(b, 1)
                v_product(b, 0)
                v_product(b, 1)
                for n in range(T):
                    max_scores(b, 0, n)
                transpose_maxima(b, 0)
                for h in range(HEADS):
                    n = 0
                    for i in range(T):
                        scores(b, h, i)
                        more = MAX_TILES[i] if h + 1 < HEADS else 0
                        if more:
                            max_scores(b, h + 1, n)
                        if h + 1 < HEADS and i == ROW_STEP:
                            transpose_maxima(b, h + 1)
                        if h + 1 == HEADS and not last:
                            prepare(b + 1, i)
                        if h + i:
                            values(b, h if i else h - 1, i - 1 if i else T - 1)
                        if more > 1:
                            max_scores(b, h + 1, n + 1)
                        n += more
                values(b, HEADS - 1, T - 1)

            def prepare(b, i):
                if i < 2:
                    transpose_x(b, i)
                if i == 2:
                    broadcast_means(b)
                if i == 4:
                    k_product(b, 0)

            pe.wait_ge(s["ident_set"], 3)
            pe.wait_ge(s["consts_set"], 6 + 3 * HEADS)
            for i in range(T):
                prepare(0, i)
            over_batches(pe, B, body)


def aggregate_layer(nc, x1, adj, w1, b1, g1, be1, scale1, shift1, pre1):
    B, N, C = x1.shape
    H = w1.shape[0]
    T, CT, HT, NH = N // P, C // P, H // P, N // BANK

    x1_v = x1.rearrange("b (t p) c -> b p t c", p=P)
    adj_v = adj.rearrange("(t p) m -> p t m", p=P)
    w1_v = w1.rearrange("(t p) c -> p t c", p=P)
    pre1_v = pre1.rearrange("b (t p) n -> b p t n", p=P)

    with ExitStack() as ctx:
        def sb(name, shape, dt=F32):
            return ctx.enter_context(nc.sbuf_tensor(name, shape, dt))

        def pb(name, shape):
            return ctx.enter_context(nc.psum_tensor(name, shape, F32))

        def sem(name):
            return ctx.enter_context(nc.semaphore(name))

        ident = sb("ident_b", [P, P])
        ones = sb("ones", [P, 1])
        neg_half = sb("neg_half_b", [P, T])
        a_hi = sb("a_hi", [P, T, N], F32R)
        a_lo = sb("a_lo", [P, T, N], F32R)
        at32 = sb("at32", [P, 2, N])
        pre = sb("pre", [P, 2, HT, N])
        adjs = pre[:, :, :, :].rearrange("p e t n -> p (e t) n")
        w1s = sb("w1s", [P, HT, C])
        w1_hi = sb("w1_hi", [P, CT, H], F32R)
        w1_lo = sb("w1_lo", [P, CT, H], F32R)
        x1s = sb("x1s", [P, 2, T, C])
        x1_hi = sb("x1_hi", [P, T, C], F32R)
        x1_lo = sb("x1_lo", [P, T, C], F32R)
        agg_hi = sb("agg_hi", [P, CT, N], F32R)
        agg_lo = sb("agg_lo", [P, CT, N], F32R)
        block_diag = sb("block_diag", [P, T, P])
        diag = sb("diag", [P, T])
        rowsum = sb("rowsum", [P, T])
        deg = sb("deg", [P, T])
        dinv = sb("dinv", [P, T])
        b1s = sb("b1s", [P, HT])
        g1s = sb("g1s", [P, HT])
        be1s = sb("be1s", [P, HT])
        stats = sb("stats1", [P, HT, B * NH, 6])
        mv = sb("mv1", [P, HT, 2])
        veps = sb("veps1", [P, HT])
        rstd = sb("rstd1", [P, HT])

        ag_ps = pb("ag_ps", [P, NH, CT, BANK])
        pre_ps = pb("pre_ps", [P, HT, BANK])

        s = {n: sem("b_" + n) for n in (
            "adj_in", "w1_in", "vec_in", "consts_set", "aug_done", "diag_done", "rowsum_done", "colsum_done", "deg_done",
            "dinv_done", "rows_scaled", "at_ready", "at_done", "ath_done", "atl_done", "w1_ready", "w1h_done",
            "w1l_done", "x1h_done", "x1l_done", "ag_ready", "agh_done", "agl_done", "pre_ready", "pre_done",
            "stats_done", "mv_done", "veps_done", "rstd_done", "scale_done", "shift_done")}
        x1_in = [sem(f"b_x1_in{e}") for e in range(2)]
        pre_out = [sem(f"b_pre_out{e}") for e in range(2)]

        block = ctx.enter_context(nc.Block())

        @block.sync
        def _(sp):
            sp.dma_start(adjs, adj_v).then_inc(s["adj_in"], 16)
            sp.dma_start(w1s[:, :, :], w1_v).then_inc(s["w1_in"], 16)
            for t, src in ((b1s, b1), (g1s, g1), (be1s, be1)):
                sp.dma_start(t[:, :], src.rearrange("(t p) -> p t", p=P), allow_slow_non_contiguous=True)\
                    .then_inc(s["vec_in"], 16)

            def load(b, e):
                wait(sp, s["x1l_done"], b - 1)
                sp.dma_start(x1s[:, e, :, :], x1_v[b]).then_inc(x1_in[e], 16)

            def pair(g, last):
                for e in range(2):
                    wait(sp, s["pre_done"], 8 * (2 * g + e) + 8)
                    sp.dma_start(pre1_v[2 * g + e], pre[:, e, :, :]).then_inc(pre_out[e], 16)
                    if not last:
                        load(2 * g + e + 2, e)

            load(0, 0)
            load(1, 1)
            over_batches(sp, B // 2, pair)
            for e in range(2):
                wait(sp, pre_out[e], 16 * (B // 2))

        @block.gpsimd
        def _(pool):
            pool.memset(ident[:, :], 0.0).then_inc(s["consts_set"], 1)
            pool.memset(ones[:, :], 1.0).then_inc(s["consts_set"], 1)
            pool.memset(neg_half[:, :], -0.5).then_inc(s["consts_set"], 1)
            pool.wait_ge(s["consts_set"], 3)
            pool.affine_select(out=ident[:, :], in_=ident[:, :], compare_op=ALU.not_equal, fill=1.0, base=0,
                               pattern=[[-1, P]], channel_multiplier=1).then_inc(s["consts_set"], 1)
            pool.wait_ge(s["deg_done"], 1)
            pool.tensor_tensor(dinv[:, :], deg[:, :], neg_half[:, :], ALU.pow).then_inc(s["dinv_done"], 1)
            pool.wait_ge(s["veps_done"], 1)
            pool.tensor_tensor(rstd[:, :], veps[:, :], neg_half[:, 0:HT], ALU.pow).then_inc(s["rstd_done"], 1)

        @block.scalar
        def _(act):
            for c in range(CT):
                act.wait_ge(s["w1_ready"], c + 1)
                nc.scalar.activation(w1_hi[:, c, :], pre_ps[:, c, :], ACT.Copy).then_inc(s["w1h_done"], 1)
            for m in range(T):
                act.wait_ge(s["at_done"], m + 1)
                nc.scalar.activation(a_hi[:, m, :], at32[:, m % 2, :], ACT.Copy).then_inc(s["ath_done"], 1)
            act.wait_ge(s["vec_in"], 48)

            def pair(g, last):
                for e in range(2):
                    b = 2 * g + e
                    for j in range(NH):
                        wait(act, s["ag_ready"], 2 * b + j + 1)
                        nc.scalar.activation(agg_hi[:, :, j * BANK:(j + 1) * BANK], ag_ps[:, j, :, :], ACT.Copy)\
                            .then_inc(s["agh_done"], 1)
                    wait(act, pre_out[e], 16 * g)
                    wait(act, s["stats_done"], 8 * b - 8)
                    for j in range(NH):
                        for t in range(HT):
                            wait(act, s["pre_ready"], 8 * b + 4 * j + t + 1)
                            nc.scalar.activation(pre[:, e, t, j * BANK:(j + 1) * BANK], pre_ps[:, t, :],
                                                 ACT.Identity, bias=b1s[:, t:t + 1]).then_inc(s["pre_done"], 1)

            over_batches(act, B // 2, pair)

        @block.vector
        def _(dve):
            dve.wait_ge(s["adj_in"], 16)
            dve.wait_ge(s["consts_set"], 4)
            for t in range(T):
                blk = adjs[:, t, t * P:(t + 1) * P]
                nc.vector.tensor_tensor(blk, blk, ident[:, :], ALU.add).then_inc(s["aug_done"], 1)
            dve.wait_ge(s["aug_done"], T)
            for t in range(T):
                nc.vector.tensor_tensor(block_diag[:, t, :], adjs[:, t, t * P:(t + 1) * P], ident[:, :], ALU.mult)\
                    .then_inc(s["diag_done"], 1)
            nc.vector.tensor_reduce(rowsum[:, :], adjs, AX.X, ALU.add).then_inc(s["rowsum_done"], 1)
            dve.wait_ge(s["diag_done"], T)
            nc.vector.tensor_reduce(diag[:, :], block_diag[:, :, :], AX.X, ALU.add).then_inc(s["diag_done"], 1)
            dve.wait_ge(s["rowsum_done"], 1)
            dve.wait_ge(s["colsum_done"], 1)
            nc.vector.tensor_tensor(rowsum[:, :], pre_ps[:, HT - 1, 0:T], rowsum[:, :], ALU.add)\
                .then_inc(s["rowsum_done"], 1)
            dve.wait_ge(s["rowsum_done"], 2)
            dve.wait_ge(s["diag_done"], T + 1)
            nc.vector.tensor_tensor(deg[:, :], rowsum[:, :], diag[:, :], ALU.subtract).then_inc(s["deg_done"], 1)
            for c in range(CT):
                dve.wait_ge(s["w1h_done"], c + 1)
                nc.vector.tensor_tensor(w1_lo[:, c, :], pre_ps[:, c, :], w1_hi[:, c, :].bitcast(F32), ALU.subtract)\
                    .then_inc(s["w1l_done"], 1)
            dve.wait_ge(s["dinv_done"], 1)
            for t in range(T):
                nc.vector.tensor_scalar(adjs[:, t, :], adjs[:, t, :], dinv[:, t:t + 1], None, ALU.mult)\
                    .then_inc(s["rows_scaled"], 1)

            def a_low(m):
                dve.wait_ge(s["ath_done"], m + 1)
                nc.vector.tensor_tensor(a_lo[:, m, :], at32[:, m % 2, :], a_hi[:, m, :].bitcast(F32), ALU.subtract)\
                    .then_inc(s["atl_done"], 1)

            for m in range(T):
                dve.wait_ge(s["at_ready"], m + 1)
                if m >= 2:
                    a_low(m - 2)
                    dve.wait_ge(s["atl_done"], m - 1)
                nc.vector.tensor_scalar(at32[:, m % 2, :], ag_ps[:, m % 2, :, :].rearrange("p c n -> p (c n)"),
                                        dinv[:, m:m + 1], None, ALU.mult).then_inc(s["at_done"], 1)
            a_low(T - 2)
            a_low(T - 1)

            def split(b, e, g):
                wait(dve, x1_in[e], 16 * (g + 1))
                wait(dve, s["ag_ready"], 2 * b)
                nc.vector.tensor_copy(x1_hi[:, :, :], x1s[:, e, :, :]).then_inc(s["x1h_done"], 1)
                wait(dve, s["x1h_done"], b + 1)
                nc.vector.tensor_tensor(x1_lo[:, :, :], x1s[:, e, :, :], x1_hi[:, :, :].bitcast(F32),
                                        ALU.subtract).then_inc(s["x1l_done"], 1)

            def pair(g, last):
                for e in range(2):
                    b = 2 * g + e
                    for j in range(NH):
                        wait(dve, s["agh_done"], 2 * b + j + 1)
                        cols = slice(j * BANK, (j + 1) * BANK)
                        nc.vector.tensor_tensor(agg_lo[:, :, cols], ag_ps[:, j, :, :],
                                                agg_hi[:, :, cols].bitcast(F32), ALU.subtract)\
                            .then_inc(s["agl_done"], 1)
                    if not (last and e == 1):
                        split(b + 1, 1 - e, g + e)
                    for j in range(NH):
                        for t in range(HT):
                            wait(dve, s["pre_done"], 8 * b + 4 * j + t + 1)
                            nc.vector.bn_stats(stats[:, t, NH * b + j, :], pre[:, e, t, j * BANK:(j + 1) * BANK])\
                                .then_inc(s["stats_done"], 1)

            split(0, 0, 0)
            over_batches(dve, B // 2, pair)
            wait(dve, s["stats_done"], 8 * B)
            for t in range(HT):
                nc.vector.bn_aggr(mv[:, t, :], stats[:, t, :, :]).then_inc(s["mv_done"], 1)
            dve.wait_ge(s["mv_done"], HT)
            nc.vector.tensor_scalar(veps[:, :].rearrange("p (t o) -> p t o", o=1), mv[:, :, 1:2], EPS, None, ALU.add)\
                .then_inc(s["veps_done"], 1)
            dve.wait_ge(s["rstd_done"], 1)
            nc.vector.tensor_tensor(scale1[:, :], g1s[:, :], rstd[:, :], ALU.mult).then_inc(s["scale_done"], 1)
            dve.wait_ge(s["scale_done"], 1)
            nc.vector.tensor_tensor(shift1[:, :], mv[:, :, 0], scale1[:, :], ALU.mult).then_inc(s["shift_done"], 1)
            dve.wait_ge(s["shift_done"], 1)
            nc.vector.tensor_tensor(shift1[:, :], be1s[:, :], shift1[:, :], ALU.subtract).then_inc(s["shift_done"], 1)

        @block.tensor
        def _(pe):
            pe.wait_ge(s["consts_set"], 4)
            pe.wait_ge(s["w1_in"], 16)
            for c in range(CT):
                for t in range(HT):
                    ins = nc.tensor.transpose(pre_ps[:, c, t * P:(t + 1) * P], w1s[:, t, c * P:(c + 1) * P],
                                              ident[:, :])
                ins.then_inc(s["w1_ready"], 1)
            pe.wait_ge(s["aug_done"], T)
            for m in range(T):
                for t in range(T):
                    ins = nc.tensor.matmul(pre_ps[:, HT - 1, m:m + 1], adjs[:, t, m * P:(m + 1) * P], ones[:, :],
                                           start=t == 0, stop=t == T - 1)
            ins.then_inc(s["colsum_done"], 1)
            pe.wait_ge(s["rows_scaled"], T)
            for m in range(T):
                if m >= 2:
                    pe.wait_ge(s["at_done"], m - 1)
                for t in range(T):
                    ins = nc.tensor.transpose(ag_ps[:, m % 2, t // 4, (t % 4) * P:(t % 4 + 1) * P],
                                              adjs[:, t, m * P:(m + 1) * P], ident[:, :])
                ins.then_inc(s["at_ready"], 1)
            pe.wait_ge(s["atl_done"], T)
            pe.wait_ge(s["w1l_done"], CT)

            def pair(g, last):
                for e in range(2):
                    b = 2 * g + e
                    wait(pe, s["x1l_done"], b + 1)
                    for j in range(NH):
                        wait(pe, s["agl_done"], 2 * b + j - 1)
                        cols = slice(j * BANK, (j + 1) * BANK)
                        for c in range(CT):
                            ch = slice(c * P, (c + 1) * P)
                            for m in range(T):
                                terms = [(x1_hi, a_hi), (x1_lo, a_hi), (x1_hi, a_lo)]
                                for k, (l, r) in enumerate(terms):
                                    ins = nc.tensor.matmul(ag_ps[:, j, c, :], l[:, m, ch], r[:, m, cols],
                                                           start=m == 0 and k == 0, stop=m == T - 1 and k == 2)
                        ins.then_inc(s["ag_ready"], 1)
                    for j in range(NH):
                        wait(pe, s["agl_done"], 2 * b + j + 1)
                        cols = slice(j * BANK, (j + 1) * BANK)
                        for t in range(HT):
                            wait(pe, s["pre_done"], 8 * b + 4 * j + t - 3)
                            for c in range(CT):
                                hid = slice(t * P, (t + 1) * P)
                                terms = [(w1_hi, agg_hi), (w1_lo, agg_hi), (w1_hi, agg_lo)]
                                for k, (l, r) in enumerate(terms):
                                    ins = nc.tensor.matmul(pre_ps[:, t, :], l[:, c, hid], r[:, c, cols],
                                                           start=c == 0 and k == 0, stop=c == CT - 1 and k == 2)
                            ins.then_inc(s["pre_ready"], 1)

            over_batches(pe, B // 2, pair)


def output_layer(nc, pre1, w2, b2, g2, be2, scale1, shift1, scale2, shift2, pre2):
    B, H, N = pre1.shape
    O = w2.shape[0]
    HT, OT, NH = H // P, O // P, N // BANK

    pre1_v = pre1.rearrange("b (t p) n -> b p t n", p=P)
    w2_v = w2.rearrange("(t p) h -> p t h", p=P)

    with ExitStack() as ctx:
        def sb(name, shape, dt=F32):
            return ctx.enter_context(nc.sbuf_tensor(name, shape, dt))

        def sem(name):
            return ctx.enter_context(nc.semaphore(name))

        ident = sb("ident_c", [P, P])
        neg_half = sb("neg_half_c", [P, OT])
        hid = sb("hid", [P, 2, HT, N])
        hid_hi = sb("hid_hi", [P, HT, N], F32R)
        hid_lo = sb("hid_lo", [P, HT, N], F32R)
        w2s = hid[:, 0, 0, :].rearrange("p (t h) -> p t h", t=OT)
        w2_hi = sb("w2_hi", [P, HT, O], F32R)
        w2_lo = sb("w2_lo", [P, HT, O], F32R)
        b2s = sb("b2s", [P, OT])
        g2s = sb("g2s", [P, OT])
        be2s = sb("be2s", [P, OT])
        stats = sb("stats2", [P, OT, B * NH, 6])
        mv = sb("mv2", [P, OT, 2])
        veps = sb("veps2", [P, OT])
        rstd = sb("rstd2", [P, OT])
        out_ps = ctx.enter_context(nc.psum_tensor("out_ps", [P, NH, OT, BANK], F32))
        w2_ps = ctx.enter_context(nc.psum_tensor("w2_ps", [P, HT, O], F32))

        s = {n: sem("c_" + n) for n in (
            "w2_in", "vec_in", "consts_set", "w2_ready", "w2h_done", "w2l_done", "relu_done", "hh_done", "hl_done",
            "out_ready", "pre2_done", "stats_done", "mv_done", "veps_done", "rstd_done", "scale_done", "shift_done")}
        pre_in = [sem(f"c_pre_in{e}") for e in range(2)]

        block = ctx.enter_context(nc.Block())

        @block.sync
        def _(sp):
            sp.dma_start(w2s, w2_v).then_inc(s["w2_in"], 16)
            for t, src in ((b2s, b2), (g2s, g2), (be2s, be2)):
                sp.dma_start(t[:, :], src.rearrange("(t p) -> p t", p=P), allow_slow_non_contiguous=True)\
                    .then_inc(s["vec_in"], 16)

            def load(b, e):
                wait(sp, s["hl_done"], 2 * b - 2)
                sp.dma_start(hid[:, e, :, :], pre1_v[b]).then_inc(pre_in[e], 16)

            def pair(g, last):
                if not last:
                    for e in range(2):
                        load(2 * g + e + 2, e)

            load(1, 1)
            sp.wait_ge(s["w2_ready"], 1)
            load(0, 0)
            over_batches(sp, B // 2, pair)

        @block.gpsimd
        def _(pool):
            pool.memset(ident[:, :], 0.0).then_inc(s["consts_set"], 1)
            pool.memset(neg_half[:, :], -0.5).then_inc(s["consts_set"], 1)
            pool.wait_ge(s["consts_set"], 2)
            pool.affine_select(out=ident[:, :], in_=ident[:, :], compare_op=ALU.not_equal, fill=1.0, base=0,
                               pattern=[[-1, P]], channel_multiplier=1).then_inc(s["consts_set"], 1)
            pool.wait_ge(s["veps_done"], 1)
            pool.tensor_tensor(rstd[:, :], veps[:, :], neg_half[:, :], ALU.pow).then_inc(s["rstd_done"], 1)

        @block.scalar
        def _(act):
            act.wait_ge(s["w2_ready"], 1)
            nc.scalar.activation(w2_hi[:, :, :], w2_ps[:, :, :], ACT.Copy).then_inc(s["w2h_done"], 1)
            act.wait_ge(s["vec_in"], 48)

            def relu(b, e, g, j):
                if j == 0:
                    wait(act, pre_in[e], 16 * (g + 1))
                for t in range(HT):
                    part = hid[:, e, t, j * BANK:(j + 1) * BANK]
                    nc.scalar.activation(part, part, ACT.Relu, bias=shift1[:, t:t + 1], scale=scale1[:, t:t + 1])\
                        .then_inc(s["relu_done"], 1)

            def pair(g, last):
                for e in range(2):
                    b = 2 * g + e
                    for j in range(NH):
                        if j + 1 < NH:
                            relu(b, e, g, j + 1)
                        elif not (last and e == 1):
                            relu(b + 1, 1 - e, g + e, 0)
                        wait(act, s["out_ready"], 2 * b + j + 1)
                        for o in range(OT):
                            nc.scalar.activation(pre2[:, o, NH * b + j, :], out_ps[:, j, o, :], ACT.Identity,
                                                 bias=b2s[:, o:o + 1]).then_inc(s["pre2_done"], 1)

            relu(0, 0, 0, 0)
            over_batches(act, B // 2, pair)

        @block.vector
        def _(dve):
            dve.wait_ge(s["w2h_done"], 1)
            nc.vector.tensor_tensor(w2_lo[:, :, :], w2_ps[:, :, :], w2_hi[:, :, :].bitcast(F32), ALU.subtract)\
                .then_inc(s["w2l_done"], 1)

            def split(b, e, j):
                cols = slice(j * BANK, (j + 1) * BANK)
                wait(dve, s["relu_done"], 8 * b + 4 * j + 4)
                wait(dve, s["out_ready"], 2 * b + j - 1)
                nc.vector.tensor_copy(hid_hi[:, :, cols], hid[:, e, :, cols]).then_inc(s["hh_done"], 1)
                wait(dve, s["hh_done"], 2 * b + j + 1)
                nc.vector.tensor_tensor(hid_lo[:, :, cols], hid[:, e, :, cols], hid_hi[:, :, cols].bitcast(F32),
                                        ALU.subtract).then_inc(s["hl_done"], 1)

            def pair(g, last):
                for e in range(2):
                    b = 2 * g + e
                    for j in range(NH):
                        if j + 1 < NH:
                            split(b, e, j + 1)
                        elif not (last and e == 1):
                            split(b + 1, 1 - e, 0)
                        for o in range(OT):
                            wait(dve, s["pre2_done"], 4 * b + 2 * j + o + 1)
                            nc.vector.bn_stats(stats[:, o, NH * b + j, :], pre2[:, o, NH * b + j, :])\
                                .then_inc(s["stats_done"], 1)

            split(0, 0, 0)
            over_batches(dve, B // 2, pair)
            wait(dve, s["stats_done"], 4 * B)
            for o in range(OT):
                nc.vector.bn_aggr(mv[:, o, :], stats[:, o, :, :]).then_inc(s["mv_done"], 1)
            dve.wait_ge(s["mv_done"], OT)
            nc.vector.tensor_scalar(veps[:, :].rearrange("p (t o) -> p t o", o=1), mv[:, :, 1:2], EPS, None, ALU.add)\
                .then_inc(s["veps_done"], 1)
            dve.wait_ge(s["rstd_done"], 1)
            dve.wait_ge(s["vec_in"], 48)
            nc.vector.tensor_tensor(scale2[:, :], g2s[:, :], rstd[:, :], ALU.mult).then_inc(s["scale_done"], 1)
            dve.wait_ge(s["scale_done"], 1)
            nc.vector.tensor_tensor(shift2[:, :], mv[:, :, 0], scale2[:, :], ALU.mult).then_inc(s["shift_done"], 1)
            dve.wait_ge(s["shift_done"], 1)
            nc.vector.tensor_tensor(shift2[:, :], be2s[:, :], shift2[:, :], ALU.subtract).then_inc(s["shift_done"], 1)

        @block.tensor
        def _(pe):
            pe.wait_ge(s["consts_set"], 3)
            pe.wait_ge(s["w2_in"], 16)
            for t in range(HT):
                for o in range(OT):
                    ins = nc.tensor.transpose(w2_ps[:, t, o * P:(o + 1) * P], w2s[:, o, t * P:(t + 1) * P],
                                              ident[:, :])
            ins.then_inc(s["w2_ready"], 1)
            pe.wait_ge(s["w2l_done"], 1)

            def pair(g, last):
                for e in range(2):
                    b = 2 * g + e
                    for j in range(NH):
                        wait(pe, s["hl_done"], 2 * b + j + 1)
                        wait(pe, s["pre2_done"], 4 * b + 2 * j - 2)
                        cols = slice(j * BANK, (j + 1) * BANK)
                        for o in range(OT):
                            ch = slice(o * P, (o + 1) * P)
                            for t in range(HT):
                                terms = [(w2_hi, hid_hi), (w2_lo, hid_hi), (w2_hi, hid_lo)]
                                for k, (l, r) in enumerate(terms):
                                    ins = nc.tensor.matmul(out_ps[:, j, o, :], l[:, t, ch], r[:, t, cols],
                                                           start=t == 0 and k == 0, stop=t == HT - 1 and k == 2)
                        ins.then_inc(s["out_ready"], 1)

            over_batches(pe, B // 2, pair)


def final_layer(nc, x1, pre2, scale2, shift2, out):
    B, N, C = x1.shape
    T, CT, NH = N // P, C // P, N // BANK
    R = 4

    x1_v = x1.rearrange("b (t p) c -> b p t c", p=P)
    out_v = out.rearrange("b (t p) c -> b p t c", p=P)

    with ExitStack() as ctx:
        def sb(name, shape, dt=F32):
            return ctx.enter_context(nc.sbuf_tensor(name, shape, dt))

        def sem(name):
            return ctx.enter_context(nc.semaphore(name))

        ident = sb("ident_d", [P, P])
        neg_half = sb("neg_half_d", [P, T])
        y = sb("y", [P, R, T, C])
        z = sb("z", [P, 2, CT, N])
        stats = sb("stats3", [P, 2, T, 6])
        mean = sb("mean3", [P, 2, T])
        part = sb("part3", [P, 3, T])
        veps = sb("veps3", [P, 2, T])
        rstd = sb("rstd3", [P, 2, T])
        z_ps = ctx.enter_context(nc.psum_tensor("z_ps", [P, 2, T, C], F32))

        s = {n: sem("d_" + n) for n in (
            "consts_set", "z_done", "zT_ready", "added", "stats_done", "mv_done", "veps_done", "rstd_done", "y_done")}
        x1_in = [sem(f"d_x1_in{r}") for r in range(R)]
        y_out = [sem(f"d_y_out{r}") for r in range(R)]

        block = ctx.enter_context(nc.Block())

        @block.sync
        def _(sp):
            def load(b, r, g):
                wait(sp, y_out[r], 16 * g)
                sp.dma_start(y[:, r, :, :], x1_v[b]).then_inc(x1_in[r], 16)

            def group(g, last):
                for r in range(R):
                    b = R * g + r
                    wait(sp, s["y_done"], b + 1)
                    sp.dma_start(out_v[b], y[:, r, :, :]).then_inc(y_out[r], 16)
                    if r > 0 and not last:
                        load(b + R - 1, r - 1, g + 1)
                if not last:
                    load(R * g + 2 * R - 1, R - 1, g + 1)

            for r in range(R):
                load(r, r, 0)
            over_batches(sp, B // R, group)
            for r in range(R):
                wait(sp, y_out[r], 16 * (B // R))

        @block.gpsimd
        def _(pool):
            pool.memset(ident[:, :], 0.0).then_inc(s["consts_set"], 1)
            pool.memset(neg_half[:, :], -0.5).then_inc(s["consts_set"], 1)
            pool.wait_ge(s["consts_set"], 2)
            pool.affine_select(out=ident[:, :], in_=ident[:, :], compare_op=ALU.not_equal, fill=1.0, base=0,
                               pattern=[[-1, P]], channel_multiplier=1).then_inc(s["consts_set"], 1)

            def group(g, last):
                for r in range(R):
                    wait(pool, s["veps_done"], R * g + r + 1)
                    pool.tensor_tensor(rstd[:, r % 2, :], veps[:, r % 2, :], neg_half[:, :], ALU.pow)\
                        .then_inc(s["rstd_done"], 1)

            over_batches(pool, B // R, group)

        @block.scalar
        def _(act):
            def group(g, last):
                for r in range(R):
                    b = R * g + r
                    wait(act, s["zT_ready"], b - 1)
                    for c in range(CT):
                        nc.scalar.activation(z[:, r % 2, c, :],
                                             pre2[:, c, bass.ds(NH * b, NH), :].rearrange("p j n -> p (j n)"),
                                             ACT.Identity, bias=shift2[:, c:c + 1], scale=scale2[:, c:c + 1])\
                            .then_inc(s["z_done"], 1)

            over_batches(act, B // R, group)

        @block.vector
        def _(dve):
            def normalise(b, r):
                wait(dve, s["rstd_done"], b + 1)
                for n in range(T):
                    last = nc.vector.tensor_scalar(y[:, r, n, :], y[:, r, n, :], mean[:, r % 2, n:n + 1],
                                                   rstd[:, r % 2, n:n + 1], ALU.subtract, ALU.mult)
                last.then_inc(s["y_done"], 1)

            def group(g, last):
                for r in range(R):
                    b = R * g + r
                    wait(dve, s["zT_ready"], b + 1)
                    wait(dve, x1_in[r], 16 * (g + 1))
                    nc.vector.tensor_tensor(y[:, r, :, :], z_ps[:, r % 2, :, :], y[:, r, :, :], ALU.add)\
                        .then_inc(s["added"], 1)
                    wait(dve, s["added"], b + 1)
                    for n in range(T):
                        nc.vector.bn_stats(stats[:, r % 2, n, :], y[:, r, n, :]).then_inc(s["stats_done"], 1)
                    wait(dve, s["stats_done"], T * (b + 1))
                    row_moments(nc, dve, stats[:, r % 2, :, :], part, mean[:, r % 2, :], veps[:, r % 2, :], C,
                                s["mv_done"], s["veps_done"], 6 * b)
                    if r > 0 or not isinstance(g, int) or g > 0:
                        normalise(b - 1, (r - 1) % R)

            over_batches(dve, B // R, group)
            normalise(B - 1, R - 1)

        @block.tensor
        def _(pe):
            pe.wait_ge(s["consts_set"], 3)

            def group(g, last):
                for r in range(R):
                    b = R * g + r
                    wait(pe, s["z_done"], 2 * b + 2)
                    wait(pe, s["added"], b - 1)
                    for n in range(T):
                        for c in range(CT):
                            ins = nc.tensor.transpose(z_ps[:, r % 2, n, c * P:(c + 1) * P],
                                                      z[:, r % 2, c, n * P:(n + 1) * P], ident[:, :])
                    ins.then_inc(s["zT_ready"], 1)

            over_batches(pe, B // R, group)


def program(nc, x, adj, para, kv_w, w1, b1, g1, be1, w2, b2, g2, be2, out):
    B, N, C = x.shape
    H, O = w1.shape[0], w2.shape[0]
    x1 = nc.dram_tensor("x1_scratch", [B, N, C], F32).ap()
    pre1 = nc.dram_tensor("pre1_scratch", [B, H, N], F32).ap()
    attention_layer(nc, x, adj, para, kv_w, x1)
    with ExitStack() as ctx:
        scale1 = ctx.enter_context(nc.sbuf_tensor("scale1", [P, H // P], F32))
        shift1 = ctx.enter_context(nc.sbuf_tensor("shift1", [P, H // P], F32))
        scale2 = ctx.enter_context(nc.sbuf_tensor("scale2", [P, O // P], F32))
        shift2 = ctx.enter_context(nc.sbuf_tensor("shift2", [P, O // P], F32))
        aggregate_layer(nc, x1, adj, w1, b1, g1, be1, scale1, shift1, pre1)
        pre2 = ctx.enter_context(nc.sbuf_tensor("pre2", [P, O // P, B * (N // BANK), BANK], F32))
        output_layer(nc, pre1, w2, b2, g2, be2, scale1, shift1, scale2, shift2, pre2)
        final_layer(nc, x1, pre2, scale2, shift2, out)


_INS = ['x', 'adj', 'L0_gnn_para', 'L0_gnn_kv_w', 'L1_gnn_W1', 'L1_gnn_b1', 'L1_gnn_g1', 'L1_gnn_be1',
        'L1_gnn_W2', 'L1_gnn_b2', 'L1_gnn_g2', 'L1_gnn_be2']


def kernel(**inputs):
    import numpy as _np
    import concourse.bacc as _bacc
    from concourse import mybir as _mybir
    from concourse.bass_utils import run_bass_kernel_spmd as _run

    nc = _bacc.Bacc("TRN2", target_bir_lowering=False, num_devices=1)
    arrays, args = {}, []
    for name in _INS:
        a = _np.ascontiguousarray(inputs[name])
        arrays[f"in_{name}_dram"] = a
        args.append(nc.dram_tensor(f"in_{name}_dram", a.shape, _mybir.dt.from_np(a.dtype), kind="ExternalInput").ap())
    args.append(nc.dram_tensor("out_0_dram", arrays["in_x_dram"].shape, _mybir.dt.float32,
                               kind="ExternalOutput").ap())
    program(nc, *args)
    r = _run(nc, [arrays], core_ids=[0])
    return r.results[0]["out_0_dram"]
```

```python
import concourse.bass as bass
from concourse import mybir
from contextlib import ExitStack

F32 = mybir.dt.float32
F32R = mybir.dt.float32r
ALU = mybir.AluOpType
ACT = mybir.ActivationFunctionType
AX = mybir.AxisListType

P = 128
BANK = 512
HEADS = 4
EPS = 1e-5


def wait(eng, sem, count):
    if isinstance(count, int) and count <= 0:
        return
    eng.wait_ge(sem, count)


def over_batches(eng, n, body):
    body(0, n == 1)
    if n > 2:
        with eng.Fori(1, n - 1) as b:
            body(b, False)
    if n > 1:
        body(n - 1, True)


def row_moments(nc, dve, stats, part, mean, veps, n, part_done, veps_done, base):
    mean_a, mean_b, sq_a, sq_b = (stats[:, :, k] for k in (1, 4, 2, 5))
    nc.vector.tensor_tensor(part[:, 0, :], mean_a, mean_b, ALU.add).then_inc(part_done, 1)
    nc.vector.tensor_tensor(part[:, 1, :], mean_a, mean_b, ALU.subtract).then_inc(part_done, 1)
    nc.vector.tensor_tensor(part[:, 2, :], sq_a, sq_b, ALU.add).then_inc(part_done, 1)
    wait(dve, part_done, base + 3)
    nc.vector.tensor_scalar(mean, part[:, 0, :], 0.5, None, ALU.mult).then_inc(part_done, 1)
    nc.vector.tensor_tensor(part[:, 1, :], part[:, 1, :], part[:, 1, :], ALU.mult).then_inc(part_done, 1)
    wait(dve, part_done, base + 5)
    nc.vector.scalar_tensor_tensor(part[:, 2, :], part[:, 2, :], 4.0 / n, part[:, 1, :], ALU.mult, ALU.add)\
        .then_inc(part_done, 1)
    wait(dve, part_done, base + 6)
    nc.vector.tensor_scalar(veps, part[:, 2, :], 0.25, EPS, ALU.mult, ALU.add).then_inc(veps_done, 1)


def attention_layer(nc, x, adj, para, kv_w, x1):
    B, N, C = x.shape
    T = N // P
    CT = C // P
    HD = C // HEADS
    NH = N // BANK
    SCALE = (1.0 + 1e-6) / (HD ** 0.5 + 1e-6)
    WR, DR, AR, PR = 3, 3, 2, 3
    MAX_BEFORE = [0, 1, 1, 1, 1, 1, 0, 0]
    MAX_AFTER = [1, 1, 1, 0, 0, 0, 0, 0]
    ROW_STEP = 6
    SUM_STEP, BACK_STEP = 1, 3
    POOL_ADDS = T - 2

    x_v = x.rearrange("b (t p) c -> b p t c", p=P)
    x1_v = x1.rearrange("b (t p) c -> b p t c", p=P)
    adj_v = adj.rearrange("(t p) m -> t p m", p=P)
    para_v = para.rearrange("o (c p) h w -> p (o c) (h w)", p=P)
    kvw_v = kv_w.rearrange("(c p) n -> p c n", p=P)

    with ExitStack() as ctx:
        def sb(name, shape, dt=F32):
            return ctx.enter_context(nc.sbuf_tensor(name, shape, dt))

        def pb(name, shape):
            return ctx.enter_context(nc.psum_tensor(name, shape, F32))

        def sem(name):
            return ctx.enter_context(nc.semaphore(name))

        ident = sb("ident", [P, P])
        mean_w = sb("mean_w", [P, P], F32R)
        neg_para = sb("neg_para", [P, CT, N])
        kvw_hi = sb("kvw_hi", [P, CT, 2 * C], F32R)
        kvw_lo = sb("kvw_lo", [P, CT, 2 * C], F32R)
        adj_ring = sb("adj_ring", [P, AR, N])
        scr = sb("scr", [P, DR, N])
        w_hi = sb("w_hi", [P, WR, N], F32R)
        w_lo = sb("w_lo", [P, WR, N], F32R)
        x32 = sb("x32", [P, T, C])
        x_hi = sb("x_hi", [P, T, C], F32R)
        x_lo = sb("x_lo", [P, T, C], F32R)
        xT_hi = sb("xT_hi", [P, CT, N], F32R)
        xT_lo = sb("xT_lo", [P, CT, N], F32R)
        cb = sb("cb", [P, N])
        ccol = sb("ccol", [P, T])
        csum = sb("csum", [P, T])
        ka = [sb(f"ka{h}", [P, N], F32R) for h in range(HEADS)]
        kb = [sb(f"kb{h}", [P, N], F32R) for h in range(HEADS)]
        qa = [sb(f"qa{h}", [P, N], F32R) for h in range(HEADS)]
        qb = [sb(f"qb{h}", [P, N], F32R) for h in range(HEADS)]
        v = sb("v", [P, T, C])
        probs = sb("probs", [P, PR, N])
        psum = sb("psum", [P, N])
        ones = sb("ones_a", [P, 1])
        rden = sb("rden", [P, 2, T])
        res = sb("res", [P, T, C])
        heads_t = sb("heads_t", [P, 2, BANK])
        mxs = sb("mxs", [P, T])
        row = sb("row", [T, P], F32R)
        stats = sb("stats", [P, T, 6])
        mean = sb("mean", [P, T])
        part = sb("part", [P, 3, T])
        veps = sb("veps", [P, T])
        rstd = sb("rstd", [P, T])
        neg_half = sb("neg_half", [P, T])

        sc_ps = pb("sc_ps", [P, 2, N])
        pv_ps = pb("pv_ps", [P, 2, BANK])
        mx_ps = pb("mx_ps", [P, 2, BANK])

        def own(h):
            return slice(HD * (h % 2), HD * (h % 2) + HD)

        def other(h):
            return slice(HD - HD * (h % 2), 2 * HD - HD * (h % 2))

        s = {n: sem(n) for n in (
            "const_in", "ident_set", "consts_set", "x_in", "res_in", "x1_out", "row_in",
            "xt_ready", "cb_ready", "k_ready", "g_step", "g_first", "v_ready", "mx_ready", "st_ready", "pv_done", "rowT_ready",
            "xth_done", "cb_done", "abs_done", "tanh_done", "whi_done", "kh_done", "qh_done", "v_evac", "exp_done",
            "xhi_done", "x_split", "csum_done", "ccol_done", "xtl_done", "w_done", "wlo_done", "kl_done", "qt_done",
            "ql_done", "max_done", "row_done", "pool_added", "acc_done", "sum_ready", "rden_done",
            "copied_out", "back_ready", "res_added", "stats_done", "mv_done", "veps_done", "rstd_done", "res_done", "kvw_hi_done")}
        adj_in = [sem(f"adj_in{i}") for i in range(AR)]
        qa_in = [sem(f"qa_in{h}") for h in range(HEADS)]
        kb_in = [sem(f"kb_in{h}") for h in range(HEADS)]

        block = ctx.enter_context(nc.Block())

        @block.sync
        def _(sp):
            sp.dma_start(neg_para[:, :, :], para_v).then_inc(s["const_in"], 16)
            sp.dma_start(scr[:, 0, :].rearrange("p (c n) -> p c n", c=CT), kvw_v).then_inc(s["const_in"], 16)

            def load_adj(b, n):
                wait(sp, s["w_done"], 8 * b + n - 1)
                sp.dma_start(adj_ring[:, n % AR, :], adj_v[n]).then_inc(adj_in[n % AR], 16)

            def load_x(b):
                wait(sp, s["xt_ready"], 2 * b)
                wait(sp, s["x_split"], b)
                wait(sp, s["csum_done"], b)
                sp.dma_start(x32[:, :, :], x_v[b]).then_inc(s["x_in"], 16)

            def copy_kb(b, h):
                wait(sp, s["kh_done"], 4 * b + h + 1)
                sp.dma_start(kb[h][own(h), :].bitcast(F32), ka[h][own(h), :].bitcast(F32)).then_inc(kb_in[h], 16)

            def copy_qa(b, h):
                wait(sp, s["qh_done"], 4 * b + h + 1)
                sp.dma_start(qa[h][other(h), :].bitcast(F32), qa[h][own(h), :].bitcast(F32)).then_inc(qa_in[h], 16)

            def store_row(b, h):
                wait(sp, s["row_done"], 4 * b + h + 1)
                r = other(h).start
                sp.dma_start(qb[h][r:r + 1, :].rearrange("o (t p) -> o t p", p=P).bitcast(F32), row[:, :].bitcast(F32)).then_inc(s["row_in"], 16)

            def store_x1(b):
                wait(sp, s["res_done"], b + 1)
                sp.dma_start(x1_v[b], res[:, :, :]).then_inc(s["x1_out"], 16)

            def body(b, last):
                if not last:
                    load_x(b + 1)
                for n in range(3, T):
                    load_adj(b, n)
                if not isinstance(b, int) or b > 0:
                    store_x1(b - 1)
                wait(sp, s["x1_out"], 16 * b)
                sp.dma_start(res[:, :, :], x_v[b]).then_inc(s["res_in"], 16)
                copy_qa(b, 0)
                copy_qa(b, 1)
                copy_kb(b, 2)
                copy_kb(b, 3)
                copy_qa(b, 2)
                copy_qa(b, 3)
                store_row(b, 0)
                if not last:
                    load_adj(b + 1, 0)
                    load_adj(b + 1, 1)
                for h in range(1, HEADS):
                    store_row(b, h)
                if not last:
                    copy_kb(b + 1, 0)
                    copy_kb(b + 1, 1)
                    load_adj(b + 1, 2)

            load_x(0)
            load_adj(0, 0)
            load_adj(0, 1)
            copy_kb(0, 0)
            copy_kb(0, 1)
            load_adj(0, 2)
            over_batches(sp, B, body)
            store_x1(B - 1)
            wait(sp, s["x1_out"], 16 * B)

        @block.gpsimd
        def _(pool):
            pool.memset(ident[:, :], 0.0).then_inc(s["ident_set"], 1)
            pool.wait_ge(s["ident_set"], 1)
            pool.affine_select(out=ident[:, :], in_=ident[:, :], compare_op=ALU.not_equal, fill=1.0, base=0,
                               pattern=[[-1, P]], channel_multiplier=1).then_inc(s["ident_set"], 1)
            pool.memset(neg_half[:, :], -0.5).then_inc(s["ident_set"], 1)
            pool.wait_ge(s["ident_set"], 3)

            def rsqrt(b):
                wait(pool, s["veps_done"], b + 1)
                pool.tensor_tensor(rstd[:, :], veps[:, :], neg_half[:, :], ALU.pow).then_inc(s["rstd_done"], 1)

            def body(b, last):
                if not isinstance(b, int) or b > 0:
                    rsqrt(b - 1)
                for h in range(HEADS):
                    for k in range(1, POOL_ADDS + 1):
                        done = POOL_ADDS * (4 * b + h) + k - 1
                        if k == 1:
                            wait(pool, s["sum_ready"], 4 * b + h)
                        else:
                            wait(pool, s["pool_added"], done)
                        wait(pool, s["exp_done"], 32 * b + 8 * h + k + 1)
                        pool.tensor_tensor(psum[:, :], probs[:, 0, :] if k == 1 else psum[:, :],
                                           probs[:, k % PR, :], ALU.add).then_inc(s["pool_added"], 1)

            over_batches(pool, B, body)
            rsqrt(B - 1)

        @block.scalar
        def _(act):
            def xt_high(b, half):
                wait(act, s["xt_ready"], 2 * b + half + 1)
                nc.scalar.activation(xT_hi[:, :, half * BANK:(half + 1) * BANK], mx_ps[:, :, :], ACT.Copy)\
                    .then_inc(s["xth_done"], 1)

            def mean_rows(b):
                wait(act, s["cb_ready"], b + 1)
                nc.scalar.activation(cb[:, :], mx_ps[:, :, :].rearrange("p a n -> p (a n)"), ACT.Copy)\
                    .then_inc(s["cb_done"], 1)

            def distance(b, n):
                if n == 0:
                    wait(act, s["cb_done"], b + 1)
                    wait(act, s["ccol_done"], b + 1)
                    wait(act, s["ql_done"], 4 * b)
                else:
                    wait(act, s["wlo_done"], 8 * b + n - 2)
                nc.scalar.activation(scr[:, n % DR, :], cb[:, :], ACT.Abs, bias=ccol[:, n:n + 1])\
                    .then_inc(s["abs_done"], 1)

            def tanh_half(b, n):
                wait(act, s["abs_done"], 8 * b + n + 1)
                d = scr[:, n % DR, :]
                nc.scalar.activation(d, d, ACT.Tanh, scale=0.5).then_inc(s["tanh_done"], 1)

            def w_high(b, n):
                wait(act, s["w_done"], 8 * b + n + 1)
                wait(act, s["g_step"], 8 * b if n < WR else 8 * b + n - WR + 1)
                nc.scalar.activation(w_hi[:, n % WR, :], scr[:, n % DR, :], ACT.Copy).then_inc(s["whi_done"], 1)

            def k_high(b, h):
                wait(act, s["k_ready"], 2 * b + h // 2 + 1)
                src = (mx_ps, pv_ps)[h // 2]
                nc.scalar.activation(ka[h][own(h), :], src[own(h), :, :].rearrange("p a n -> p (a n)"), ACT.Copy)\
                    .then_inc(s["kh_done"], 1)

            def q_high(b, h):
                wait(act, s["qt_done"], 2 * b + h // 2 + 1)
                nc.scalar.activation(qa[h][own(h), :], scr[own(h), h // 2, :], ACT.Relu).then_inc(s["qh_done"], 1)

            def v_copy(b, j):
                wait(act, s["v_ready"], 2 * b + j + 1)
                nc.scalar.activation(v[:, 4 * j:4 * j + 4, :], mx_ps[:, :, :].rearrange("p a (m c) -> p (a m) c", m=2),
                                     ACT.Copy).then_inc(s["v_evac"], 1)

            def exponential(b, h, i):
                t = 8 * h + i
                wait(act, s["st_ready"], 32 * b + t + 1)
                wait(act, s["pv_done"], 32 * b + t + 1 - (2 if i < 2 else 5 if i == 2 else PR))
                if i == 1:
                    wait(act, s["acc_done"], 4 * b + h)
                elif i != 2:
                    wait(act, s["pool_added"], POOL_ADDS * (4 * b + h) + (max(1, i - PR) if i else 0))
                nc.scalar.activation(probs[:, i % PR, :], sc_ps[:, t % 2, :], ACT.Exp, scale=SCALE)\
                    .then_inc(s["exp_done"], 1)

            def head_copy(b, h):
                wait(act, s["pv_done"], 32 * b + 8 * h + 8)
                wait(act, s["back_ready"], 4 * b + h - 1)
                nc.scalar.activation(heads_t[:, h % 2, :], pv_ps[:, h % 2, :], ACT.Copy).then_inc(s["copied_out"], 1)

            def x_high(b):
                wait(act, s["x_in"], 16 * (b + 1))
                wait(act, s["g_step"], 8 * b)
                for half in range(2):
                    tiles = slice(half * T // 2, (half + 1) * T // 2)
                    nc.scalar.activation(x_hi[:, tiles, :], x32[:, tiles, :], ACT.Copy).then_inc(s["xhi_done"], 1)

            def prepare(b, h, i):
                if (h, i) == (0, 7):
                    xt_high(b, 0)
                if (h, i) == (1, 3):
                    x_high(b)
                if (h, i) == (1, 7):
                    xt_high(b, 1)
                if (h, i) == (2, 7):
                    mean_rows(b)
                if (h, i) == (3, 0):
                    distance(b, 0)
                    tanh_half(b, 0)
                if (h, i) == (3, 1):
                    distance(b, 1)
                if (h, i) == (3, 2):
                    tanh_half(b, 1)
                if (h, i) == (3, 3):
                    k_high(b, 0)
                    k_high(b, 1)
                if (h, i) == (3, 4):
                    distance(b, 2)
                    w_high(b, 0)
                if (h, i) == (3, 5):
                    tanh_half(b, 2)
                if (h, i) == (3, 6):
                    w_high(b, 1)
                if (h, i) == (3, 7):
                    w_high(b, 2)

            def body(b, last):
                before = not isinstance(b, int) or b > 0
                if before:
                    head_copy(b - 1, HEADS - 1)
                for n in range(3, T + 1):
                    if n < T:
                        distance(b, n)
                        tanh_half(b, n)
                    if n > 3:
                        w_high(b, n - 1)
                q_high(b, 0)
                q_high(b, 1)
                v_copy(b, 0)
                k_high(b, 2)
                k_high(b, 3)
                q_high(b, 2)
                q_high(b, 3)
                v_copy(b, 1)
                for h in range(HEADS):
                    for i in range(T):
                        if h and i == 1:
                            head_copy(b, h - 1)
                        exponential(b, h, i)
                        if not last:
                            prepare(b + 1, h, i)

            for h in range(HEADS):
                for i in range(T):
                    prepare(0, h, i)
            over_batches(act, B, body)
            head_copy(B - 1, HEADS - 1)

        @block.vector
        def _(dve):
            dve.memset(cb[:, 0:P], 1.0 / C).then_inc(s["consts_set"], 1)
            for h in range(HEADS):
                o = other(h)
                dve.memset(kb[h][o, :].bitcast(F32), 0.0).then_inc(s["consts_set"], 1)
                dve.memset(qb[h][o, :].bitcast(F32), 0.0).then_inc(s["consts_set"], 1)
            dve.wait_ge(s["consts_set"], 1 + 2 * HEADS)
            nc.vector.tensor_copy(mean_w[:, :], cb[:, 0:P]).then_inc(s["consts_set"], 1)
            for h in range(HEADS):
                r = other(h).start
                dve.memset(kb[h][r:r + 1, :].bitcast(F32), 1.0).then_inc(s["consts_set"], 1)
            dve.memset(ones[:, :], 1.0).then_inc(s["consts_set"], 1)
            dve.wait_ge(s["const_in"], 32)
            nc.vector.tensor_scalar(neg_para[:, :, :], neg_para[:, :, :], -1.0, None, ALU.mult)\
                .then_inc(s["consts_set"], 1)
            kvw32 = scr[:, 0, :].rearrange("p (c n) -> p c n", c=CT)
            nc.vector.tensor_copy(kvw_hi[:, :, :], kvw32).then_inc(s["consts_set"], 1)
            dve.wait_ge(s["consts_set"], 4 + 3 * HEADS + 1)
            nc.vector.tensor_tensor(kvw_lo[:, :, :], kvw32, kvw_hi[:, :, :].bitcast(F32), ALU.subtract)\
                .then_inc(s["consts_set"], 1)

            def split_x(b):
                wait(dve, s["xhi_done"], 2 * b + 2)
                nc.vector.tensor_tensor(x_lo[:, :, :], x32[:, :, :], x_hi[:, :, :].bitcast(F32), ALU.subtract)\
                    .then_inc(s["x_split"], 1)

            def sum_channels(b):
                wait(dve, s["x_in"], 16 * (b + 1))
                nc.vector.tensor_reduce(csum[:, :], x32[:, :, :], AX.X, ALU.add).then_inc(s["csum_done"], 1)

            def mean_columns(b):
                wait(dve, s["tanh_done"], 8 * b)
                wait(dve, s["csum_done"], b + 1)
                nc.vector.tensor_scalar(ccol[:, :], csum[:, :], -1.0 / C, None, ALU.mult).then_inc(s["ccol_done"], 1)

            def xt_low(b, half):
                wait(dve, s["xth_done"], 2 * b + half + 1)
                cols = slice(half * BANK, (half + 1) * BANK)
                nc.vector.tensor_tensor(xT_lo[:, :, cols], mx_ps[:, :, :], xT_hi[:, :, cols].bitcast(F32),
                                        ALU.subtract).then_inc(s["xtl_done"], 1)

            def weigh(b, n):
                wait(dve, s["tanh_done"], 8 * b + n + 1)
                wait(dve, adj_in[n % AR], 16 * (4 * b + n // AR + 1))
                d = scr[:, n % DR, :]
                nc.vector.scalar_tensor_tensor(d, d, -1.0, adj_ring[:, n % AR, :], ALU.add, ALU.mult)\
                    .then_inc(s["w_done"], 1)

            def w_low(b, n):
                wait(dve, s["whi_done"], 8 * b + n + 1)
                nc.vector.tensor_tensor(w_lo[:, n % WR, :], scr[:, n % DR, :], w_hi[:, n % WR, :].bitcast(F32),
                                        ALU.subtract).then_inc(s["wlo_done"], 1)

            def k_low(b, h):
                wait(dve, s["kh_done"], 4 * b + h + 1)
                src = (mx_ps, pv_ps)[h // 2]
                nc.vector.tensor_tensor(ka[h][other(h), :], src[own(h), :, :].rearrange("p a n -> p (a n)"),
                                        ka[h][own(h), :].bitcast(F32), ALU.subtract).then_inc(s["kl_done"], 1)

            def q_times_para(b, c):
                if c == 0:
                    wait(dve, s["g_first"], b + 1)
                else:
                    wait(dve, s["g_step"], 8 * b + 8)
                nc.vector.tensor_tensor(scr[:, c, :], sc_ps[:, c, :], neg_para[:, c, :], ALU.mult)\
                    .then_inc(s["qt_done"], 1)

            def q_low(b, h):
                wait(dve, s["qh_done"], 4 * b + h + 1)
                nc.vector.scalar_tensor_tensor(qb[h][own(h), :], scr[own(h), h // 2, :], 0.0,
                                               qa[h][own(h), :].bitcast(F32), ALU.max, ALU.subtract)\
                    .then_inc(s["ql_done"], 1)

            def maxima(b, h, tiles):
                for n in tiles:
                    wait(dve, s["mx_ready"], 32 * b + 8 * h + n + 1)
                    src = mx_ps[:, :, :].rearrange("p a n -> p (a n)") if h else sc_ps[:, n % 2, :]
                    nc.vector.tensor_reduce(mxs[:, n:n + 1], src, AX.X, ALU.max).then_inc(s["max_done"], 1)

            def maxima_row(b, h):
                wait(dve, s["rowT_ready"], 4 * b + h + 1)
                wait(dve, s["row_in"], 16 * (4 * b + h))
                src = (mx_ps if h else sc_ps)[0:T, 0, 0:P]
                nc.vector.tensor_scalar(row[:, :], src, -1.0, None, ALU.mult).then_inc(s["row_done"], 1)

            def add_last(b, h):
                wait(dve, s["exp_done"], 32 * b + 8 * h + 8)
                wait(dve, s["pool_added"], POOL_ADDS * (4 * b + h + 1))
                nc.vector.tensor_tensor(psum[:, :], psum[:, :], probs[:, (T - 1) % PR, :], ALU.add)\
                    .then_inc(s["acc_done"], 1)

            def invert_sums(b, h):
                wait(dve, s["sum_ready"], 4 * b + h + 1)
                nc.vector.reciprocal(rden[:, h % 2, :], pv_ps[:, h % 2, 0:T]).then_inc(s["rden_done"], 1)

            def add_head(b, h):
                wait(dve, s["back_ready"], 4 * b + h + 1)
                wait(dve, s["rden_done"], 4 * b + h + 1)
                if h == 0:
                    wait(dve, s["res_in"], 16 * (b + 1))
                for n in range(T):
                    out = res[:, n, h * HD:(h + 1) * HD]
                    col = (n % 4) * P + (n // 4) * HD
                    last = nc.vector.scalar_tensor_tensor(out, pv_ps[:, h % 2, col:col + HD],
                                                          rden[:, h % 2, n:n + 1], out, ALU.mult, ALU.add)
                last.then_inc(s["res_added"], 1)

            def row_stats(b):
                wait(dve, s["res_added"], 4 * b + 4)
                for n in range(T):
                    nc.vector.bn_stats(stats[:, n, :], res[:, n, :]).then_inc(s["stats_done"], 1)

            def moments(b):
                wait(dve, s["stats_done"], T * (b + 1))
                row_moments(nc, dve, stats, part, mean[:, :], veps[:, :], C, s["mv_done"], s["veps_done"], 6 * b)

            def normalise(b):
                wait(dve, s["rstd_done"], b + 1)
                for n in range(T):
                    last = nc.vector.tensor_scalar(res[:, n, :], res[:, n, :], mean[:, n:n + 1], rstd[:, n:n + 1],
                                                   ALU.subtract, ALU.mult)
                last.then_inc(s["res_done"], 1)

            def body(b, last):
                before = not isinstance(b, int) or b > 0
                if before:
                    add_last(b - 1, HEADS - 1)
                weigh(b, 3)
                if before:
                    invert_sums(b - 1, HEADS - 1)
                weigh(b, 4)
                w_low(b, 3)
                if before:
                    add_head(b - 1, HEADS - 1)
                weigh(b, 5)
                w_low(b, 4)
                if before:
                    row_stats(b - 1)
                weigh(b, 6)
                w_low(b, 5)
                if before:
                    moments(b - 1)
                weigh(b, 7)
                w_low(b, 6)
                w_low(b, 7)
                if before:
                    normalise(b - 1)
                q_times_para(b, 0)
                q_times_para(b, 1)
                maxima(b, 0, range(T))
                maxima_row(b, 0)
                q_low(b, 0)
                k_low(b, 2)
                k_low(b, 3)
                maxima(b, 1, range(0, 5))
                q_low(b, 1)
                maxima(b, 1, range(5, 7))
                q_low(b, 2)
                maxima(b, 1, range(7, T))
                maxima_row(b, 1)
                if not last:
                    xt_low(b + 1, 0)
                q_low(b, 3)
                for h in (1, 2):
                    add_last(b, h - 1)
                    maxima(b, h + 1, range(0, 3))
                    invert_sums(b, h - 1)
                    maxima(b, h + 1, range(3, 6))
                    add_head(b, h - 1)
                    maxima(b, h + 1, range(6, T))
                    maxima_row(b, h + 1)
                    if h == 1 and not last:
                        xt_low(b + 1, 1)
                    if h == 2 and not last:
                        sum_channels(b + 1)
                        mean_columns(b + 1)
                add_last(b, 2)
                if not last:
                    weigh(b + 1, 0)
                invert_sums(b, 2)
                if not last:
                    weigh(b + 1, 1)
                add_head(b, 2)
                if not last:
                    k_low(b + 1, 0)
                    k_low(b + 1, 1)
                    split_x(b + 1)
                    w_low(b + 1, 0)
                    weigh(b + 1, 2)
                    w_low(b + 1, 1)
                    w_low(b + 1, 2)

            xt_low(0, 0)
            xt_low(0, 1)
            sum_channels(0)
            mean_columns(0)
            for n in range(2):
                weigh(0, n)
            k_low(0, 0)
            k_low(0, 1)
            split_x(0)
            w_low(0, 0)
            weigh(0, 2)
            w_low(0, 1)
            w_low(0, 2)
            over_batches(dve, B, body)
            add_last(B - 1, HEADS - 1)
            invert_sums(B - 1, HEADS - 1)
            add_head(B - 1, HEADS - 1)
            row_stats(B - 1)
            moments(B - 1)
            normalise(B - 1)

        @block.tensor
        def _(pe):
            def product(out, terms):
                for k, (lhsT, rhs) in enumerate(terms):
                    ins = nc.tensor.matmul(out, lhsT, rhs, start=k == 0, stop=k == len(terms) - 1)
                return ins

            def split_terms(pairs):
                out = []
                for (a_hi, a_lo), (b_hi, b_lo) in pairs:
                    out += [(a_hi, b_hi), (a_lo, b_hi), (a_hi, b_lo)]
                return out

            def transpose_x(b, half):
                wait(pe, s["x_in"], 16 * (b + 1))
                wait(pe, s["xtl_done"], 2 * b + half)
                wait(pe, s["row_done"], 4 * b - 2 + half)
                for c in range(CT):
                    for q in range(4):
                        ins = nc.tensor.transpose(mx_ps[:, c, q * P:(q + 1) * P],
                                                  x32[:, 4 * half + q, c * P:(c + 1) * P], ident[:, :])
                ins.then_inc(s["xt_ready"], 1)

            def broadcast_means(b):
                wait(pe, s["xtl_done"], 2 * b + 2)
                wait(pe, s["row_done"], 4 * b)
                for nh in range(NH):
                    cols = slice(nh * BANK, (nh + 1) * BANK)
                    ins = product(mx_ps[:, nh, :], [(mean_w[:, :], t[:, c, cols]) for c in range(CT)
                                                    for t in (xT_hi, xT_lo)])
                ins.then_inc(s["cb_ready"], 1)

            def k_product(b, c, halves=range(NH)):
                if c == 0:
                    wait(pe, s["cb_done"], b + 1)
                else:
                    wait(pe, s["res_added"], 4 * b)
                out = (mx_ps, pv_ps)[c]
                ws = slice(c * P, (c + 1) * P)
                for nh in halves:
                    cols = slice(nh * BANK, (nh + 1) * BANK)
                    ins = product(out[:, nh, :], split_terms(
                        [((kvw_hi[:, k, ws], kvw_lo[:, k, ws]), (xT_hi[:, k, cols], xT_lo[:, k, cols]))
                         for k in range(CT)]))
                if nh == NH - 1:
                    ins.then_inc(s["k_ready"], 1)

            def v_product(b, j):
                if j == 0:
                    wait(pe, s["kl_done"], 4 * b + 2)
                else:
                    wait(pe, s["v_evac"], 2 * b + 1)
                for m in range(4):
                    rows = slice((4 * j + m) * P, (4 * j + m + 1) * P)
                    ins = product(mx_ps[:, m // 2, (m % 2) * C:(m % 2 + 1) * C], split_terms(
                        [((xT_hi[:, k, rows], xT_lo[:, k, rows]), (kvw_hi[:, k, C:2 * C], kvw_lo[:, k, C:2 * C]))
                         for k in range(CT)]))
                ins.then_inc(s["v_ready"], 1)

            def g_product(b):
                before = not isinstance(b, int) or b > 0
                wait(pe, s["exp_done"], 32 * b)
                wait(pe, s["x_split"], b + 1)
                for n in range(T):
                    wait(pe, s["wlo_done"], 8 * b + n + 1)
                    for c in range(CT):
                        ch = slice(c * P, (c + 1) * P)
                        for nh in range(NH):
                            cols = slice(nh * BANK, (nh + 1) * BANK)
                            terms = split_terms([((x_hi[:, n, ch], x_lo[:, n, ch]),
                                                  (w_hi[:, n % WR, cols], w_lo[:, n % WR, cols]))])
                            for k, (lhsT, rhs) in enumerate(terms):
                                ins = nc.tensor.matmul(sc_ps[:, c, cols], lhsT, rhs,
                                                       start=n == 0 and k == 0, stop=n == T - 1 and k == 2)
                        if n == T - 1 and c == 0:
                            ins.then_inc(s["g_first"], 1)
                    ins.then_inc(s["g_step"], 1)
                    if before and n == 1:
                        sum_up(b - 1, HEADS - 1)
                    if before and n == 3:
                        transpose_back(b - 1, HEADS - 1)

            def max_scores(b, h, n, last=True):
                if h == 0:
                    if n == 0:
                        wait(pe, s["qh_done"], 4 * b + 1)
                        wait(pe, s["kh_done"], 4 * b + 1)
                    if n < 2:
                        wait(pe, s["qt_done"], 2 * b + n + 1)
                    else:
                        wait(pe, s["max_done"], 32 * b + n - 1)
                elif n == 0:
                    wait(pe, s["row_done"], 4 * b + h)
                    wait(pe, s["qh_done"], 4 * b + h + 1)
                    if h == 1:
                        wait(pe, s["v_evac"], 2 * b + 2)
                    elif not last:
                        wait(pe, s["xtl_done"], 2 * b + h + 1)
                else:
                    wait(pe, s["max_done"], 32 * b + 8 * h + n)
                for nh in range(NH):
                    out = mx_ps[:, nh, :] if h else sc_ps[:, n % 2, nh * BANK:(nh + 1) * BANK]
                    ins = nc.tensor.matmul(out, qa[h][own(h), n * P:(n + 1) * P],
                                           ka[h][own(h), nh * BANK:(nh + 1) * BANK], start=True, stop=True)
                ins.then_inc(s["mx_ready"], 1)

            def transpose_maxima(b, h):
                wait(pe, s["max_done"], 32 * b + 8 * h + 8)
                out = (mx_ps if h else sc_ps)[0:T, 0, 0:P]
                nc.tensor.transpose(out, mxs[:, :], ident[:, :]).then_inc(s["rowT_ready"], 1)

            def scores(b, h, i):
                t = 8 * h + i
                wait(pe, s["exp_done"], 32 * b + t - 1)
                if t < 2:
                    wait(pe, s["qt_done"], 2 * b + t + 1)
                if i == 0:
                    wait(pe, s["row_in"], 16 * (4 * b + h + 1))
                    wait(pe, qa_in[h], 16 * (b + 1))
                    wait(pe, kb_in[h], 16 * (b + 1))
                    wait(pe, s["ql_done"], 4 * b + h + 1)
                    wait(pe, s["kl_done"], 4 * b + h + 1)
                keys = slice(i * P, (i + 1) * P)
                for nh in range(NH):
                    cols = slice(nh * BANK, (nh + 1) * BANK)
                    ins = product(sc_ps[:, t % 2, cols], [(ka[h][:, keys], qa[h][:, cols]),
                                                          (kb[h][:, keys], qb[h][:, cols])])
                ins.then_inc(s["st_ready"], 1)

            def values(b, h, i):
                t = 8 * h + i
                wait(pe, s["exp_done"], 32 * b + t + 1)
                if i == 0 and h < 2:
                    wait(pe, s["v_evac"], 2 * b + 2)
                    wait(pe, s["kl_done"], 4 * b + 4)
                elif i == 0:
                    wait(pe, s["res_added"], 4 * b + h - 1)
                for nh in range(NH):
                    ins = nc.tensor.matmul(pv_ps[nh * HD:(nh + 1) * HD, h % 2, :], v[:, i, h * HD:(h + 1) * HD],
                                           probs[:, i % PR, nh * BANK:(nh + 1) * BANK],
                                           start=i == 0, stop=i == T - 1)
                ins.then_inc(s["pv_done"], 1)

            def sum_up(b, h):
                wait(pe, s["acc_done"], 4 * b + h + 1)
                wait(pe, s["copied_out"], 4 * b + h + 1)
                for n in range(T):
                    ins = nc.tensor.matmul(pv_ps[:, h % 2, n:n + 1], psum[:, n * P:(n + 1) * P], ones[:, :],
                                           start=True, stop=True)
                ins.then_inc(s["sum_ready"], 1)

            def transpose_back(b, h):
                wait(pe, s["rden_done"], 4 * b + h + 1)
                for q in range(4):
                    ins = nc.tensor.transpose(pv_ps[:, h % 2, q * P:(q + 1) * P],
                                              heads_t[:, h % 2, q * P:(q + 1) * P], ident[:, :])
                ins.then_inc(s["back_ready"], 1)

            def prepare(b, h, i):
                if (h, i) == (0, 7):
                    transpose_x(b, 0)
                if (h, i) == (1, 7):
                    transpose_x(b, 1)
                if (h, i) == (2, 7):
                    broadcast_means(b)
                if (h, i) == (3, 1):
                    k_product(b, 0)

            def body(b, last):
                g_product(b)
                v_product(b, 0)
                max_scores(b, 0, 0)
                max_scores(b, 0, 1)
                k_product(b, 1, [0])
                max_scores(b, 0, 2)
                k_product(b, 1, [1])
                for n in range(3, T):
                    max_scores(b, 0, n)
                transpose_maxima(b, 0)
                v_product(b, 1)
                for h in range(HEADS):
                    n = 0
                    more = h + 1 < HEADS
                    for i in range(T):
                        scores(b, h, i)
                        if more and MAX_BEFORE[i]:
                            max_scores(b, h + 1, n, last)
                            n += 1
                        if more and i == ROW_STEP:
                            transpose_maxima(b, h + 1)
                        if not last:
                            prepare(b + 1, h, i)
                        if h + i:
                            values(b, h if i else h - 1, i - 1 if i else T - 1)
                        if more and MAX_AFTER[i]:
                            max_scores(b, h + 1, n, last)
                            n += 1
                        if h and i == SUM_STEP:
                            sum_up(b, h - 1)
                        if h and i == BACK_STEP:
                            transpose_back(b, h - 1)
                values(b, HEADS - 1, T - 1)

            pe.wait_ge(s["ident_set"], 3)
            pe.wait_ge(s["consts_set"], 6 + 3 * HEADS)
            for h in range(HEADS):
                for i in range(T):
                    prepare(0, h, i)
            over_batches(pe, B, body)
            sum_up(B - 1, HEADS - 1)
            transpose_back(B - 1, HEADS - 1)


def aggregate_layer(nc, x1, adj, w1, b1, g1, be1, scale1, shift1, pre1):
    B, N, C = x1.shape
    H = w1.shape[0]
    T, CT, HT, NH = N // P, C // P, H // P, N // BANK

    x1_v = x1.rearrange("b (t p) c -> b p t c", p=P)
    adj_v = adj.rearrange("(t p) m -> p t m", p=P)
    w1_v = w1.rearrange("(t p) c -> p t c", p=P)
    pre1_v = pre1.rearrange("b (t p) n -> b p t n", p=P)

    with ExitStack() as ctx:
        def sb(name, shape, dt=F32):
            return ctx.enter_context(nc.sbuf_tensor(name, shape, dt))

        def pb(name, shape):
            return ctx.enter_context(nc.psum_tensor(name, shape, F32))

        def sem(name):
            return ctx.enter_context(nc.semaphore(name))

        ident = sb("ident_b", [P, P])
        ones = sb("ones", [P, 1])
        neg_half = sb("neg_half_b", [P, T])
        a_hi = sb("a_hi", [P, T, N], F32R)
        a_lo = sb("a_lo", [P, T, N], F32R)
        at32 = sb("at32", [P, 2, N])
        pre = sb("pre", [P, 2, HT, N])
        adjs = pre[:, :, :, :].rearrange("p e t n -> p (e t) n")
        w1s = sb("w1s", [P, HT, C])
        w1_hi = sb("w1_hi", [P, CT, H], F32R)
        w1_lo = sb("w1_lo", [P, CT, H], F32R)
        x1s = sb("x1s", [P, 2, T, C])
        x1_hi = sb("x1_hi", [P, T, C], F32R)
        x1_lo = sb("x1_lo", [P, T, C], F32R)
        agg_hi = sb("agg_hi", [P, CT, N], F32R)
        agg_lo = sb("agg_lo", [P, CT, N], F32R)
        block_diag = sb("block_diag", [P, T, P])
        diag = sb("diag", [P, T])
        rowsum = sb("rowsum", [P, T])
        deg = sb("deg", [P, T])
        dinv = sb("dinv", [P, T])
        b1s = sb("b1s", [P, HT])
        g1s = sb("g1s", [P, HT])
        be1s = sb("be1s", [P, HT])
        stats = sb("stats1", [P, HT, B * NH, 6])
        mv = sb("mv1", [P, HT, 2])
        veps = sb("veps1", [P, HT])
        rstd = sb("rstd1", [P, HT])

        ag_ps = pb("ag_ps", [P, NH, CT, BANK])
        pre_ps = pb("pre_ps", [P, HT, BANK])

        s = {n: sem("b_" + n) for n in (
            "adj_in", "w1_in", "vec_in", "consts_set", "aug_done", "diag_done", "rowsum_done", "colsum_done", "deg_done",
            "dinv_done", "rows_scaled", "at_ready", "at_done", "ath_done", "atl_done", "w1_ready", "w1h_done",
            "w1l_done", "x1h_done", "x1l_done", "ag_ready", "agh_done", "agl_done", "pre_ready", "pre_done",
            "stats_done", "mv_done", "veps_done", "rstd_done", "scale_done", "shift_done")}
        x1_in = [sem(f"b_x1_in{e}") for e in range(2)]
        pre_out = [sem(f"b_pre_out{e}") for e in range(2)]

        block = ctx.enter_context(nc.Block())

        @block.sync
        def _(sp):
            sp.dma_start(adjs, adj_v).then_inc(s["adj_in"], 16)
            sp.dma_start(w1s[:, :, :], w1_v).then_inc(s["w1_in"], 16)
            for t, src in ((b1s, b1), (g1s, g1), (be1s, be1)):
                sp.dma_start(t[:, :], src.rearrange("(t p) -> p t", p=P), allow_slow_non_contiguous=True)\
                    .then_inc(s["vec_in"], 16)

            def load(b, e):
                wait(sp, s["x1l_done"], b - 1)
                sp.dma_start(x1s[:, e, :, :], x1_v[b]).then_inc(x1_in[e], 16)

            def pair(g, last):
                for e in range(2):
                    wait(sp, s["pre_done"], 8 * (2 * g + e) + 8)
                    sp.dma_start(pre1_v[2 * g + e], pre[:, e, :, :]).then_inc(pre_out[e], 16)
                    if not last:
                        load(2 * g + e + 2, e)

            load(0, 0)
            load(1, 1)
            over_batches(sp, B // 2, pair)
            for e in range(2):
                wait(sp, pre_out[e], 16 * (B // 2))

        @block.gpsimd
        def _(pool):
            pool.memset(ident[:, :], 0.0).then_inc(s["consts_set"], 1)
            pool.memset(ones[:, :], 1.0).then_inc(s["consts_set"], 1)
            pool.memset(neg_half[:, :], -0.5).then_inc(s["consts_set"], 1)
            pool.wait_ge(s["consts_set"], 3)
            pool.affine_select(out=ident[:, :], in_=ident[:, :], compare_op=ALU.not_equal, fill=1.0, base=0,
                               pattern=[[-1, P]], channel_multiplier=1).then_inc(s["consts_set"], 1)
            pool.wait_ge(s["deg_done"], 1)
            pool.tensor_tensor(dinv[:, :], deg[:, :], neg_half[:, :], ALU.pow).then_inc(s["dinv_done"], 1)
            pool.wait_ge(s["veps_done"], 1)
            pool.tensor_tensor(rstd[:, :], veps[:, :], neg_half[:, 0:HT], ALU.pow).then_inc(s["rstd_done"], 1)

        @block.scalar
        def _(act):
            for c in range(CT):
                act.wait_ge(s["w1_ready"], c + 1)
                nc.scalar.activation(w1_hi[:, c, :], pre_ps[:, c, :], ACT.Copy).then_inc(s["w1h_done"], 1)
            for m in range(T):
                act.wait_ge(s["at_done"], m + 1)
                nc.scalar.activation(a_hi[:, m, :], at32[:, m % 2, :], ACT.Copy).then_inc(s["ath_done"], 1)
            act.wait_ge(s["vec_in"], 48)

            def pair(g, last):
                for e in range(2):
                    b = 2 * g + e
                    for j in range(NH):
                        wait(act, s["ag_ready"], 2 * b + j + 1)
                        nc.scalar.activation(agg_hi[:, :, j * BANK:(j + 1) * BANK], ag_ps[:, j, :, :], ACT.Copy)\
                            .then_inc(s["agh_done"], 1)
                    wait(act, pre_out[e], 16 * g)
                    wait(act, s["stats_done"], 8 * b - 8)
                    for j in range(NH):
                        for t in range(HT):
                            wait(act, s["pre_ready"], 8 * b + 4 * j + t + 1)
                            nc.scalar.activation(pre[:, e, t, j * BANK:(j + 1) * BANK], pre_ps[:, t, :],
                                                 ACT.Identity, bias=b1s[:, t:t + 1]).then_inc(s["pre_done"], 1)

            over_batches(act, B // 2, pair)

        @block.vector
        def _(dve):
            dve.wait_ge(s["adj_in"], 16)
            dve.wait_ge(s["consts_set"], 4)
            for t in range(T):
                blk = adjs[:, t, t * P:(t + 1) * P]
                nc.vector.tensor_tensor(blk, blk, ident[:, :], ALU.add).then_inc(s["aug_done"], 1)
            dve.wait_ge(s["aug_done"], T)
            for t in range(T):
                nc.vector.tensor_tensor(block_diag[:, t, :], adjs[:, t, t * P:(t + 1) * P], ident[:, :], ALU.mult)\
                    .then_inc(s["diag_done"], 1)
            nc.vector.tensor_reduce(rowsum[:, :], adjs, AX.X, ALU.add).then_inc(s["rowsum_done"], 1)
            dve.wait_ge(s["diag_done"], T)
            nc.vector.tensor_reduce(diag[:, :], block_diag[:, :, :], AX.X, ALU.add).then_inc(s["diag_done"], 1)
            dve.wait_ge(s["rowsum_done"], 1)
            dve.wait_ge(s["colsum_done"], 1)
            nc.vector.tensor_tensor(rowsum[:, :], pre_ps[:, HT - 1, 0:T], rowsum[:, :], ALU.add)\
                .then_inc(s["rowsum_done"], 1)
            dve.wait_ge(s["rowsum_done"], 2)
            dve.wait_ge(s["diag_done"], T + 1)
            nc.vector.tensor_tensor(deg[:, :], rowsum[:, :], diag[:, :], ALU.subtract).then_inc(s["deg_done"], 1)
            for c in range(CT):
                dve.wait_ge(s["w1h_done"], c + 1)
                nc.vector.tensor_tensor(w1_lo[:, c, :], pre_ps[:, c, :], w1_hi[:, c, :].bitcast(F32), ALU.subtract)\
                    .then_inc(s["w1l_done"], 1)
            dve.wait_ge(s["dinv_done"], 1)
            for t in range(T):
                nc.vector.tensor_scalar(adjs[:, t, :], adjs[:, t, :], dinv[:, t:t + 1], None, ALU.mult)\
                    .then_inc(s["rows_scaled"], 1)

            def a_low(m):
                dve.wait_ge(s["ath_done"], m + 1)
                nc.vector.tensor_tensor(a_lo[:, m, :], at32[:, m % 2, :], a_hi[:, m, :].bitcast(F32), ALU.subtract)\
                    .then_inc(s["atl_done"], 1)

            for m in range(T):
                dve.wait_ge(s["at_ready"], m + 1)
                if m >= 2:
                    a_low(m - 2)
                    dve.wait_ge(s["atl_done"], m - 1)
                nc.vector.tensor_scalar(at32[:, m % 2, :], ag_ps[:, m % 2, :, :].rearrange("p c n -> p (c n)"),
                                        dinv[:, m:m + 1], None, ALU.mult).then_inc(s["at_done"], 1)
            a_low(T - 2)
            a_low(T - 1)

            def split(b, e, g):
                wait(dve, x1_in[e], 16 * (g + 1))
                wait(dve, s["ag_ready"], 2 * b)
                nc.vector.tensor_copy(x1_hi[:, :, :], x1s[:, e, :, :]).then_inc(s["x1h_done"], 1)
                wait(dve, s["x1h_done"], b + 1)
                nc.vector.tensor_tensor(x1_lo[:, :, :], x1s[:, e, :, :], x1_hi[:, :, :].bitcast(F32),
                                        ALU.subtract).then_inc(s["x1l_done"], 1)

            def pair(g, last):
                for e in range(2):
                    b = 2 * g + e
                    for j in range(NH):
                        wait(dve, s["agh_done"], 2 * b + j + 1)
                        cols = slice(j * BANK, (j + 1) * BANK)
                        nc.vector.tensor_tensor(agg_lo[:, :, cols], ag_ps[:, j, :, :],
                                                agg_hi[:, :, cols].bitcast(F32), ALU.subtract)\
                            .then_inc(s["agl_done"], 1)
                    if not (last and e == 1):
                        split(b + 1, 1 - e, g + e)
                    for j in range(NH):
                        for t in range(HT):
                            wait(dve, s["pre_done"], 8 * b + 4 * j + t + 1)
                            nc.vector.bn_stats(stats[:, t, NH * b + j, :], pre[:, e, t, j * BANK:(j + 1) * BANK])\
                                .then_inc(s["stats_done"], 1)

            split(0, 0, 0)
            over_batches(dve, B // 2, pair)
            wait(dve, s["stats_done"], 8 * B)
            for t in range(HT):
                nc.vector.bn_aggr(mv[:, t, :], stats[:, t, :, :]).then_inc(s["mv_done"], 1)
            dve.wait_ge(s["mv_done"], HT)
            nc.vector.tensor_scalar(veps[:, :].rearrange("p (t o) -> p t o", o=1), mv[:, :, 1:2], EPS, None, ALU.add)\
                .then_inc(s["veps_done"], 1)
            dve.wait_ge(s["rstd_done"], 1)
            nc.vector.tensor_tensor(scale1[:, :], g1s[:, :], rstd[:, :], ALU.mult).then_inc(s["scale_done"], 1)
            dve.wait_ge(s["scale_done"], 1)
            nc.vector.tensor_tensor(shift1[:, :], mv[:, :, 0], scale1[:, :], ALU.mult).then_inc(s["shift_done"], 1)
            dve.wait_ge(s["shift_done"], 1)
            nc.vector.tensor_tensor(shift1[:, :], be1s[:, :], shift1[:, :], ALU.subtract).then_inc(s["shift_done"], 1)

        @block.tensor
        def _(pe):
            pe.wait_ge(s["consts_set"], 4)
            pe.wait_ge(s["w1_in"], 16)
            for c in range(CT):
                for t in range(HT):
                    ins = nc.tensor.transpose(pre_ps[:, c, t * P:(t + 1) * P], w1s[:, t, c * P:(c + 1) * P],
                                              ident[:, :])
                ins.then_inc(s["w1_ready"], 1)
            pe.wait_ge(s["aug_done"], T)
            for m in range(T):
                for t in range(T):
                    ins = nc.tensor.matmul(pre_ps[:, HT - 1, m:m + 1], adjs[:, t, m * P:(m + 1) * P], ones[:, :],
                                           start=t == 0, stop=t == T - 1)
            ins.then_inc(s["colsum_done"], 1)
            pe.wait_ge(s["rows_scaled"], T)
            for m in range(T):
                if m >= 2:
                    pe.wait_ge(s["at_done"], m - 1)
                for t in range(T):
                    ins = nc.tensor.transpose(ag_ps[:, m % 2, t // 4, (t % 4) * P:(t % 4 + 1) * P],
                                              adjs[:, t, m * P:(m + 1) * P], ident[:, :])
                ins.then_inc(s["at_ready"], 1)
            pe.wait_ge(s["atl_done"], T)
            pe.wait_ge(s["w1l_done"], CT)

            def pair(g, last):
                for e in range(2):
                    b = 2 * g + e
                    wait(pe, s["x1l_done"], b + 1)
                    for j in range(NH):
                        wait(pe, s["agl_done"], 2 * b + j - 1)
                        cols = slice(j * BANK, (j + 1) * BANK)
                        for c in range(CT):
                            ch = slice(c * P, (c + 1) * P)
                            for m in range(T):
                                terms = [(x1_hi, a_hi), (x1_lo, a_hi), (x1_hi, a_lo)]
                                for k, (l, r) in enumerate(terms):
                                    ins = nc.tensor.matmul(ag_ps[:, j, c, :], l[:, m, ch], r[:, m, cols],
                                                           start=m == 0 and k == 0, stop=m == T - 1 and k == 2)
                        ins.then_inc(s["ag_ready"], 1)
                    for j in range(NH):
                        wait(pe, s["agl_done"], 2 * b + j + 1)
                        cols = slice(j * BANK, (j + 1) * BANK)
                        for t in range(HT):
                            wait(pe, s["pre_done"], 8 * b + 4 * j + t - 3)
                            for c in range(CT):
                                hid = slice(t * P, (t + 1) * P)
                                terms = [(w1_hi, agg_hi), (w1_lo, agg_hi), (w1_hi, agg_lo)]
                                for k, (l, r) in enumerate(terms):
                                    ins = nc.tensor.matmul(pre_ps[:, t, :], l[:, c, hid], r[:, c, cols],
                                                           start=c == 0 and k == 0, stop=c == CT - 1 and k == 2)
                            ins.then_inc(s["pre_ready"], 1)

            over_batches(pe, B // 2, pair)


def output_layer(nc, pre1, w2, b2, g2, be2, scale1, shift1, scale2, shift2, pre2):
    B, H, N = pre1.shape
    O = w2.shape[0]
    HT, OT, NH = H // P, O // P, N // BANK

    pre1_v = pre1.rearrange("b (t p) n -> b p t n", p=P)
    w2_v = w2.rearrange("(t p) h -> p t h", p=P)

    with ExitStack() as ctx:
        def sb(name, shape, dt=F32):
            return ctx.enter_context(nc.sbuf_tensor(name, shape, dt))

        def sem(name):
            return ctx.enter_context(nc.semaphore(name))

        ident = sb("ident_c", [P, P])
        neg_half = sb("neg_half_c", [P, OT])
        hid = sb("hid", [P, 2, HT, N])
        hid_hi = sb("hid_hi", [P, HT, N], F32R)
        hid_lo = sb("hid_lo", [P, HT, N], F32R)
        w2s = hid[:, 0, 0, :].rearrange("p (t h) -> p t h", t=OT)
        w2_hi = sb("w2_hi", [P, HT, O], F32R)
        w2_lo = sb("w2_lo", [P, HT, O], F32R)
        b2s = sb("b2s", [P, OT])
        g2s = sb("g2s", [P, OT])
        be2s = sb("be2s", [P, OT])
        stats = sb("stats2", [P, OT, B * NH, 6])
        mv = sb("mv2", [P, OT, 2])
        veps = sb("veps2", [P, OT])
        rstd = sb("rstd2", [P, OT])
        out_ps = ctx.enter_context(nc.psum_tensor("out_ps", [P, NH, OT, BANK], F32))
        w2_ps = ctx.enter_context(nc.psum_tensor("w2_ps", [P, HT, O], F32))

        s = {n: sem("c_" + n) for n in (
            "w2_in", "vec_in", "consts_set", "w2_ready", "w2h_done", "w2l_done", "relu_done", "hh_done", "hl_done",
            "out_ready", "pre2_done", "stats_done", "mv_done", "veps_done", "rstd_done", "scale_done", "shift_done")}
        pre_in = [sem(f"c_pre_in{e}") for e in range(2)]

        block = ctx.enter_context(nc.Block())

        @block.sync
        def _(sp):
            sp.dma_start(w2s, w2_v).then_inc(s["w2_in"], 16)
            for t, src in ((b2s, b2), (g2s, g2), (be2s, be2)):
                sp.dma_start(t[:, :], src.rearrange("(t p) -> p t", p=P), allow_slow_non_contiguous=True)\
                    .then_inc(s["vec_in"], 16)

            def load(b, e):
                wait(sp, s["hl_done"], 2 * b - 2)
                sp.dma_start(hid[:, e, :, :], pre1_v[b]).then_inc(pre_in[e], 16)

            def pair(g, last):
                if not last:
                    for e in range(2):
                        load(2 * g + e + 2, e)

            load(1, 1)
            sp.wait_ge(s["w2_ready"], 1)
            load(0, 0)
            over_batches(sp, B // 2, pair)

        @block.gpsimd
        def _(pool):
            pool.memset(ident[:, :], 0.0).then_inc(s["consts_set"], 1)
            pool.memset(neg_half[:, :], -0.5).then_inc(s["consts_set"], 1)
            pool.wait_ge(s["consts_set"], 2)
            pool.affine_select(out=ident[:, :], in_=ident[:, :], compare_op=ALU.not_equal, fill=1.0, base=0,
                               pattern=[[-1, P]], channel_multiplier=1).then_inc(s["consts_set"], 1)
            pool.wait_ge(s["veps_done"], 1)
            pool.tensor_tensor(rstd[:, :], veps[:, :], neg_half[:, :], ALU.pow).then_inc(s["rstd_done"], 1)

        @block.scalar
        def _(act):
            act.wait_ge(s["w2_ready"], 1)
            nc.scalar.activation(w2_hi[:, :, :], w2_ps[:, :, :], ACT.Copy).then_inc(s["w2h_done"], 1)
            act.wait_ge(s["vec_in"], 48)

            def relu(b, e, g, j):
                if j == 0:
                    wait(act, pre_in[e], 16 * (g + 1))
                for t in range(HT):
                    part = hid[:, e, t, j * BANK:(j + 1) * BANK]
                    nc.scalar.activation(part, part, ACT.Relu, bias=shift1[:, t:t + 1], scale=scale1[:, t:t + 1])\
                        .then_inc(s["relu_done"], 1)

            def pair(g, last):
                for e in range(2):
                    b = 2 * g + e
                    for j in range(NH):
                        if j + 1 < NH:
                            relu(b, e, g, j + 1)
                        elif not (last and e == 1):
                            relu(b + 1, 1 - e, g + e, 0)
                        wait(act, s["out_ready"], 2 * b + j + 1)
                        for o in range(OT):
                            nc.scalar.activation(pre2[:, o, NH * b + j, :], out_ps[:, j, o, :], ACT.Identity,
                                                 bias=b2s[:, o:o + 1]).then_inc(s["pre2_done"], 1)

            relu(0, 0, 0, 0)
            over_batches(act, B // 2, pair)

        @block.vector
        def _(dve):
            dve.wait_ge(s["w2h_done"], 1)
            nc.vector.tensor_tensor(w2_lo[:, :, :], w2_ps[:, :, :], w2_hi[:, :, :].bitcast(F32), ALU.subtract)\
                .then_inc(s["w2l_done"], 1)

            def split(b, e, j):
                cols = slice(j * BANK, (j + 1) * BANK)
                wait(dve, s["relu_done"], 8 * b + 4 * j + 4)
                wait(dve, s["out_ready"], 2 * b + j - 1)
                nc.vector.tensor_copy(hid_hi[:, :, cols], hid[:, e, :, cols]).then_inc(s["hh_done"], 1)
                wait(dve, s["hh_done"], 2 * b + j + 1)
                nc.vector.tensor_tensor(hid_lo[:, :, cols], hid[:, e, :, cols], hid_hi[:, :, cols].bitcast(F32),
                                        ALU.subtract).then_inc(s["hl_done"], 1)

            def pair(g, last):
                for e in range(2):
                    b = 2 * g + e
                    for j in range(NH):
                        if j + 1 < NH:
                            split(b, e, j + 1)
                        elif not (last and e == 1):
                            split(b + 1, 1 - e, 0)
                        for o in range(OT):
                            wait(dve, s["pre2_done"], 4 * b + 2 * j + o + 1)
                            nc.vector.bn_stats(stats[:, o, NH * b + j, :], pre2[:, o, NH * b + j, :])\
                                .then_inc(s["stats_done"], 1)

            split(0, 0, 0)
            over_batches(dve, B // 2, pair)
            wait(dve, s["stats_done"], 4 * B)
            for o in range(OT):
                nc.vector.bn_aggr(mv[:, o, :], stats[:, o, :, :]).then_inc(s["mv_done"], 1)
            dve.wait_ge(s["mv_done"], OT)
            nc.vector.tensor_scalar(veps[:, :].rearrange("p (t o) -> p t o", o=1), mv[:, :, 1:2], EPS, None, ALU.add)\
                .then_inc(s["veps_done"], 1)
            dve.wait_ge(s["rstd_done"], 1)
            dve.wait_ge(s["vec_in"], 48)
            nc.vector.tensor_tensor(scale2[:, :], g2s[:, :], rstd[:, :], ALU.mult).then_inc(s["scale_done"], 1)
            dve.wait_ge(s["scale_done"], 1)
            nc.vector.tensor_tensor(shift2[:, :], mv[:, :, 0], scale2[:, :], ALU.mult).then_inc(s["shift_done"], 1)
            dve.wait_ge(s["shift_done"], 1)
            nc.vector.tensor_tensor(shift2[:, :], be2s[:, :], shift2[:, :], ALU.subtract).then_inc(s["shift_done"], 1)

        @block.tensor
        def _(pe):
            pe.wait_ge(s["consts_set"], 3)
            pe.wait_ge(s["w2_in"], 16)
            for t in range(HT):
                for o in range(OT):
                    ins = nc.tensor.transpose(w2_ps[:, t, o * P:(o + 1) * P], w2s[:, o, t * P:(t + 1) * P],
                                              ident[:, :])
            ins.then_inc(s["w2_ready"], 1)
            pe.wait_ge(s["w2l_done"], 1)

            def pair(g, last):
                for e in range(2):
                    b = 2 * g + e
                    for j in range(NH):
                        wait(pe, s["hl_done"], 2 * b + j + 1)
                        wait(pe, s["pre2_done"], 4 * b + 2 * j - 2)
                        cols = slice(j * BANK, (j + 1) * BANK)
                        for o in range(OT):
                            ch = slice(o * P, (o + 1) * P)
                            for t in range(HT):
                                terms = [(w2_hi, hid_hi), (w2_lo, hid_hi), (w2_hi, hid_lo)]
                                for k, (l, r) in enumerate(terms):
                                    ins = nc.tensor.matmul(out_ps[:, j, o, :], l[:, t, ch], r[:, t, cols],
                                                           start=t == 0 and k == 0, stop=t == HT - 1 and k == 2)
                        ins.then_inc(s["out_ready"], 1)

            over_batches(pe, B // 2, pair)


def final_layer(nc, x1, pre2, scale2, shift2, out):
    B, N, C = x1.shape
    T, CT, NH = N // P, C // P, N // BANK
    R = 4

    x1_v = x1.rearrange("b (t p) c -> b p t c", p=P)
    out_v = out.rearrange("b (t p) c -> b p t c", p=P)

    with ExitStack() as ctx:
        def sb(name, shape, dt=F32):
            return ctx.enter_context(nc.sbuf_tensor(name, shape, dt))

        def sem(name):
            return ctx.enter_context(nc.semaphore(name))

        ident = sb("ident_d", [P, P])
        neg_half = sb("neg_half_d", [P, T])
        y = sb("y", [P, R, T, C])
        z = sb("z", [P, 2, CT, N])
        stats = sb("stats3", [P, 2, T, 6])
        mean = sb("mean3", [P, 2, T])
        part = sb("part3", [P, 3, T])
        veps = sb("veps3", [P, 2, T])
        rstd = sb("rstd3", [P, 2, T])
        z_ps = ctx.enter_context(nc.psum_tensor("z_ps", [P, 2, T, C], F32))

        s = {n: sem("d_" + n) for n in (
            "consts_set", "z_done", "zT_ready", "added", "stats_done", "mv_done", "veps_done", "rstd_done", "y_done")}
        x1_in = [sem(f"d_x1_in{r}") for r in range(R)]
        y_out = [sem(f"d_y_out{r}") for r in range(R)]

        block = ctx.enter_context(nc.Block())

        @block.sync
        def _(sp):
            def load(b, r, g):
                wait(sp, y_out[r], 16 * g)
                sp.dma_start(y[:, r, :, :], x1_v[b]).then_inc(x1_in[r], 16)

            def group(g, last):
                for r in range(R):
                    b = R * g + r
                    wait(sp, s["y_done"], b + 1)
                    sp.dma_start(out_v[b], y[:, r, :, :]).then_inc(y_out[r], 16)
                    if r > 0 and not last:
                        load(b + R - 1, r - 1, g + 1)
                if not last:
                    load(R * g + 2 * R - 1, R - 1, g + 1)

            for r in range(R):
                load(r, r, 0)
            over_batches(sp, B // R, group)
            for r in range(R):
                wait(sp, y_out[r], 16 * (B // R))

        @block.gpsimd
        def _(pool):
            pool.memset(ident[:, :], 0.0).then_inc(s["consts_set"], 1)
            pool.memset(neg_half[:, :], -0.5).then_inc(s["consts_set"], 1)
            pool.wait_ge(s["consts_set"], 2)
            pool.affine_select(out=ident[:, :], in_=ident[:, :], compare_op=ALU.not_equal, fill=1.0, base=0,
                               pattern=[[-1, P]], channel_multiplier=1).then_inc(s["consts_set"], 1)

            def group(g, last):
                for r in range(R):
                    wait(pool, s["veps_done"], R * g + r + 1)
                    pool.tensor_tensor(rstd[:, r % 2, :], veps[:, r % 2, :], neg_half[:, :], ALU.pow)\
                        .then_inc(s["rstd_done"], 1)

            over_batches(pool, B // R, group)

        @block.scalar
        def _(act):
            def group(g, last):
                for r in range(R):
                    b = R * g + r
                    wait(act, s["zT_ready"], b - 1)
                    for c in range(CT):
                        nc.scalar.activation(z[:, r % 2, c, :],
                                             pre2[:, c, bass.ds(NH * b, NH), :].rearrange("p j n -> p (j n)"),
                                             ACT.Identity, bias=shift2[:, c:c + 1], scale=scale2[:, c:c + 1])\
                            .then_inc(s["z_done"], 1)

            over_batches(act, B // R, group)

        @block.vector
        def _(dve):
            def normalise(b, r):
                wait(dve, s["rstd_done"], b + 1)
                for n in range(T):
                    last = nc.vector.tensor_scalar(y[:, r, n, :], y[:, r, n, :], mean[:, r % 2, n:n + 1],
                                                   rstd[:, r % 2, n:n + 1], ALU.subtract, ALU.mult)
                last.then_inc(s["y_done"], 1)

            def group(g, last):
                for r in range(R):
                    b = R * g + r
                    wait(dve, s["zT_ready"], b + 1)
                    wait(dve, x1_in[r], 16 * (g + 1))
                    nc.vector.tensor_tensor(y[:, r, :, :], z_ps[:, r % 2, :, :], y[:, r, :, :], ALU.add)\
                        .then_inc(s["added"], 1)
                    wait(dve, s["added"], b + 1)
                    for n in range(T):
                        nc.vector.bn_stats(stats[:, r % 2, n, :], y[:, r, n, :]).then_inc(s["stats_done"], 1)
                    wait(dve, s["stats_done"], T * (b + 1))
                    row_moments(nc, dve, stats[:, r % 2, :, :], part, mean[:, r % 2, :], veps[:, r % 2, :], C,
                                s["mv_done"], s["veps_done"], 6 * b)
                    if r > 0 or not isinstance(g, int) or g > 0:
                        normalise(b - 1, (r - 1) % R)

            over_batches(dve, B // R, group)
            normalise(B - 1, R - 1)

        @block.tensor
        def _(pe):
            pe.wait_ge(s["consts_set"], 3)

            def group(g, last):
                for r in range(R):
                    b = R * g + r
                    wait(pe, s["z_done"], 2 * b + 2)
                    wait(pe, s["added"], b - 1)
                    for n in range(T):
                        for c in range(CT):
                            ins = nc.tensor.transpose(z_ps[:, r % 2, n, c * P:(c + 1) * P],
                                                      z[:, r % 2, c, n * P:(n + 1) * P], ident[:, :])
                    ins.then_inc(s["zT_ready"], 1)

            over_batches(pe, B // R, group)


def program(nc, x, adj, para, kv_w, w1, b1, g1, be1, w2, b2, g2, be2, out):
    B, N, C = x.shape
    H, O = w1.shape[0], w2.shape[0]
    x1 = nc.dram_tensor("x1_scratch", [B, N, C], F32).ap()
    pre1 = nc.dram_tensor("pre1_scratch", [B, H, N], F32).ap()
    attention_layer(nc, x, adj, para, kv_w, x1)
    with ExitStack() as ctx:
        scale1 = ctx.enter_context(nc.sbuf_tensor("scale1", [P, H // P], F32))
        shift1 = ctx.enter_context(nc.sbuf_tensor("shift1", [P, H // P], F32))
        scale2 = ctx.enter_context(nc.sbuf_tensor("scale2", [P, O // P], F32))
        shift2 = ctx.enter_context(nc.sbuf_tensor("shift2", [P, O // P], F32))
        aggregate_layer(nc, x1, adj, w1, b1, g1, be1, scale1, shift1, pre1)
        pre2 = ctx.enter_context(nc.sbuf_tensor("pre2", [P, O // P, B * (N // BANK), BANK], F32))
        output_layer(nc, pre1, w2, b2, g2, be2, scale1, shift1, scale2, shift2, pre2)
        final_layer(nc, x1, pre2, scale2, shift2, out)


_INS = ['x', 'adj', 'L0_gnn_para', 'L0_gnn_kv_w', 'L1_gnn_W1', 'L1_gnn_b1', 'L1_gnn_g1', 'L1_gnn_be1',
        'L1_gnn_W2', 'L1_gnn_b2', 'L1_gnn_g2', 'L1_gnn_be2']


def kernel(**inputs):
    import numpy as _np
    import concourse.bacc as _bacc
    from concourse import mybir as _mybir
    from concourse.bass_utils import run_bass_kernel_spmd as _run

    nc = _bacc.Bacc("TRN2", target_bir_lowering=False, num_devices=1)
    arrays, args = {}, []
    for name in _INS:
        a = _np.ascontiguousarray(inputs[name])
        arrays[f"in_{name}_dram"] = a
        args.append(nc.dram_tensor(f"in_{name}_dram", a.shape, _mybir.dt.from_np(a.dtype), kind="ExternalInput").ap())
    args.append(nc.dram_tensor("out_0_dram", arrays["in_x_dram"].shape, _mybir.dt.float32,
                               kind="ExternalOutput").ap())
    program(nc, *args)
    r = _run(nc, [arrays], core_ids=[0])
    return r.results[0]["out_0_dram"]
```

```python
import concourse.bass as bass
from concourse import mybir
from contextlib import ExitStack

F32 = mybir.dt.float32
F32R = mybir.dt.float32r
ALU = mybir.AluOpType
ACT = mybir.ActivationFunctionType
AX = mybir.AxisListType

P = 128
BANK = 512
HEADS = 4
EPS = 1e-5


def wait(eng, sem, count):
    if isinstance(count, int) and count <= 0:
        return
    eng.wait_ge(sem, count)


def over_batches(eng, n, body):
    body(0, n == 1)
    if n > 2:
        with eng.Fori(1, n - 1) as b:
            body(b, False)
    if n > 1:
        body(n - 1, True)


def row_moments(nc, dve, stats, part, mean, veps, n, part_done, veps_done, base, sign=1.0):
    mean_a, mean_b, sq_a, sq_b = (stats[:, :, k] for k in (1, 4, 2, 5))
    nc.vector.tensor_tensor(part[:, 0, :], mean_a, mean_b, ALU.add).then_inc(part_done, 1)
    nc.vector.tensor_tensor(part[:, 1, :], mean_a, mean_b, ALU.subtract).then_inc(part_done, 1)
    nc.vector.tensor_tensor(part[:, 2, :], sq_a, sq_b, ALU.add).then_inc(part_done, 1)
    wait(dve, part_done, base + 3)
    nc.vector.tensor_scalar(mean, part[:, 0, :], 0.5 * sign, None, ALU.mult).then_inc(part_done, 1)
    nc.vector.tensor_tensor(part[:, 1, :], part[:, 1, :], part[:, 1, :], ALU.mult).then_inc(part_done, 1)
    wait(dve, part_done, base + 5)
    nc.vector.scalar_tensor_tensor(part[:, 2, :], part[:, 2, :], 4.0 / n, part[:, 1, :], ALU.mult, ALU.add)\
        .then_inc(part_done, 1)
    wait(dve, part_done, base + 6)
    nc.vector.tensor_scalar(veps, part[:, 2, :], 0.25, EPS, ALU.mult, ALU.add).then_inc(veps_done, 1)


def attention_layer(nc, x, adj, para, kv_w, x1):
    B, N, C = x.shape
    T = N // P
    CT = C // P
    HD = C // HEADS
    NH = N // BANK
    SCALE = (1.0 + 1e-6) / (HD ** 0.5 + 1e-6)
    WR, DR, AR, PR = 3, 3, 2, 3
    MAX_BEFORE = [0, 1, 1, 1, 1, 1, 0, 0]
    MAX_AFTER = [1, 1, 0, 1, 0, 0, 0, 0]
    ROW_STEP = 6
    SUM_STEP, BACK_STEP = 1, 3
    POOL_ADDS = T - 2

    x_v = x.rearrange("b (t p) c -> b p t c", p=P)
    x1_v = x1.rearrange("b (t p) c -> b p t c", p=P)
    adj_v = adj.rearrange("(t p) m -> t p m", p=P)
    para_v = para.rearrange("o (c p) h w -> p (o c) (h w)", p=P)
    kvw_v = kv_w.rearrange("(c p) n -> p c n", p=P)

    with ExitStack() as ctx:
        def sb(name, shape, dt=F32):
            return ctx.enter_context(nc.sbuf_tensor(name, shape, dt))

        def pb(name, shape):
            return ctx.enter_context(nc.psum_tensor(name, shape, F32))

        def sem(name):
            return ctx.enter_context(nc.semaphore(name))

        ident = sb("ident", [P, P])
        mean_w = sb("mean_w", [P, P], F32R)
        neg_para = sb("neg_para", [P, CT, N])
        kvw_hi = sb("kvw_hi", [P, CT, 2 * C], F32R)
        kvw_lo = sb("kvw_lo", [P, CT, 2 * C], F32R)
        adj_ring = sb("adj_ring", [P, AR, N])
        scr = sb("scr", [P, DR, N])
        w_hi = sb("w_hi", [P, WR, N], F32R)
        w_lo = sb("w_lo", [P, WR, N], F32R)
        x32 = sb("x32", [P, T, C])
        x_hi = sb("x_hi", [P, T, C], F32R)
        x_lo = sb("x_lo", [P, T, C], F32R)
        xT_hi = sb("xT_hi", [P, CT, N], F32R)
        xT_lo = sb("xT_lo", [P, CT, N], F32R)
        cb = sb("cb", [P, N])
        ccol = sb("ccol", [P, T])
        csum = sb("csum", [P, T])
        ka = [sb(f"ka{h}", [P, N], F32R) for h in range(HEADS)]
        kb = [sb(f"kb{h}", [P, N], F32R) for h in range(HEADS)]
        qa = [sb(f"qa{h}", [P, N], F32R) for h in range(HEADS)]
        qb = [sb(f"qb{h}", [P, N], F32R) for h in range(HEADS)]
        v = sb("v", [P, T, C])
        probs = sb("probs", [P, PR, N])
        psum = sb("psum", [P, N])
        ones = sb("ones_a", [P, 1])
        rden = sb("rden", [P, 2, T])
        res = sb("res", [P, T, C])
        heads_t = sb("heads_t", [P, 2, BANK])
        mxs = sb("mxs", [P, T])
        mx2 = sb("mx2", [P, NH, T])
        row = sb("row", [T, P], F32R)
        stats = sb("stats", [P, T, 6])
        neg_mean = sb("neg_mean", [P, T])
        part = sb("part", [P, 3, T])
        veps = sb("veps", [P, T])
        rstd = sb("rstd", [P, T])
        shift = sb("shift", [P, T])
        neg_half = sb("neg_half", [P, T])

        sc_ps = pb("sc_ps", [P, 2, N])
        pv_ps = pb("pv_ps", [P, 2, BANK])
        mx_ps = pb("mx_ps", [P, 2, BANK])

        def own(h):
            return slice(HD * (h % 2), HD * (h % 2) + HD)

        def other(h):
            return slice(HD - HD * (h % 2), 2 * HD - HD * (h % 2))

        s = {n: sem(n) for n in (
            "kvw_in", "para_in", "ident_set", "kq_set", "consts_set", "x_in", "res_in", "x1_out", "row_in",
            "xt_ready", "cb_ready", "k_ready", "g_step", "g_first", "v_ready", "mx_ready", "st_ready", "pv_done",
            "rowT_ready",
            "xth_done", "cb_done", "abs_done", "tanh_done", "whi_done", "kh_done", "qh_done", "v_evac", "exp_done",
            "xhi_done", "x_split", "csum_done", "ccol_done", "xtl_done", "w_done", "wlo_done", "kl_done", "qt_done",
            "ql_done", "max_done", "merged", "row_done", "pool_added", "acc_done", "sum_ready", "rden_done",
            "copied_out", "back_ready", "res_added", "stats_done", "mv_done", "veps_done", "rstd_done", "res_done")}
        adj_in = [sem(f"adj_in{i}") for i in range(AR)]
        qa_in = [sem(f"qa_in{h}") for h in range(HEADS)]
        kb_in = [sem(f"kb_in{h}") for h in range(HEADS)]

        block = ctx.enter_context(nc.Block())

        @block.sync
        def _(sp):
            def load_adj(b, n):
                wait(sp, s["w_done"], 8 * b + n - 1)
                sp.dma_start(adj_ring[:, n % AR, :], adj_v[n]).then_inc(adj_in[n % AR], 16)

            def load_x(b):
                wait(sp, s["xt_ready"], 2 * b)
                wait(sp, s["x_split"], b)
                wait(sp, s["csum_done"], b)
                sp.dma_start(x32[:, :, :], x_v[b]).then_inc(s["x_in"], 16)

            def copy_kb(b, h):
                wait(sp, s["kh_done"], 4 * b + h + 1)
                sp.dma_start(kb[h][own(h), :].bitcast(F32), ka[h][own(h), :].bitcast(F32)).then_inc(kb_in[h], 16)

            def copy_qa(b, h):
                wait(sp, s["qh_done"], 4 * b + h + 1)
                sp.dma_start(qa[h][other(h), :].bitcast(F32), qa[h][own(h), :].bitcast(F32)).then_inc(qa_in[h], 16)

            def store_row(b, h):
                wait(sp, s["row_done"], 4 * b + h + 1)
                r = other(h).start
                sp.dma_start(qb[h][r:r + 1, :].rearrange("o (t p) -> o t p", p=P).bitcast(F32),
                             row[:, :].bitcast(F32)).then_inc(s["row_in"], 16)

            def store_x1(b):
                wait(sp, s["res_done"], b + 1)
                sp.dma_start(x1_v[b], res[:, :, :]).then_inc(s["x1_out"], 16)

            def body(b, last):
                if not last:
                    load_x(b + 1)
                for n in range(3, T):
                    load_adj(b, n)
                copy_qa(b, 0)
                copy_qa(b, 1)
                copy_kb(b, 2)
                copy_kb(b, 3)
                copy_qa(b, 2)
                copy_qa(b, 3)
                store_row(b, 0)
                if not isinstance(b, int) or b > 0:
                    store_x1(b - 1)
                wait(sp, s["x1_out"], 16 * b)
                sp.dma_start(res[:, :, :], x_v[b]).then_inc(s["res_in"], 16)
                if not last:
                    load_adj(b + 1, 0)
                    load_adj(b + 1, 1)
                for h in range(1, HEADS):
                    store_row(b, h)
                if not last:
                    copy_kb(b + 1, 0)
                    copy_kb(b + 1, 1)
                    load_adj(b + 1, 2)

            load_x(0)
            sp.dma_start(scr[:, 0, :].rearrange("p (c n) -> p c n", c=CT), kvw_v).then_inc(s["kvw_in"], 16)
            load_adj(0, 0)
            load_adj(0, 1)
            sp.dma_start(neg_para[:, :, :], para_v).then_inc(s["para_in"], 16)
            sp.wait_ge(s["kq_set"], 3 * HEADS)
            copy_kb(0, 0)
            copy_kb(0, 1)
            load_adj(0, 2)
            over_batches(sp, B, body)
            store_x1(B - 1)
            wait(sp, s["x1_out"], 16 * B)

        @block.gpsimd
        def _(pool):
            pool.memset(ident[:, :], 0.0).then_inc(s["ident_set"], 1)
            pool.wait_ge(s["ident_set"], 1)
            pool.affine_select(out=ident[:, :], in_=ident[:, :], compare_op=ALU.not_equal, fill=1.0, base=0,
                               pattern=[[-1, P]], channel_multiplier=1).then_inc(s["ident_set"], 1)
            pool.memset(neg_half[:, :], -0.5).then_inc(s["ident_set"], 1)
            pool.wait_ge(s["ident_set"], 3)
            for k in range(2 * HEADS):
                if k:
                    pool.wait_ge(s["kq_set"], k)
                operand = (kb, qb)[k % 2][k // 2]
                pool.memset(operand[other(k // 2), :].bitcast(F32), 0.0).then_inc(s["kq_set"], 1)
            for h in range(HEADS):
                pool.wait_ge(s["kq_set"], 2 * HEADS + h)
                r = other(h).start
                pool.memset(kb[h][r:r + 1, :].bitcast(F32), 1.0).then_inc(s["kq_set"], 1)
            pool.wait_ge(s["kq_set"], 3 * HEADS)

            def rsqrt(b):
                wait(pool, s["veps_done"], b + 1)
                wait(pool, s["res_done"], b)
                pool.tensor_tensor(rstd[:, :], veps[:, :], neg_half[:, :], ALU.pow).then_inc(s["rstd_done"], 1)
                wait(pool, s["rstd_done"], 2 * b + 1)
                pool.tensor_tensor(shift[:, :], neg_mean[:, :], rstd[:, :], ALU.mult).then_inc(s["rstd_done"], 1)

            def body(b, last):
                if not isinstance(b, int) or b > 0:
                    rsqrt(b - 1)
                for h in range(HEADS):
                    for k in range(1, POOL_ADDS + 1):
                        done = POOL_ADDS * (4 * b + h) + k - 1
                        if k == 1:
                            wait(pool, s["sum_ready"], 4 * b + h)
                        else:
                            wait(pool, s["pool_added"], done)
                        wait(pool, s["exp_done"], 32 * b + 8 * h + k + 1)
                        pool.tensor_tensor(psum[:, :], probs[:, 0, :] if k == 1 else psum[:, :],
                                           probs[:, k % PR, :], ALU.add).then_inc(s["pool_added"], 1)

            over_batches(pool, B, body)
            rsqrt(B - 1)

        @block.scalar
        def _(act):
            def xt_high(b, half):
                wait(act, s["xt_ready"], 2 * b + half + 1)
                nc.scalar.activation(xT_hi[:, :, half * BANK:(half + 1) * BANK], mx_ps[:, :, :], ACT.Copy)\
                    .then_inc(s["xth_done"], 1)

            def mean_rows(b):
                wait(act, s["cb_ready"], b + 1)
                nc.scalar.activation(cb[:, :], mx_ps[:, :, :].rearrange("p a n -> p (a n)"), ACT.Copy)\
                    .then_inc(s["cb_done"], 1)

            def distance(b, n):
                if n == 0:
                    wait(act, s["cb_done"], b + 1)
                    wait(act, s["ccol_done"], b + 1)
                    wait(act, s["ql_done"], 4 * b)
                else:
                    wait(act, s["wlo_done"], 8 * b + n - 2)
                nc.scalar.activation(scr[:, n % DR, :], cb[:, :], ACT.Abs, bias=ccol[:, n:n + 1])\
                    .then_inc(s["abs_done"], 1)

            def tanh_half(b, n):
                wait(act, s["abs_done"], 8 * b + n + 1)
                d = scr[:, n % DR, :]
                nc.scalar.activation(d, d, ACT.Tanh, scale=0.5).then_inc(s["tanh_done"], 1)

            def w_high(b, n):
                wait(act, s["w_done"], 8 * b + n + 1)
                wait(act, s["g_step"], 8 * b if n < WR else 8 * b + n - WR + 1)
                nc.scalar.activation(w_hi[:, n % WR, :], scr[:, n % DR, :], ACT.Copy).then_inc(s["whi_done"], 1)

            def k_high(b, h):
                wait(act, s["k_ready"], 2 * b + h // 2 + 1)
                src = (mx_ps, pv_ps)[h // 2]
                nc.scalar.activation(ka[h][own(h), :], src[own(h), :, :].rearrange("p a n -> p (a n)"), ACT.Copy)\
                    .then_inc(s["kh_done"], 1)

            def q_high(b, h):
                wait(act, s["qt_done"], 2 * b + h // 2 + 1)
                nc.scalar.activation(qa[h][own(h), :], scr[own(h), h // 2, :], ACT.Relu).then_inc(s["qh_done"], 1)

            def v_copy(b, j):
                wait(act, s["v_ready"], 2 * b + j + 1)
                nc.scalar.activation(v[:, 4 * j:4 * j + 4, :], mx_ps[:, :, :].rearrange("p a (m c) -> p (a m) c", m=2),
                                     ACT.Copy).then_inc(s["v_evac"], 1)

            def exponential(b, h, i):
                t = 8 * h + i
                wait(act, s["st_ready"], 32 * b + t + 1)
                wait(act, s["pv_done"], 32 * b + t + 1 - (2 if i < 2 else 5 if i == 2 else PR))
                if i == 1:
                    wait(act, s["acc_done"], 4 * b + h)
                elif i != 2:
                    wait(act, s["pool_added"], POOL_ADDS * (4 * b + h) + (max(1, i - PR) if i else 0))
                nc.scalar.activation(probs[:, i % PR, :], sc_ps[:, t % 2, :], ACT.Exp, scale=SCALE)\
                    .then_inc(s["exp_done"], 1)

            def head_copy(b, h):
                wait(act, s["pv_done"], 32 * b + 8 * h + 8)
                wait(act, s["back_ready"], 4 * b + h - 1)
                nc.scalar.activation(heads_t[:, h % 2, :], pv_ps[:, h % 2, :], ACT.Copy).then_inc(s["copied_out"], 1)

            def normalise(b):
                wait(act, s["rstd_done"], 2 * b + 2)
                for n in range(T):
                    last = nc.scalar.activation(res[:, n, :], res[:, n, :], ACT.Identity, bias=shift[:, n:n + 1],
                                                scale=rstd[:, n:n + 1])
                last.then_inc(s["res_done"], 1)

            def x_high(b):
                wait(act, s["x_in"], 16 * (b + 1))
                wait(act, s["g_step"], 8 * b)
                for half in range(2):
                    tiles = slice(half * T // 2, (half + 1) * T // 2)
                    nc.scalar.activation(x_hi[:, tiles, :], x32[:, tiles, :], ACT.Copy).then_inc(s["xhi_done"], 1)

            def prepare(b, h, i):
                if (h, i) == (0, 7):
                    xt_high(b, 0)
                if (h, i) == (1, 3):
                    x_high(b)
                if (h, i) == (1, 7):
                    xt_high(b, 1)
                if (h, i) == (2, 7):
                    mean_rows(b)
                if (h, i) == (3, 0):
                    distance(b, 0)
                    tanh_half(b, 0)
                if (h, i) == (3, 1):
                    distance(b, 1)
                    tanh_half(b, 1)
                if (h, i) == (3, 2):
                    k_high(b, 0)
                if (h, i) == (3, 3):
                    k_high(b, 1)
                if (h, i) == (3, 4):
                    distance(b, 2)
                if (h, i) == (3, 5):
                    w_high(b, 0)
                if (h, i) == (3, 6):
                    tanh_half(b, 2)
                if (h, i) == (3, 7):
                    w_high(b, 1)
                    w_high(b, 2)

            def body(b, last):
                before = not isinstance(b, int) or b > 0
                if before:
                    head_copy(b - 1, HEADS - 1)
                for n in range(3, T + 1):
                    if n < T:
                        distance(b, n)
                        tanh_half(b, n)
                    if n > 3:
                        w_high(b, n - 1)
                q_high(b, 0)
                q_high(b, 1)
                v_copy(b, 0)
                k_high(b, 2)
                k_high(b, 3)
                q_high(b, 2)
                q_high(b, 3)
                if before:
                    normalise(b - 1)
                v_copy(b, 1)
                for h in range(HEADS):
                    for i in range(T):
                        if h and i == 1:
                            head_copy(b, h - 1)
                        exponential(b, h, i)
                        if not last:
                            prepare(b + 1, h, i)

            act.wait_ge(s["consts_set"], 5)
            for h in range(HEADS):
                for i in range(T):
                    prepare(0, h, i)
            over_batches(act, B, body)
            head_copy(B - 1, HEADS - 1)
            normalise(B - 1)

        @block.vector
        def _(dve):
            dve.memset(cb[:, 0:P], 1.0 / C).then_inc(s["consts_set"], 1)
            dve.memset(ones[:, :], 1.0).then_inc(s["consts_set"], 1)
            dve.wait_ge(s["consts_set"], 2)
            nc.vector.tensor_copy(mean_w[:, :], cb[:, 0:P]).then_inc(s["consts_set"], 1)
            kvw32 = scr[:, 0, :].rearrange("p (c n) -> p c n", c=CT)
            dve.wait_ge(s["kvw_in"], 16)
            nc.vector.tensor_copy(kvw_hi[:, :, :], kvw32).then_inc(s["consts_set"], 1)
            dve.wait_ge(s["consts_set"], 4)
            nc.vector.tensor_tensor(kvw_lo[:, :, :], kvw32, kvw_hi[:, :, :].bitcast(F32), ALU.subtract)\
                .then_inc(s["consts_set"], 1)

            def split_x(b):
                wait(dve, s["xhi_done"], 2 * b + 2)
                nc.vector.tensor_tensor(x_lo[:, :, :], x32[:, :, :], x_hi[:, :, :].bitcast(F32), ALU.subtract)\
                    .then_inc(s["x_split"], 1)

            def sum_channels(b):
                wait(dve, s["x_in"], 16 * (b + 1))
                nc.vector.tensor_reduce(csum[:, :], x32[:, :, :], AX.X, ALU.add).then_inc(s["csum_done"], 1)

            def mean_columns(b):
                wait(dve, s["tanh_done"], 8 * b)
                wait(dve, s["csum_done"], b + 1)
                nc.vector.tensor_scalar(ccol[:, :], csum[:, :], -1.0 / C, None, ALU.mult).then_inc(s["ccol_done"], 1)

            def xt_low(b, half):
                wait(dve, s["xth_done"], 2 * b + half + 1)
                cols = slice(half * BANK, (half + 1) * BANK)
                nc.vector.tensor_tensor(xT_lo[:, :, cols], mx_ps[:, :, :], xT_hi[:, :, cols].bitcast(F32),
                                        ALU.subtract).then_inc(s["xtl_done"], 1)

            def weigh(b, n):
                wait(dve, s["tanh_done"], 8 * b + n + 1)
                wait(dve, adj_in[n % AR], 16 * (4 * b + n // AR + 1))
                d = scr[:, n % DR, :]
                nc.vector.scalar_tensor_tensor(d, d, -1.0, adj_ring[:, n % AR, :], ALU.add, ALU.mult)\
                    .then_inc(s["w_done"], 1)

            def w_low(b, n):
                wait(dve, s["whi_done"], 8 * b + n + 1)
                nc.vector.tensor_tensor(w_lo[:, n % WR, :], scr[:, n % DR, :], w_hi[:, n % WR, :].bitcast(F32),
                                        ALU.subtract).then_inc(s["wlo_done"], 1)

            def k_low(b, h):
                wait(dve, s["kh_done"], 4 * b + h + 1)
                src = (mx_ps, pv_ps)[h // 2]
                nc.vector.tensor_tensor(ka[h][other(h), :], src[own(h), :, :].rearrange("p a n -> p (a n)"),
                                        ka[h][own(h), :].bitcast(F32), ALU.subtract).then_inc(s["kl_done"], 1)

            def q_times_para(b, c):
                if c == 0:
                    wait(dve, s["g_first"], b + 1)
                else:
                    wait(dve, s["g_step"], 8 * b + 8)
                nc.vector.tensor_tensor(scr[:, c, :], sc_ps[:, c, :], neg_para[:, c, :], ALU.mult)\
                    .then_inc(s["qt_done"], 1)

            def q_low(b, h):
                wait(dve, s["qh_done"], 4 * b + h + 1)
                nc.vector.scalar_tensor_tensor(qb[h][own(h), :], scr[own(h), h // 2, :], 0.0,
                                               qa[h][own(h), :].bitcast(F32), ALU.max, ALU.subtract)\
                    .then_inc(s["ql_done"], 1)

            def maxima(b, h, tiles):
                for n in tiles:
                    count = 16 * (4 * b + h) + 2 * n
                    if h == 0:
                        wait(dve, s["mx_ready"], count + 2)
                        nc.vector.tensor_reduce(mxs[:, n:n + 1], sc_ps[:, n % 2, :], AX.X, ALU.max)\
                            .then_inc(s["max_done"], 2)
                        continue
                    for nh in range(NH):
                        wait(dve, s["mx_ready"], count + nh + 1)
                        nc.vector.tensor_reduce(mx2[:, nh, n:n + 1], mx_ps[:, nh, :], AX.X, ALU.max)\
                            .then_inc(s["max_done"], 1)
                if h and T - 1 in tiles:
                    wait(dve, s["max_done"], 16 * (4 * b + h) + 16)
                    nc.vector.tensor_tensor(mxs[:, :], mx2[:, 0, :], mx2[:, 1, :], ALU.max).then_inc(s["merged"], 1)

            def maxima_row(b, h):
                wait(dve, s["rowT_ready"], 4 * b + h + 1)
                wait(dve, s["row_in"], 16 * (4 * b + h))
                src = (mx_ps if h else sc_ps)[0:T, 0, 0:P]
                nc.vector.tensor_scalar(row[:, :], src, -1.0, None, ALU.mult).then_inc(s["row_done"], 1)

            def add_last(b, h):
                wait(dve, s["exp_done"], 32 * b + 8 * h + 8)
                wait(dve, s["pool_added"], POOL_ADDS * (4 * b + h + 1))
                nc.vector.tensor_tensor(psum[:, :], psum[:, :], probs[:, (T - 1) % PR, :], ALU.add)\
                    .then_inc(s["acc_done"], 1)

            def invert_sums(b, h):
                wait(dve, s["sum_ready"], 4 * b + h + 1)
                nc.vector.reciprocal(rden[:, h % 2, :], pv_ps[:, h % 2, 0:T]).then_inc(s["rden_done"], 1)

            def add_head(b, h):
                wait(dve, s["back_ready"], 4 * b + h + 1)
                wait(dve, s["rden_done"], 4 * b + h + 1)
                if h == 0:
                    wait(dve, s["res_in"], 16 * (b + 1))
                for n in range(T):
                    out = res[:, n, h * HD:(h + 1) * HD]
                    col = (n % 4) * P + (n // 4) * HD
                    last = nc.vector.scalar_tensor_tensor(out, pv_ps[:, h % 2, col:col + HD],
                                                          rden[:, h % 2, n:n + 1], out, ALU.mult, ALU.add)
                last.then_inc(s["res_added"], 1)

            def row_stats(b):
                wait(dve, s["res_added"], 4 * b + 4)
                for n in range(T):
                    nc.vector.bn_stats(stats[:, n, :], res[:, n, :]).then_inc(s["stats_done"], 1)

            def moments(b):
                wait(dve, s["stats_done"], T * (b + 1))
                row_moments(nc, dve, stats, part, neg_mean[:, :], veps[:, :], C, s["mv_done"], s["veps_done"], 6 * b,
                            sign=-1.0)

            def body(b, last):
                before = not isinstance(b, int) or b > 0
                if before:
                    add_last(b - 1, HEADS - 1)
                weigh(b, 3)
                weigh(b, 4)
                w_low(b, 3)
                if before:
                    invert_sums(b - 1, HEADS - 1)
                weigh(b, 5)
                w_low(b, 4)
                if before:
                    add_head(b - 1, HEADS - 1)
                weigh(b, 6)
                w_low(b, 5)
                weigh(b, 7)
                w_low(b, 6)
                if before:
                    row_stats(b - 1)
                w_low(b, 7)
                if before:
                    moments(b - 1)
                q_times_para(b, 0)
                q_times_para(b, 1)
                maxima(b, 0, range(T))
                maxima_row(b, 0)
                q_low(b, 0)
                k_low(b, 2)
                k_low(b, 3)
                maxima(b, 1, range(T))
                maxima_row(b, 1)
                q_low(b, 1)
                if not last:
                    xt_low(b + 1, 0)
                for h in (1, 2):
                    add_last(b, h - 1)
                    maxima(b, h + 1, range(0, 3))
                    invert_sums(b, h - 1)
                    maxima(b, h + 1, range(3, 6))
                    add_head(b, h - 1)
                    maxima(b, h + 1, range(6, T))
                    maxima_row(b, h + 1)
                    if h == 1:
                        q_low(b, 2)
                        q_low(b, 3)
                        if not last:
                            xt_low(b + 1, 1)
                    if h == 2 and not last:
                        sum_channels(b + 1)
                        mean_columns(b + 1)
                add_last(b, 2)
                if not last:
                    weigh(b + 1, 0)
                invert_sums(b, 2)
                if not last:
                    weigh(b + 1, 1)
                add_head(b, 2)
                if not last:
                    k_low(b + 1, 0)
                    k_low(b + 1, 1)
                    split_x(b + 1)
                    w_low(b + 1, 0)
                    weigh(b + 1, 2)
                    w_low(b + 1, 1)
                    w_low(b + 1, 2)

            xt_low(0, 0)
            xt_low(0, 1)
            sum_channels(0)
            mean_columns(0)
            for n in range(2):
                weigh(0, n)
            k_low(0, 0)
            k_low(0, 1)
            split_x(0)
            w_low(0, 0)
            weigh(0, 2)
            w_low(0, 1)
            w_low(0, 2)
            dve.wait_ge(s["para_in"], 16)
            nc.vector.tensor_scalar(neg_para[:, :, :], neg_para[:, :, :], -1.0, None, ALU.mult)\
                .then_inc(s["consts_set"], 1)
            dve.wait_ge(s["consts_set"], 6)
            over_batches(dve, B, body)
            add_last(B - 1, HEADS - 1)
            invert_sums(B - 1, HEADS - 1)
            add_head(B - 1, HEADS - 1)
            row_stats(B - 1)
            moments(B - 1)

        @block.tensor
        def _(pe):
            def product(out, terms):
                for k, (lhsT, rhs) in enumerate(terms):
                    ins = nc.tensor.matmul(out, lhsT, rhs, start=k == 0, stop=k == len(terms) - 1)
                return ins

            def split_terms(pairs):
                out = []
                for (a_hi, a_lo), (b_hi, b_lo) in pairs:
                    out += [(a_hi, b_hi), (a_lo, b_hi), (a_hi, b_lo)]
                return out

            def transpose_x(b, half):
                wait(pe, s["x_in"], 16 * (b + 1))
                wait(pe, s["xtl_done"], 2 * b + half)
                wait(pe, s["row_done"], 4 * b - 2 + half)
                for c in range(CT):
                    for q in range(4):
                        ins = nc.tensor.transpose(mx_ps[:, c, q * P:(q + 1) * P],
                                                  x32[:, 4 * half + q, c * P:(c + 1) * P], ident[:, :])
                ins.then_inc(s["xt_ready"], 1)

            def broadcast_means(b):
                wait(pe, s["xtl_done"], 2 * b + 2)
                wait(pe, s["row_done"], 4 * b)
                for nh in range(NH):
                    cols = slice(nh * BANK, (nh + 1) * BANK)
                    ins = product(mx_ps[:, nh, :], [(mean_w[:, :], t[:, c, cols]) for c in range(CT)
                                                    for t in (xT_hi, xT_lo)])
                ins.then_inc(s["cb_ready"], 1)

            def k_product(b, c, halves=range(NH)):
                if c == 0:
                    wait(pe, s["cb_done"], b + 1)
                else:
                    wait(pe, s["res_added"], 4 * b)
                out = (mx_ps, pv_ps)[c]
                ws = slice(c * P, (c + 1) * P)
                for nh in halves:
                    cols = slice(nh * BANK, (nh + 1) * BANK)
                    ins = product(out[:, nh, :], split_terms(
                        [((kvw_hi[:, k, ws], kvw_lo[:, k, ws]), (xT_hi[:, k, cols], xT_lo[:, k, cols]))
                         for k in range(CT)]))
                if nh == NH - 1:
                    ins.then_inc(s["k_ready"], 1)

            def v_product(b, j, tiles=range(4)):
                if j == 0:
                    wait(pe, s["kl_done"], 4 * b + 2)
                else:
                    wait(pe, s["v_evac"], 2 * b + 1)
                for m in tiles:
                    rows = slice((4 * j + m) * P, (4 * j + m + 1) * P)
                    ins = product(mx_ps[:, m // 2, (m % 2) * C:(m % 2 + 1) * C], split_terms(
                        [((xT_hi[:, k, rows], xT_lo[:, k, rows]), (kvw_hi[:, k, C:2 * C], kvw_lo[:, k, C:2 * C]))
                         for k in range(CT)]))
                if m == 3:
                    ins.then_inc(s["v_ready"], 1)

            def g_product(b):
                before = not isinstance(b, int) or b > 0
                wait(pe, s["exp_done"], 32 * b)
                wait(pe, s["x_split"], b + 1)
                for n in range(T):
                    wait(pe, s["wlo_done"], 8 * b + n + 1)
                    for c in range(CT):
                        ch = slice(c * P, (c + 1) * P)
                        for nh in range(NH):
                            cols = slice(nh * BANK, (nh + 1) * BANK)
                            terms = split_terms([((x_hi[:, n, ch], x_lo[:, n, ch]),
                                                  (w_hi[:, n % WR, cols], w_lo[:, n % WR, cols]))])
                            for k, (lhsT, rhs) in enumerate(terms):
                                ins = nc.tensor.matmul(sc_ps[:, c, cols], lhsT, rhs,
                                                       start=n == 0 and k == 0, stop=n == T - 1 and k == 2)
                        if n == T - 1 and c == 0:
                            ins.then_inc(s["g_first"], 1)
                        if before and n == 1:
                            sum_up(b - 1, HEADS - 1, range(c * T // 2, (c + 1) * T // 2))
                    ins.then_inc(s["g_step"], 1)
                    if before and n == 2:
                        transpose_back(b - 1, HEADS - 1)

            def max_scores(b, h, n, last=True):
                if h == 0:
                    if n == 0:
                        wait(pe, s["qh_done"], 4 * b + 1)
                        wait(pe, s["kh_done"], 4 * b + 1)
                    if n < 2:
                        wait(pe, s["qt_done"], 2 * b + n + 1)
                    else:
                        wait(pe, s["max_done"], 64 * b + 2 * (n - 1))
                elif n == 0:
                    wait(pe, s["row_done"], 4 * b + h)
                    wait(pe, s["qh_done"], 4 * b + h + 1)
                    if h == 1:
                        wait(pe, s["v_evac"], 2 * b + 2)
                    elif not last:
                        wait(pe, s["xtl_done"], 2 * b + h + 1)
                for nh in range(NH):
                    if h and n:
                        wait(pe, s["max_done"], 16 * (4 * b + h) + 2 * (n - 1) + nh + 1)
                    out = mx_ps[:, nh, :] if h else sc_ps[:, n % 2, nh * BANK:(nh + 1) * BANK]
                    nc.tensor.matmul(out, qa[h][own(h), n * P:(n + 1) * P], ka[h][own(h), nh * BANK:(nh + 1) * BANK],
                                     start=True, stop=True).then_inc(s["mx_ready"], 1)

            def transpose_maxima(b, h):
                if h == 0:
                    wait(pe, s["max_done"], 64 * b + 16)
                else:
                    wait(pe, s["merged"], 3 * b + h)
                out = (mx_ps if h else sc_ps)[0:T, 0, 0:P]
                nc.tensor.transpose(out, mxs[:, :], ident[:, :]).then_inc(s["rowT_ready"], 1)

            def scores(b, h, i, parts=(0, 1)):
                t = 8 * h + i
                if 0 in parts:
                    wait(pe, s["exp_done"], 32 * b + t - 1)
                    if t < 2:
                        wait(pe, s["qt_done"], 2 * b + t + 1)
                        wait(pe, s["row_done"], 4 * b + 1)
                    if i == 0:
                        wait(pe, qa_in[h], 16 * (b + 1))
                        wait(pe, s["kl_done"], 4 * b + h + 1)
                if 1 in parts and i == 0:
                    wait(pe, s["row_in"], 16 * (4 * b + h + 1))
                    wait(pe, kb_in[h], 16 * (b + 1))
                    wait(pe, s["ql_done"], 4 * b + h + 1)
                keys = slice(i * P, (i + 1) * P)
                for nh in range(NH):
                    cols = slice(nh * BANK, (nh + 1) * BANK)
                    for part in parts:
                        k, q = (ka, qa) if part == 0 else (kb, qb)
                        ins = nc.tensor.matmul(sc_ps[:, t % 2, cols], k[h][:, keys], q[h][:, cols],
                                               start=part == 0, stop=part == 1)
                if 1 in parts:
                    ins.then_inc(s["st_ready"], 1)

            def values(b, h, i):
                t = 8 * h + i
                wait(pe, s["exp_done"], 32 * b + t + 1)
                if i == 0 and h < 2:
                    wait(pe, s["v_evac"], 2 * b + 2)
                    wait(pe, s["kl_done"], 4 * b + 4)
                elif i == 0:
                    wait(pe, s["res_added"], 4 * b + h - 1)
                for nh in range(NH):
                    ins = nc.tensor.matmul(pv_ps[nh * HD:(nh + 1) * HD, h % 2, :], v[:, i, h * HD:(h + 1) * HD],
                                           probs[:, i % PR, nh * BANK:(nh + 1) * BANK],
                                           start=i == 0, stop=i == T - 1)
                ins.then_inc(s["pv_done"], 1)

            def sum_up(b, h, rows=range(T)):
                wait(pe, s["acc_done"], 4 * b + h + 1)
                wait(pe, s["copied_out"], 4 * b + h + 1)
                for n in rows:
                    ins = nc.tensor.matmul(pv_ps[:, h % 2, n:n + 1], psum[:, n * P:(n + 1) * P], ones[:, :],
                                           start=True, stop=True)
                if T - 1 in rows:
                    ins.then_inc(s["sum_ready"], 1)

            def transpose_back(b, h):
                wait(pe, s["rden_done"], 4 * b + h + 1)
                for q in range(4):
                    ins = nc.tensor.transpose(pv_ps[:, h % 2, q * P:(q + 1) * P],
                                              heads_t[:, h % 2, q * P:(q + 1) * P], ident[:, :])
                ins.then_inc(s["back_ready"], 1)

            def prepare(b, h, i):
                if (h, i) == (0, 7):
                    transpose_x(b, 0)
                if (h, i) == (1, 7):
                    transpose_x(b, 1)
                if (h, i) == (2, 7):
                    broadcast_means(b)
                if (h, i) == (3, 1):
                    k_product(b, 0)

            def body(b, last):
                g_product(b)
                v_product(b, 0, [0, 1])
                max_scores(b, 0, 0)
                max_scores(b, 0, 1)
                v_product(b, 0, [2, 3])
                max_scores(b, 0, 2)
                k_product(b, 1, [0])
                max_scores(b, 0, 3)
                k_product(b, 1, [1])
                max_scores(b, 0, 4)
                max_scores(b, 0, 5)
                v_product(b, 1, [0, 1])
                max_scores(b, 0, 6)
                max_scores(b, 0, 7)
                transpose_maxima(b, 0)
                v_product(b, 1, [2, 3])
                scores(b, 0, 0, [0])
                scores(b, 0, 1, [0])
                for h in range(HEADS):
                    n = 0
                    more = h + 1 < HEADS
                    for i in range(T):
                        scores(b, h, i, [1] if h == 0 and i < 2 else (0, 1))
                        if more and MAX_BEFORE[i]:
                            max_scores(b, h + 1, n, last)
                            n += 1
                        if more and i == ROW_STEP:
                            transpose_maxima(b, h + 1)
                        if not last:
                            prepare(b + 1, h, i)
                        if h and i == SUM_STEP:
                            sum_up(b, h - 1, range(0, T // 2))
                        if h + i:
                            values(b, h if i else h - 1, i - 1 if i else T - 1)
                        if more and MAX_AFTER[i]:
                            max_scores(b, h + 1, n, last)
                            n += 1
                        if h and i == SUM_STEP:
                            sum_up(b, h - 1, range(T // 2, T))
                        if h and i == BACK_STEP:
                            transpose_back(b, h - 1)
                values(b, HEADS - 1, T - 1)

            pe.wait_ge(s["ident_set"], 3)
            pe.wait_ge(s["consts_set"], 5)
            for h in range(HEADS):
                for i in range(T):
                    prepare(0, h, i)
            pe.wait_ge(s["kq_set"], 3 * HEADS)
            over_batches(pe, B, body)
            sum_up(B - 1, HEADS - 1)
            transpose_back(B - 1, HEADS - 1)


def aggregate_layer(nc, x1, adj, w1, b1, g1, be1, scale1, shift1, pre1):
    B, N, C = x1.shape
    H = w1.shape[0]
    T, CT, HT, NH = N // P, C // P, H // P, N // BANK

    x1_v = x1.rearrange("b (t p) c -> b p t c", p=P)
    adj_v = adj.rearrange("(t p) m -> p t m", p=P)
    w1_v = w1.rearrange("(t p) c -> p t c", p=P)
    pre1_v = pre1.rearrange("b (t p) n -> b p t n", p=P)

    with ExitStack() as ctx:
        def sb(name, shape, dt=F32):
            return ctx.enter_context(nc.sbuf_tensor(name, shape, dt))

        def pb(name, shape):
            return ctx.enter_context(nc.psum_tensor(name, shape, F32))

        def sem(name):
            return ctx.enter_context(nc.semaphore(name))

        ident = sb("ident_b", [P, P])
        ones = sb("ones", [P, P])
        neg_half = sb("neg_half_b", [P, T])
        a_hi = sb("a_hi", [P, T, N], F32R)
        a_lo = sb("a_lo", [P, T, N], F32R)
        at32 = sb("at32", [P, T, N])
        junk = sb("junk", [P, N])
        pre = sb("pre", [P, 2, HT, N])
        adjs = pre[:, :, :, :].rearrange("p e t n -> p (e t) n")
        w1s = sb("w1s", [P, HT, C])
        w1_hi = sb("w1_hi", [P, CT, H], F32R)
        w1_lo = sb("w1_lo", [P, CT, H], F32R)
        x1s = sb("x1s", [P, 2, T, C])
        x1_hi = sb("x1_hi", [P, T, C], F32R)
        x1_lo = sb("x1_lo", [P, T, C], F32R)
        agg_hi = sb("agg_hi", [P, CT, N], F32R)
        agg_lo = sb("agg_lo", [P, CT, N], F32R)
        block_diag = sb("block_diag", [P, T, P])
        colparts = sb("colparts", [P, T, T])
        colsum = sb("colsum", [P, T])
        diag = sb("diag", [P, T])
        rowsum = sb("rowsum", [P, T])
        deg = sb("deg", [P, T])
        dinv = sb("dinv", [P, T])
        b1s = sb("b1s", [P, HT])
        g1s = sb("g1s", [P, HT])
        be1s = sb("be1s", [P, HT])
        stats = sb("stats1", [P, HT, B * NH, 6])
        mv = sb("mv1", [P, HT, 2])
        veps = sb("veps1", [P, HT])
        rstd = sb("rstd1", [P, HT])

        ag_ps = pb("ag_ps", [P, NH, CT, BANK])
        pre_ps = pb("pre_ps", [P, HT, BANK])

        s = {n: sem("b_" + n) for n in (
            "w1_in", "vec_in", "consts_set", "aug_done", "diag_done", "rowsum_done", "colsum_done", "deg_done",
            "atc_done", "colpart_done", "bc_ready", "at_scaled", "atl_odd", "diag_scaled",
            "dinv_done", "at_ready", "ath_done", "atl_even", "w1_ready", "w1h_done",
            "w1l_done", "x1h_done", "x1l_done", "ag_ready", "agh_done", "agl_done", "pre_ready", "pre_done",
            "stats_done", "mv_done", "veps_done", "rstd_done", "scale_done", "shift_done")}
        adj_in = [sem(f"b_adj_in{t}") for t in range(T)]
        x1_in = [sem(f"b_x1_in{e}") for e in range(2)]
        pre_out = [sem(f"b_pre_out{e}") for e in range(2)]

        block = ctx.enter_context(nc.Block())

        @block.sync
        def _(sp):
            for t in range(T):
                sp.dma_start(adjs[:, t, :], adj_v[:, t, :]).then_inc(adj_in[t], 16)
                if t == 0:
                    sp.dma_start(w1s[:, :, :], w1_v).then_inc(s["w1_in"], 16)
            def load(b, e):
                wait(sp, s["x1l_done"], b - 1)
                sp.dma_start(x1s[:, e, :, :], x1_v[b]).then_inc(x1_in[e], 16)

            def pair(g, last):
                for e in range(2):
                    for j in range(NH):
                        wait(sp, s["pre_done"], 8 * (2 * g + e) + 4 * j + 4)
                        cols = slice(j * BANK, (j + 1) * BANK)
                        sp.dma_start(pre1_v[2 * g + e][:, :, cols], pre[:, e, :, cols]).then_inc(pre_out[e], 16)
                    if not last:
                        load(2 * g + e + 2, e)

            load(0, 0)
            load(1, 1)
            for t, src in ((b1s, b1), (g1s, g1), (be1s, be1)):
                sp.dma_start(t[:, :], src.rearrange("(t p) -> p t", p=P), allow_slow_non_contiguous=True)\
                    .then_inc(s["vec_in"], 16)
            over_batches(sp, B // 2, pair)
            for e in range(2):
                wait(sp, pre_out[e], 16 * NH * (B // 2))

        @block.gpsimd
        def _(pool):
            pool.memset(ident[:, :], 0.0).then_inc(s["consts_set"], 1)
            pool.memset(ones[:, :], 1.0).then_inc(s["consts_set"], 1)
            pool.memset(neg_half[:, :], -0.5).then_inc(s["consts_set"], 1)
            pool.wait_ge(s["consts_set"], 3)
            pool.affine_select(out=ident[:, :], in_=ident[:, :], compare_op=ALU.not_equal, fill=1.0, base=0,
                               pattern=[[-1, P]], channel_multiplier=1).then_inc(s["consts_set"], 1)
            pool.wait_ge(s["consts_set"], 4)
            for t in range(T):
                pool.wait_ge(adj_in[t], 16)
                blk = adjs[:, t, t * P:(t + 1) * P]
                pool.tensor_tensor(blk, blk, ident[:, :], ALU.add).then_inc(s["aug_done"], 1)
                pool.wait_ge(s["aug_done"], t + 1)
                pool.tensor_tensor(block_diag[:, t, :], blk, ident[:, :], ALU.mult).then_inc(s["diag_done"], 1)
            pool.wait_ge(s["deg_done"], 1)
            pool.tensor_tensor(dinv[:, :], deg[:, :], neg_half[:, :], ALU.pow).then_inc(s["dinv_done"], 1)
            for m in range(1, T, 2):
                pool.wait_ge(s["ath_done"], m + 1)
                pool.tensor_tensor(a_lo[:, m, :], at32[:, m, :], a_hi[:, m, :].bitcast(F32), ALU.subtract)\
                    .then_inc(s["atl_odd"], 1)
            pool.wait_ge(s["veps_done"], 1)
            pool.tensor_tensor(rstd[:, :], veps[:, :], neg_half[:, 0:HT], ALU.pow).then_inc(s["rstd_done"], 1)

        @block.scalar
        def _(act):
            for t in range(T):
                act.wait_ge(s["aug_done"], t + 1)
                if t >= 1:
                    act.wait_ge(s["rowsum_done"], t)
                nc.scalar.activation(junk[:, :], adjs[:, t, :], ACT.Copy, accum_out=rowsum[:, t:t + 1])\
                    .then_inc(s["rowsum_done"], 1)
                act.wait_ge(s["at_ready"], t + 1)
                nc.scalar.activation(at32[:, :, t * P:(t + 1) * P],
                                     ag_ps[:, t % 2, :, :].rearrange("p c (m n) -> p (c m) n", n=P), ACT.Copy)\
                    .then_inc(s["atc_done"], 1)
                if t == 0:
                    for c in range(CT):
                        act.wait_ge(s["w1_ready"], c + 1)
                        nc.scalar.activation(w1_hi[:, c, :], pre_ps[:, c, :], ACT.Copy).then_inc(s["w1h_done"], 1)
            for m in range(T):
                act.wait_ge(s["at_scaled"], m + 1)
                nc.scalar.activation(a_hi[:, m, :], at32[:, m, :], ACT.Copy).then_inc(s["ath_done"], 1)
            act.wait_ge(s["vec_in"], 48)

            def pair(g, last):
                for e in range(2):
                    b = 2 * g + e
                    for j in range(NH):
                        wait(act, s["ag_ready"], 2 * b + j + 1)
                        nc.scalar.activation(agg_hi[:, :, j * BANK:(j + 1) * BANK], ag_ps[:, j, :, :], ACT.Copy)\
                            .then_inc(s["agh_done"], 1)
                    wait(act, pre_out[e], 16 * NH * g)
                    wait(act, s["stats_done"], 8 * b - 8)
                    for j in range(NH):
                        for t in range(HT):
                            wait(act, s["pre_ready"], 8 * b + 4 * j + t + 1)
                            nc.scalar.activation(pre[:, e, t, j * BANK:(j + 1) * BANK], pre_ps[:, t, :],
                                                 ACT.Identity, bias=b1s[:, t:t + 1]).then_inc(s["pre_done"], 1)

            over_batches(act, B // 2, pair)

        @block.vector
        def _(dve):
            def split(b, e, g):
                wait(dve, x1_in[e], 16 * (g + 1))
                wait(dve, s["ag_ready"], 2 * b)
                nc.vector.tensor_copy(x1_hi[:, :, :], x1s[:, e, :, :]).then_inc(s["x1h_done"], 1)
                wait(dve, s["x1h_done"], b + 1)
                nc.vector.tensor_tensor(x1_lo[:, :, :], x1s[:, e, :, :], x1_hi[:, :, :].bitcast(F32),
                                        ALU.subtract).then_inc(s["x1l_done"], 1)

            for t in range(T):
                dve.wait_ge(s["atc_done"], t + 1)
                nc.vector.tensor_reduce(colparts[:, t, :], at32[:, :, t * P:(t + 1) * P], AX.X, ALU.add)\
                    .then_inc(s["colpart_done"], 1)
                if t == 0:
                    for c in range(CT):
                        dve.wait_ge(s["w1h_done"], c + 1)
                        nc.vector.tensor_tensor(w1_lo[:, c, :], pre_ps[:, c, :], w1_hi[:, c, :].bitcast(F32),
                                                ALU.subtract).then_inc(s["w1l_done"], 1)
            dve.wait_ge(s["diag_done"], T)
            nc.vector.tensor_reduce(diag[:, :], block_diag[:, :, :], AX.X, ALU.add).then_inc(s["diag_done"], 1)
            dve.wait_ge(s["colpart_done"], T)
            nc.vector.tensor_reduce(colsum[:, :], colparts[:, :, :].rearrange("p t m -> p m t"), AX.X, ALU.add)\
                .then_inc(s["colsum_done"], 1)
            dve.wait_ge(s["rowsum_done"], T)
            dve.wait_ge(s["colsum_done"], 1)
            nc.vector.tensor_tensor(colsum[:, :], rowsum[:, :], colsum[:, :], ALU.add).then_inc(s["colsum_done"], 1)
            dve.wait_ge(s["colsum_done"], 2)
            dve.wait_ge(s["diag_done"], T + 1)
            nc.vector.tensor_tensor(deg[:, :], colsum[:, :], diag[:, :], ALU.subtract).then_inc(s["deg_done"], 1)
            dve.wait_ge(s["dinv_done"], 1)
            for t in range(T):
                nc.vector.tensor_scalar(block_diag[:, t, :], ident[:, :], dinv[:, t:t + 1], None, ALU.mult)\
                    .then_inc(s["diag_scaled"], 1)
            split(0, 0, 0)
            dve.wait_ge(s["bc_ready"], 1)

            def a_low(m):
                dve.wait_ge(s["ath_done"], m + 1)
                nc.vector.tensor_tensor(a_lo[:, m, :], at32[:, m, :], a_hi[:, m, :].bitcast(F32), ALU.subtract)\
                    .then_inc(s["atl_even"], 1)

            for m in range(T):
                nc.vector.scalar_tensor_tensor(at32[:, m, :], at32[:, m, :], dinv[:, m:m + 1],
                                               pre_ps[:, 2:4, :].rearrange("p c n -> p (c n)"), ALU.mult, ALU.mult)\
                    .then_inc(s["at_scaled"], 1)
                if m % 2 == 1:
                    a_low(m - 1)

            def pair(g, last):
                for e in range(2):
                    b = 2 * g + e
                    for j in range(NH):
                        wait(dve, s["agh_done"], 2 * b + j + 1)
                        cols = slice(j * BANK, (j + 1) * BANK)
                        nc.vector.tensor_tensor(agg_lo[:, :, cols], ag_ps[:, j, :, :],
                                                agg_hi[:, :, cols].bitcast(F32), ALU.subtract)\
                            .then_inc(s["agl_done"], 1)
                    if not (last and e == 1):
                        split(b + 1, 1 - e, g + e)
                    for j in range(NH):
                        for t in range(HT):
                            wait(dve, s["pre_done"], 8 * b + 4 * j + t + 1)
                            nc.vector.bn_stats(stats[:, t, NH * b + j, :], pre[:, e, t, j * BANK:(j + 1) * BANK])\
                                .then_inc(s["stats_done"], 1)

            over_batches(dve, B // 2, pair)
            wait(dve, s["stats_done"], 8 * B)
            for t in range(HT):
                nc.vector.bn_aggr(mv[:, t, :], stats[:, t, :, :]).then_inc(s["mv_done"], 1)
            dve.wait_ge(s["mv_done"], HT)
            nc.vector.tensor_scalar(veps[:, :].rearrange("p (t o) -> p t o", o=1), mv[:, :, 1:2], EPS, None, ALU.add)\
                .then_inc(s["veps_done"], 1)
            dve.wait_ge(s["rstd_done"], 1)
            nc.vector.tensor_tensor(scale1[:, :], g1s[:, :], rstd[:, :], ALU.mult).then_inc(s["scale_done"], 1)
            dve.wait_ge(s["scale_done"], 1)
            nc.vector.tensor_tensor(shift1[:, :], mv[:, :, 0], scale1[:, :], ALU.mult).then_inc(s["shift_done"], 1)
            dve.wait_ge(s["shift_done"], 1)
            nc.vector.tensor_tensor(shift1[:, :], be1s[:, :], shift1[:, :], ALU.subtract).then_inc(s["shift_done"], 1)

        @block.tensor
        def _(pe):
            pe.wait_ge(s["consts_set"], 4)
            for t in range(T):
                pe.wait_ge(s["aug_done"], t + 1)
                if t >= 2:
                    pe.wait_ge(s["atc_done"], t - 1)
                for m in range(T):
                    ins = nc.tensor.transpose(ag_ps[:, t % 2, m // 4, (m % 4) * P:(m % 4 + 1) * P],
                                              adjs[:, t, m * P:(m + 1) * P], ident[:, :])
                ins.then_inc(s["at_ready"], 1)
                if t == 0:
                    pe.wait_ge(s["w1_in"], 16)
                    for c in range(CT):
                        for k in range(HT):
                            ins = nc.tensor.transpose(pre_ps[:, c, k * P:(k + 1) * P],
                                                      w1s[:, k, c * P:(c + 1) * P], ident[:, :])
                        ins.then_inc(s["w1_ready"], 1)
            pe.wait_ge(s["diag_scaled"], T)
            for j in range(NH):
                ins = nc.tensor.matmul(pre_ps[:, 2 + j, :], ones[:, :],
                                       block_diag[:, 4 * j:4 * j + 4, :].rearrange("p t n -> p (t n)"),
                                       start=True, stop=True)
            ins.then_inc(s["bc_ready"], 1)
            pe.wait_ge(s["w1l_done"], CT)
            pe.wait_ge(s["atc_done"], T)

            def first_aggregate():
                for m in range(T):
                    pe.wait_ge(s["atl_odd" if m % 2 else "atl_even"], m // 2 + 1)
                    for j in range(NH):
                        cols = slice(j * BANK, (j + 1) * BANK)
                        for c in range(CT):
                            ch = slice(c * P, (c + 1) * P)
                            for k, (l, r) in enumerate([(x1_hi, a_hi), (x1_lo, a_hi), (x1_hi, a_lo)]):
                                ins = nc.tensor.matmul(ag_ps[:, j, c, :], l[:, m, ch], r[:, m, cols],
                                                       start=m == 0 and k == 0, stop=m == T - 1 and k == 2)
                        if m == T - 1:
                            ins.then_inc(s["ag_ready"], 1)

            def pair(g, last):
                for e in range(2):
                    b = 2 * g + e
                    wait(pe, s["x1l_done"], b + 1)
                    first = isinstance(b, int) and b == 0
                    if first:
                        first_aggregate()
                    for j in () if first else range(NH):
                        wait(pe, s["agl_done"], 2 * b + j - 1)
                        cols = slice(j * BANK, (j + 1) * BANK)
                        for c in range(CT):
                            ch = slice(c * P, (c + 1) * P)
                            for m in range(T):
                                terms = [(x1_hi, a_hi), (x1_lo, a_hi), (x1_hi, a_lo)]
                                for k, (l, r) in enumerate(terms):
                                    ins = nc.tensor.matmul(ag_ps[:, j, c, :], l[:, m, ch], r[:, m, cols],
                                                           start=m == 0 and k == 0, stop=m == T - 1 and k == 2)
                        ins.then_inc(s["ag_ready"], 1)
                    for j in range(NH):
                        wait(pe, s["agl_done"], 2 * b + j + 1)
                        cols = slice(j * BANK, (j + 1) * BANK)
                        for t in range(HT):
                            wait(pe, s["pre_done"], 8 * b + 4 * j + t - 3)
                            for c in range(CT):
                                hid = slice(t * P, (t + 1) * P)
                                terms = [(w1_hi, agg_hi), (w1_lo, agg_hi), (w1_hi, agg_lo)]
                                for k, (l, r) in enumerate(terms):
                                    ins = nc.tensor.matmul(pre_ps[:, t, :], l[:, c, hid], r[:, c, cols],
                                                           start=c == 0 and k == 0, stop=c == CT - 1 and k == 2)
                            ins.then_inc(s["pre_ready"], 1)

            over_batches(pe, B // 2, pair)


def output_layer(nc, pre1, w2, b2, g2, be2, scale1, shift1, scale2, shift2, pre2):
    B, H, N = pre1.shape
    O = w2.shape[0]
    HT, OT, NH = H // P, O // P, N // BANK

    pre1_v = pre1.rearrange("b (t p) n -> b p t n", p=P)
    w2_v = w2.rearrange("(t p) h -> p t h", p=P)

    with ExitStack() as ctx:
        def sb(name, shape, dt=F32):
            return ctx.enter_context(nc.sbuf_tensor(name, shape, dt))

        def sem(name):
            return ctx.enter_context(nc.semaphore(name))

        ident = sb("ident_c", [P, P])
        neg_half = sb("neg_half_c", [P, OT])
        hid = sb("hid", [P, 2, HT, N])
        hid_hi = sb("hid_hi", [P, HT, N], F32R)
        hid_lo = sb("hid_lo", [P, HT, N], F32R)
        w2s = pre2[:, :, B * NH - 1, :]
        w2_hi = sb("w2_hi", [P, HT, O], F32R)
        w2_lo = sb("w2_lo", [P, HT, O], F32R)
        b2s = sb("b2s", [P, OT])
        g2s = sb("g2s", [P, OT])
        be2s = sb("be2s", [P, OT])
        stats = sb("stats2", [P, OT, B * NH, 6])
        mv = sb("mv2", [P, OT, 2])
        veps = sb("veps2", [P, OT])
        rstd = sb("rstd2", [P, OT])
        out_ps = ctx.enter_context(nc.psum_tensor("out_ps", [P, NH, OT, BANK], F32))
        w2_ps = ctx.enter_context(nc.psum_tensor("w2_ps", [P, HT, O], F32))

        s = {n: sem("c_" + n) for n in (
            "w2_in", "vec_in", "consts_set", "w2_ready", "w2h_done", "w2l_done", "relu_done", "hh_done", "hl_done",
            "out_ready", "pre2_done", "stats_done", "mv_done", "veps_done", "rstd_done", "scale_done", "shift_done")}
        pre_in = [[sem(f"c_pre_in{e}{j}") for j in range(NH)] for e in range(2)]

        block = ctx.enter_context(nc.Block())

        @block.sync
        def _(sp):
            def load(b, e, j):
                wait(sp, s["hl_done"], 2 * b + j - 3)
                cols = slice(j * BANK, (j + 1) * BANK)
                sp.dma_start(hid[:, e, :, cols], pre1_v[b][:, :, cols]).then_inc(pre_in[e][j], 16)

            def pair(g, last):
                if not last:
                    for e in range(2):
                        for j in range(NH):
                            load(2 * g + e + 2, e, j)

            load(0, 0, 0)
            sp.dma_start(w2s, w2_v).then_inc(s["w2_in"], 16)
            load(0, 0, 1)
            for t, src in ((b2s, b2), (g2s, g2), (be2s, be2)):
                sp.dma_start(t[:, :], src.rearrange("(t p) -> p t", p=P), allow_slow_non_contiguous=True)\
                    .then_inc(s["vec_in"], 16)
            for j in range(NH):
                load(1, 1, j)
            over_batches(sp, B // 2, pair)

        @block.gpsimd
        def _(pool):
            pool.memset(ident[:, :], 0.0).then_inc(s["consts_set"], 1)
            pool.memset(neg_half[:, :], -0.5).then_inc(s["consts_set"], 1)
            pool.wait_ge(s["consts_set"], 2)
            pool.affine_select(out=ident[:, :], in_=ident[:, :], compare_op=ALU.not_equal, fill=1.0, base=0,
                               pattern=[[-1, P]], channel_multiplier=1).then_inc(s["consts_set"], 1)
            pool.wait_ge(s["veps_done"], 1)
            pool.tensor_tensor(rstd[:, :], veps[:, :], neg_half[:, :], ALU.pow).then_inc(s["rstd_done"], 1)

        @block.scalar
        def _(act):
            act.wait_ge(s["w2_ready"], 1)
            nc.scalar.activation(w2_hi[:, :, :], w2_ps[:, :, :], ACT.Copy).then_inc(s["w2h_done"], 1)
            act.wait_ge(s["vec_in"], 48)

            def relu(b, e, g, j):
                wait(act, pre_in[e][j], 16 * (g + 1))
                for t in range(HT):
                    part = hid[:, e, t, j * BANK:(j + 1) * BANK]
                    nc.scalar.activation(part, part, ACT.Relu, bias=shift1[:, t:t + 1], scale=scale1[:, t:t + 1])\
                        .then_inc(s["relu_done"], 1)

            def pair(g, last):
                for e in range(2):
                    b = 2 * g + e
                    for j in range(NH):
                        if not (last and e == 1):
                            relu(b + 1, 1 - e, g + e, j)
                        wait(act, s["out_ready"], 2 * b + j + 1)
                        for o in range(OT):
                            nc.scalar.activation(pre2[:, o, NH * b + j, :], out_ps[:, j, o, :], ACT.Identity,
                                                 bias=b2s[:, o:o + 1]).then_inc(s["pre2_done"], 1)

            for j in range(NH):
                relu(0, 0, 0, j)
            over_batches(act, B // 2, pair)

        @block.vector
        def _(dve):
            dve.wait_ge(s["w2h_done"], 1)
            nc.vector.tensor_tensor(w2_lo[:, :, :], w2_ps[:, :, :], w2_hi[:, :, :].bitcast(F32), ALU.subtract)\
                .then_inc(s["w2l_done"], 1)

            def split(b, e, j):
                cols = slice(j * BANK, (j + 1) * BANK)
                wait(dve, s["relu_done"], 8 * b + 4 * j + 4)
                wait(dve, s["out_ready"], 2 * b + j - 1)
                nc.vector.tensor_copy(hid_hi[:, :, cols], hid[:, e, :, cols]).then_inc(s["hh_done"], 1)
                wait(dve, s["hh_done"], 2 * b + j + 1)
                nc.vector.tensor_tensor(hid_lo[:, :, cols], hid[:, e, :, cols], hid_hi[:, :, cols].bitcast(F32),
                                        ALU.subtract).then_inc(s["hl_done"], 1)

            def pair(g, last):
                for e in range(2):
                    b = 2 * g + e
                    for j in range(NH):
                        if j + 1 < NH:
                            split(b, e, j + 1)
                        elif not (last and e == 1):
                            split(b + 1, 1 - e, 0)
                        if not isinstance(b, int) or b or j:
                            half_stats(NH * b + j - 1)

            def half_stats(k):
                for o in range(OT):
                    wait(dve, s["pre2_done"], 2 * k + o + 1)
                    nc.vector.bn_stats(stats[:, o, k, :], pre2[:, o, k, :]).then_inc(s["stats_done"], 1)

            split(0, 0, 0)
            over_batches(dve, B // 2, pair)
            half_stats(NH * B - 1)
            wait(dve, s["stats_done"], 4 * B)
            for o in range(OT):
                nc.vector.bn_aggr(mv[:, o, :], stats[:, o, :, :]).then_inc(s["mv_done"], 1)
            dve.wait_ge(s["mv_done"], OT)
            nc.vector.tensor_scalar(veps[:, :].rearrange("p (t o) -> p t o", o=1), mv[:, :, 1:2], EPS, None, ALU.add)\
                .then_inc(s["veps_done"], 1)
            dve.wait_ge(s["rstd_done"], 1)
            dve.wait_ge(s["vec_in"], 48)
            nc.vector.tensor_tensor(scale2[:, :], g2s[:, :], rstd[:, :], ALU.mult).then_inc(s["scale_done"], 1)
            dve.wait_ge(s["scale_done"], 1)
            nc.vector.tensor_tensor(shift2[:, :], mv[:, :, 0], scale2[:, :], ALU.mult).then_inc(s["shift_done"], 1)
            dve.wait_ge(s["shift_done"], 1)
            nc.vector.tensor_tensor(shift2[:, :], be2s[:, :], shift2[:, :], ALU.subtract).then_inc(s["shift_done"], 1)

        @block.tensor
        def _(pe):
            pe.wait_ge(s["consts_set"], 3)
            pe.wait_ge(s["w2_in"], 16)
            for t in range(HT):
                for o in range(OT):
                    ins = nc.tensor.transpose(w2_ps[:, t, o * P:(o + 1) * P], w2s[:, o, t * P:(t + 1) * P],
                                              ident[:, :])
            ins.then_inc(s["w2_ready"], 1)
            pe.wait_ge(s["w2l_done"], 1)

            def pair(g, last):
                for e in range(2):
                    b = 2 * g + e
                    for j in range(NH):
                        wait(pe, s["hl_done"], 2 * b + j + 1)
                        wait(pe, s["pre2_done"], 4 * b + 2 * j - 2)
                        cols = slice(j * BANK, (j + 1) * BANK)
                        for o in range(OT):
                            ch = slice(o * P, (o + 1) * P)
                            for t in range(HT):
                                terms = [(w2_hi, hid_hi), (w2_lo, hid_hi), (w2_hi, hid_lo)]
                                for k, (l, r) in enumerate(terms):
                                    ins = nc.tensor.matmul(out_ps[:, j, o, :], l[:, t, ch], r[:, t, cols],
                                                           start=t == 0 and k == 0, stop=t == HT - 1 and k == 2)
                        ins.then_inc(s["out_ready"], 1)

            over_batches(pe, B // 2, pair)


def final_layer(nc, x1, pre2, scale2, shift2, out):
    B, N, C = x1.shape
    T, CT, NH = N // P, C // P, N // BANK
    R = 4

    x1_v = x1.rearrange("b (t p) c -> b p t c", p=P)
    out_v = out.rearrange("b (t p) c -> b p t c", p=P)

    with ExitStack() as ctx:
        def sb(name, shape, dt=F32):
            return ctx.enter_context(nc.sbuf_tensor(name, shape, dt))

        def sem(name):
            return ctx.enter_context(nc.semaphore(name))

        ident = sb("ident_d", [P, P])
        neg_half = sb("neg_half_d", [P, T])
        y = sb("y", [P, R, T, C])
        z = sb("z", [P, 2, CT, N])
        stats = sb("stats3", [P, 2, T, 6])
        neg_mean = sb("neg_mean3", [P, 2, T])
        shift = sb("shift3", [P, 2, T])
        part = sb("part3", [P, 3, T])
        veps = sb("veps3", [P, 2, T])
        rstd = sb("rstd3", [P, 2, T])
        z_ps = ctx.enter_context(nc.psum_tensor("z_ps", [P, 2, T, C], F32))

        s = {n: sem("d_" + n) for n in (
            "consts_set", "z_done", "zT_ready", "added", "stats_done", "mv_done", "veps_done", "rstd_done", "y_done")}
        x1_in = [sem(f"d_x1_in{r}") for r in range(R)]
        y_out = [sem(f"d_y_out{r}") for r in range(R)]

        block = ctx.enter_context(nc.Block())

        @block.sync
        def _(sp):
            def load(b, r, g):
                wait(sp, y_out[r], 16 * g)
                sp.dma_start(y[:, r, :, :], x1_v[b]).then_inc(x1_in[r], 16)

            def group(g, last):
                for r in range(R):
                    b = R * g + r
                    wait(sp, s["y_done"], b + 1)
                    sp.dma_start(out_v[b], y[:, r, :, :]).then_inc(y_out[r], 16)
                    if r > 0 and not last:
                        load(b + R - 1, r - 1, g + 1)
                if not last:
                    load(R * g + 2 * R - 1, R - 1, g + 1)

            for r in range(R):
                load(r, r, 0)
            over_batches(sp, B // R, group)
            for r in range(R):
                wait(sp, y_out[r], 16 * (B // R))

        @block.gpsimd
        def _(pool):
            pool.memset(ident[:, :], 0.0).then_inc(s["consts_set"], 1)
            pool.memset(neg_half[:, :], -0.5).then_inc(s["consts_set"], 1)
            pool.wait_ge(s["consts_set"], 2)
            pool.affine_select(out=ident[:, :], in_=ident[:, :], compare_op=ALU.not_equal, fill=1.0, base=0,
                               pattern=[[-1, P]], channel_multiplier=1).then_inc(s["consts_set"], 1)

            def group(g, last):
                for r in range(R):
                    b = R * g + r
                    wait(pool, s["veps_done"], b + 1)
                    wait(pool, s["y_done"], b - 1)
                    pool.tensor_tensor(rstd[:, r % 2, :], veps[:, r % 2, :], neg_half[:, :], ALU.pow)\
                        .then_inc(s["rstd_done"], 1)
                    wait(pool, s["rstd_done"], 2 * b + 1)
                    pool.tensor_tensor(shift[:, r % 2, :], neg_mean[:, r % 2, :], rstd[:, r % 2, :], ALU.mult)\
                        .then_inc(s["rstd_done"], 1)

            over_batches(pool, B // R, group)

        @block.scalar
        def _(act):
            def normalise(b, r):
                wait(act, s["rstd_done"], 2 * b + 2)
                for n in range(T):
                    last = nc.scalar.activation(y[:, r, n, :], y[:, r, n, :], ACT.Identity,
                                                bias=shift[:, r % 2, n:n + 1], scale=rstd[:, r % 2, n:n + 1])
                last.then_inc(s["y_done"], 1)

            def affine(b, r):
                wait(act, s["zT_ready"], b - 1)
                for c in range(CT):
                    nc.scalar.activation(z[:, r % 2, c, :],
                                         pre2[:, c, bass.ds(NH * b, NH), :].rearrange("p j n -> p (j n)"),
                                         ACT.Identity, bias=shift2[:, c:c + 1], scale=scale2[:, c:c + 1])\
                        .then_inc(s["z_done"], 1)

            def group(g, last):
                for r in range(R):
                    b = R * g + r
                    if not (last and r == R - 1):
                        affine(b + 1, r + 1)
                    if r > 0 or not isinstance(g, int) or g > 0:
                        normalise(b - 1, (r - 1) % R)

            affine(0, 0)
            over_batches(act, B // R, group)
            normalise(B - 1, R - 1)

        @block.vector
        def _(dve):
            def group(g, last):
                for r in range(R):
                    b = R * g + r
                    wait(dve, s["zT_ready"], b + 1)
                    wait(dve, x1_in[r], 16 * (g + 1))
                    nc.vector.tensor_tensor(y[:, r, :, :], z_ps[:, r % 2, :, :], y[:, r, :, :], ALU.add)\
                        .then_inc(s["added"], 1)
                    wait(dve, s["added"], b + 1)
                    for n in range(T):
                        nc.vector.bn_stats(stats[:, r % 2, n, :], y[:, r, n, :]).then_inc(s["stats_done"], 1)
                    wait(dve, s["stats_done"], T * (b + 1))
                    wait(dve, s["rstd_done"], 2 * b - 2)
                    row_moments(nc, dve, stats[:, r % 2, :, :], part, neg_mean[:, r % 2, :], veps[:, r % 2, :], C,
                                s["mv_done"], s["veps_done"], 6 * b, sign=-1.0)

            over_batches(dve, B // R, group)

        @block.tensor
        def _(pe):
            pe.wait_ge(s["consts_set"], 3)

            def group(g, last):
                for r in range(R):
                    b = R * g + r
                    wait(pe, s["z_done"], 2 * b + 2)
                    wait(pe, s["added"], b - 1)
                    for n in range(T):
                        for c in range(CT):
                            ins = nc.tensor.transpose(z_ps[:, r % 2, n, c * P:(c + 1) * P],
                                                      z[:, r % 2, c, n * P:(n + 1) * P], ident[:, :])
                    ins.then_inc(s["zT_ready"], 1)

            over_batches(pe, B // R, group)


def program(nc, x, adj, para, kv_w, w1, b1, g1, be1, w2, b2, g2, be2, out):
    B, N, C = x.shape
    H, O = w1.shape[0], w2.shape[0]
    x1 = nc.dram_tensor("x1_scratch", [B, N, C], F32).ap()
    pre1 = nc.dram_tensor("pre1_scratch", [B, H, N], F32).ap()
    attention_layer(nc, x, adj, para, kv_w, x1)
    with ExitStack() as ctx:
        scale1 = ctx.enter_context(nc.sbuf_tensor("scale1", [P, H // P], F32))
        shift1 = ctx.enter_context(nc.sbuf_tensor("shift1", [P, H // P], F32))
        scale2 = ctx.enter_context(nc.sbuf_tensor("scale2", [P, O // P], F32))
        shift2 = ctx.enter_context(nc.sbuf_tensor("shift2", [P, O // P], F32))
        aggregate_layer(nc, x1, adj, w1, b1, g1, be1, scale1, shift1, pre1)
        pre2 = ctx.enter_context(nc.sbuf_tensor("pre2", [P, O // P, B * (N // BANK), BANK], F32))
        output_layer(nc, pre1, w2, b2, g2, be2, scale1, shift1, scale2, shift2, pre2)
        final_layer(nc, x1, pre2, scale2, shift2, out)


_INS = ['x', 'adj', 'L0_gnn_para', 'L0_gnn_kv_w', 'L1_gnn_W1', 'L1_gnn_b1', 'L1_gnn_g1', 'L1_gnn_be1',
        'L1_gnn_W2', 'L1_gnn_b2', 'L1_gnn_g2', 'L1_gnn_be2']


def kernel(**inputs):
    import numpy as _np
    import concourse.bacc as _bacc
    from concourse import mybir as _mybir
    from concourse.bass_utils import run_bass_kernel_spmd as _run

    nc = _bacc.Bacc("TRN2", target_bir_lowering=False, num_devices=1)
    arrays, args = {}, []
    for name in _INS:
        a = _np.ascontiguousarray(inputs[name])
        arrays[f"in_{name}_dram"] = a
        args.append(nc.dram_tensor(f"in_{name}_dram", a.shape, _mybir.dt.from_np(a.dtype), kind="ExternalInput").ap())
    args.append(nc.dram_tensor("out_0_dram", arrays["in_x_dram"].shape, _mybir.dt.float32,
                               kind="ExternalOutput").ap())
    program(nc, *args)
    r = _run(nc, [arrays], core_ids=[0])
    return r.results[0]["out_0_dram"]
```
